# Optimizing a Trainium2 kernel written in Bass

```python
import numpy as np
import jax
import jax.numpy as jnp

def _softmax(x, axis=-1):
    return jax.nn.softmax(x, axis=axis)

def _gelu(x):
    return jax.nn.gelu(x, approximate=True)

def _silu(x):
    return jax.nn.silu(x)

def _sigmoid(x):
    return jax.nn.sigmoid(x)

def _layernorm(x, axis=-1, eps=1e-05):
    m = jnp.mean(x, axis=axis, keepdims=True)
    v = jnp.var(x, axis=axis, keepdims=True)
    return (x - m) / jnp.sqrt(v + eps)

def _scatter_add(tgt, idx, src, axis=0):
    return tgt.at[idx].add(src)

def _segment_sum(src, seg, n):
    return jax.ops.segment_sum(src, seg, n)
kernel_name = 'mk_xattn_seq_d4_seqx_r4_f59229'

def setup_inputs(seed: int=0):
    np.random.seed(seed)
    _w = jnp.asarray

    def _rec_inputs():
        import jax
        import jax.numpy as jnp
        _rk = jax.random.key(seed)
        x = -0.0005207 + 1.001 * jax.random.normal(jax.random.fold_in(_rk, 1), (4, 512, 512), jnp.float32)
        _lenS = 512 - jax.random.randint(jax.random.fold_in(_rk, 7), (4,), 0, max(1, 512 // 4) + 1, jnp.int32)
        _lenS2 = 64 - jax.random.randint(jax.random.fold_in(_rk, 8), (4,), 0, max(1, 64 // 4) + 1, jnp.int32)
        _ctx_2048P = jax.random.normal(jax.random.fold_in(_rk, 11), (4, 16, 512), jnp.float32)
        _ctx_2048c = jax.random.dirichlet(jax.random.fold_in(_rk, 511), 0.3 * jnp.ones((16,), jnp.float32), (4, 64))
        _ctx_2048t = jnp.einsum('bsk,bkd->bsd', _ctx_2048c, _ctx_2048P)
        _ctx_2048t = _ctx_2048t * jax.lax.rsqrt(jnp.mean(jnp.square(_ctx_2048t)) + 1e-12) * 0.953939
        ctx_2048 = 2.81802e-05 + 1.00001 * (_ctx_2048t + 0.3 * jax.random.normal(jax.random.fold_in(_rk, 611), (4, 64, 512), jnp.float32))
        _validS = jnp.arange(512)[None, :] < _lenS[:, None]
        _validS2 = jnp.arange(64)[None, :] < _lenS2[:, None]
        _causal = jnp.tril(jnp.ones((512, 512), dtype=bool))
        mask_BxS2_ik0 = jnp.where(jnp.broadcast_to(_validS2[:, :], (4, 64)), 0, 1).astype(jnp.int32)
        mask_BxS2_bf1 = jnp.ones((4, 64), dtype=bool)
        return (x, ctx_2048, mask_BxS2_ik0, mask_BxS2_bf1)
    x, ctx_2048, mask_BxS2_ik0, mask_BxS2_bf1 = _rec_inputs()

    def _L0_xattn_setup():
        import jax, jax.numpy as jnp
        import numpy as np
        B, Q, S1, S2 = (4, 64, 512, 512)
        D, H, K, F = (512, 16, 128, 2048)
        LN_EPS = 1e-05

        def _layer_norm(x, scale, offset):
            mu = jnp.mean(x, axis=-1, keepdims=True)
            var = jnp.var(x, axis=-1, keepdims=True)
            return (x - mu) * jax.lax.rsqrt(var + LN_EPS) * scale + offset

        def _cross_attention(q_in, kv_in, wq, bq, wk, bk, wv, bv, wo, bo, bias_k, bias_v):
            b, q_len, _ = q_in.shape
            t = kv_in.shape[1]
            qh = (q_in @ wq + bq).reshape(b, q_len, H, K)
            kh = (kv_in @ wk + bk).reshape(b, t, H, K)
            vh = (kv_in @ wv + bv).reshape(b, t, H, K)
            kh = jnp.concatenate([kh, jnp.broadcast_to(bias_k, (b, 1, H, K))], axis=1)
            vh = jnp.concatenate([vh, jnp.broadcast_to(bias_v, (b, 1, H, K))], axis=1)
            scale = jnp.sqrt(jnp.asarray(K, q_in.dtype))
            logits = jnp.einsum('bqhk,bthk->bhqt', qh, kh) / scale
            weights = jax.nn.softmax(logits, axis=-1)
            ctx = jnp.einsum('bhqt,bthk->bqhk', weights, vh).reshape(b, q_len, H * K)
            return ctx @ wo + bo

        def _forward(x, xf_1, xf_2, ln1_scale, ln1_offset, wq1, bq1, wk1, bk1, wv1, bv1, wo1, bo1, bias_k1, bias_v1, ln2_scale, ln2_offset, wq2, bq2, wk2, bk2, wv2, bv2, wo2, bo2, bias_k2, bias_v2, ln_mlp_scale, ln_mlp_offset, w_fc1, b_fc1, w_fc2, b_fc2):
            res = x
            h = _layer_norm(x, ln1_scale, ln1_offset)
            x = res + _cross_attention(h, xf_1, wq1, bq1, wk1, bk1, wv1, bv1, wo1, bo1, bias_k1, bias_v1)
            res = x
            h = _layer_norm(x, ln2_scale, ln2_offset)
            x = res + _cross_attention(h, xf_2, wq2, bq2, wk2, bk2, wv2, bv2, wo2, bo2, bias_k2, bias_v2)
            h = _layer_norm(x, ln_mlp_scale, ln_mlp_offset)
            h = jax.nn.gelu(h @ w_fc1 + b_fc1, approximate=False) @ w_fc2 + b_fc2
            return x + h
        key = jax.random.key(seed)
        ks = iter(jax.random.split(key, 64))

        def rn(shape, s=0.02):
            return jax.random.normal(next(ks), shape, jnp.float32) * s
        inp = {'x': rn((B, Q, D), 1.0), 'xf_1': rn((B, S1, D), 1.0), 'xf_2': rn((B, S2, D), 1.0)}
        for i in (1, 2):
            inp[f'ln{i}_scale'] = jnp.ones((D,), jnp.float32)
            inp[f'ln{i}_offset'] = jnp.zeros((D,), jnp.float32)
            inp[f'wq{i}'] = rn((D, H * K))
            inp[f'bq{i}'] = jnp.zeros((H * K,), jnp.float32)
            inp[f'wk{i}'] = rn((D, H * K))
            inp[f'bk{i}'] = jnp.zeros((H * K,), jnp.float32)
            inp[f'wv{i}'] = rn((D, H * K))
            inp[f'bv{i}'] = jnp.zeros((H * K,), jnp.float32)
            inp[f'wo{i}'] = rn((H * K, D))
            inp[f'bo{i}'] = jnp.zeros((D,), jnp.float32)
            inp[f'bias_k{i}'] = rn((1, 1, H, K))
            inp[f'bias_v{i}'] = rn((1, 1, H, K))
        inp['ln_mlp_scale'] = jnp.ones((D,), jnp.float32)
        inp['ln_mlp_offset'] = jnp.zeros((D,), jnp.float32)
        inp['w_fc1'] = rn((D, F))
        inp['b_fc1'] = jnp.zeros((F,), jnp.float32)
        inp['w_fc2'] = rn((F, D))
        inp['b_fc2'] = jnp.zeros((D,), jnp.float32)
        return inp
    _L0_xattn_all = _L0_xattn_setup()
    _L0_xattn_in = {k: v for k, v in _L0_xattn_all.items() if k in ('ln1_scale', 'ln1_offset', 'wq1', 'bq1', 'wk1', 'bk1', 'wv1', 'bv1', 'wo1', 'bo1', 'bias_k1', 'bias_v1', 'ln2_scale', 'ln2_offset', 'wq2', 'bq2', 'wk2', 'bk2', 'wv2', 'bv2', 'wo2', 'bo2', 'bias_k2', 'bias_v2', 'ln_mlp_scale', 'ln_mlp_offset', 'w_fc1', 'b_fc1', 'w_fc2', 'b_fc2')}
    del _L0_xattn_all

    def _L1_xattn_setup():
        import jax, jax.numpy as jnp
        import numpy as np
        H = 512
        B, L, S = (4, 1024, 10)
        key = jax.random.key(seed)
        k1, k2, k3, k4, k5, k6 = jax.random.split(key, 6)
        scale = 1.0 / np.sqrt(H)
        return {'h_english': jax.random.normal(k1, (B, L, H), dtype=jnp.float32), 'h_lojban': jax.random.normal(k2, (B, S, H), dtype=jnp.float32), 'w_q': jax.random.normal(k3, (H, H), dtype=jnp.float32) * scale, 'w_k': jax.random.normal(k4, (H, H), dtype=jnp.float32) * scale, 'w_v': jax.random.normal(k5, (H, H), dtype=jnp.float32) * scale, 'w_o': jax.random.normal(k6, (H, H), dtype=jnp.float32) * scale, 'alpha': jnp.float32(0.1)}
    _L1_xattn_all = _L1_xattn_setup()
    _L1_xattn_in = {k: v for k, v in _L1_xattn_all.items() if k in ('w_q', 'w_k', 'w_v', 'w_o', 'alpha')}
    del _L1_xattn_all

    def _L2_xattn_setup():
        import jax, jax.numpy as jnp
        import numpy as np
        B, P, K, H, NH = (4, 512, 64, 512, 16)
        DH = H // NH
        EPS = 1e-06

        def rmsnorm(x, w):
            var = jnp.mean(jnp.square(x), axis=-1, keepdims=True)
            return x * jax.lax.rsqrt(var + EPS) * w
        key = jax.random.key(seed)
        ks = jax.random.split(key, 12)
        s = 0.02
        return {'x': jax.random.normal(ks[0], (B, P, H), jnp.float32), 'latents': jax.random.normal(ks[1], (B, K, H), jnp.float32), 'attention_mask': jax.random.randint(ks[2], (B, P), 0, 2, jnp.int32), 'q_w': s * jax.random.normal(ks[3], (H, H), jnp.float32), 'q_b': jnp.zeros((H,), jnp.float32), 'kv_w': s * jax.random.normal(ks[4], (H, 2 * H), jnp.float32), 'kv_b': jnp.zeros((2 * H,), jnp.float32), 'out_w': s * jax.random.normal(ks[5], (H, H), jnp.float32), 'out_b': jnp.zeros((H,), jnp.float32), 'postnorm_w': jnp.ones((H,), jnp.float32), 'mlp_w1': s * jax.random.normal(ks[6], (H, 4 * H), jnp.float32), 'mlp_b1': jnp.zeros((4 * H,), jnp.float32), 'mlp_w2': s * jax.random.normal(ks[7], (4 * H, H), jnp.float32), 'mlp_b2': jnp.zeros((H,), jnp.float32)}
    _L2_xattn_all = _L2_xattn_setup()
    _L2_xattn_in = {k: v for k, v in _L2_xattn_all.items() if k in ('q_w', 'q_b', 'kv_w', 'kv_b', 'out_w', 'out_b', 'postnorm_w', 'mlp_w1', 'mlp_b1', 'mlp_w2', 'mlp_b2')}
    del _L2_xattn_all

    def _L3_xattn_setup():
        import jax, jax.numpy as jnp
        import numpy as np
        D = 512
        H = 16
        HD = D // H
        INNER = 4 * D
        EPS = 1e-05

        def layer_norm(x, w, b):
            mu = jnp.mean(x, axis=-1, keepdims=True)
            var = jnp.mean(jnp.square(x - mu), axis=-1, keepdims=True)
            return (x - mu) * jax.lax.rsqrt(var + EPS) * w + b
        key = jax.random.key(seed)
        ks = jax.random.split(key, 12)
        B, LQ, LK = (4, 256, 512)
        std = 0.02
        inp = {'hidden_states': jax.random.normal(ks[0], (B, LQ, D), jnp.float32), 'encoder_hidden_states': jax.random.normal(ks[1], (B, LK, D), jnp.float32), 'encoder_attention_mask': jnp.ones((B, LK), dtype=bool), 'ln1_w': jnp.ones((D,), jnp.float32), 'ln1_b': jnp.zeros((D,), jnp.float32), 'q_w': jax.random.normal(ks[2], (D, D), jnp.float32) * std, 'q_b': jnp.zeros((D,), jnp.float32), 'k_w': jax.random.normal(ks[3], (D, D), jnp.float32) * std, 'k_b': jnp.zeros((D,), jnp.float32), 'v_w': jax.random.normal(ks[4], (D, D), jnp.float32) * std, 'v_b': jnp.zeros((D,), jnp.float32), 'cproj_w': jax.random.normal(ks[5], (D, D), jnp.float32) * std, 'cproj_b': jnp.zeros((D,), jnp.float32), 'ln2_w': jnp.ones((D,), jnp.float32), 'ln2_b': jnp.zeros((D,), jnp.float32), 'fc_w': jax.random.normal(ks[6], (D, INNER), jnp.float32) * std, 'fc_b': jnp.zeros((INNER,), jnp.float32), 'proj_w': jax.random.normal(ks[7], (INNER, D), jnp.float32) * std, 'proj_b': jnp.zeros((D,), jnp.float32)}
        return inp
    _L3_xattn_all = _L3_xattn_setup()
    _L3_xattn_in = {k: v for k, v in _L3_xattn_all.items() if k in ('ln1_w', 'ln1_b', 'q_w', 'q_b', 'k_w', 'k_b', 'v_w', 'v_b', 'cproj_w', 'cproj_b', 'ln2_w', 'ln2_b', 'fc_w', 'fc_b', 'proj_w', 'proj_b')}
    del _L3_xattn_all
    return {'x': x, 'ctx_2048': ctx_2048, 'mask_BxS2_ik0': mask_BxS2_ik0, 'mask_BxS2_bf1': mask_BxS2_bf1, 'L0_xattn_ln1_scale': _L0_xattn_in['ln1_scale'], 'L0_xattn_ln1_offset': _L0_xattn_in['ln1_offset'], 'L0_xattn_wq1': _L0_xattn_in['wq1'], 'L0_xattn_bq1': _L0_xattn_in['bq1'], 'L0_xattn_wk1': _L0_xattn_in['wk1'], 'L0_xattn_bk1': _L0_xattn_in['bk1'], 'L0_xattn_wv1': _L0_xattn_in['wv1'], 'L0_xattn_bv1': _L0_xattn_in['bv1'], 'L0_xattn_wo1': _L0_xattn_in['wo1'], 'L0_xattn_bo1': _L0_xattn_in['bo1'], 'L0_xattn_bias_k1': _L0_xattn_in['bias_k1'], 'L0_xattn_bias_v1': _L0_xattn_in['bias_v1'], 'L0_xattn_ln2_scale': _L0_xattn_in['ln2_scale'], 'L0_xattn_ln2_offset': _L0_xattn_in['ln2_offset'], 'L0_xattn_wq2': _L0_xattn_in['wq2'], 'L0_xattn_bq2': _L0_xattn_in['bq2'], 'L0_xattn_wk2': _L0_xattn_in['wk2'], 'L0_xattn_bk2': _L0_xattn_in['bk2'], 'L0_xattn_wv2': _L0_xattn_in['wv2'], 'L0_xattn_bv2': _L0_xattn_in['bv2'], 'L0_xattn_wo2': _L0_xattn_in['wo2'], 'L0_xattn_bo2': _L0_xattn_in['bo2'], 'L0_xattn_bias_k2': _L0_xattn_in['bias_k2'], 'L0_xattn_bias_v2': _L0_xattn_in['bias_v2'], 'L0_xattn_ln_mlp_scale': _L0_xattn_in['ln_mlp_scale'], 'L0_xattn_ln_mlp_offset': _L0_xattn_in['ln_mlp_offset'], 'L0_xattn_w_fc1': _L0_xattn_in['w_fc1'], 'L0_xattn_b_fc1': _L0_xattn_in['b_fc1'], 'L0_xattn_w_fc2': _L0_xattn_in['w_fc2'], 'L0_xattn_b_fc2': _L0_xattn_in['b_fc2'], 'L1_xattn_w_q': _L1_xattn_in['w_q'], 'L1_xattn_w_k': _L1_xattn_in['w_k'], 'L1_xattn_w_v': _L1_xattn_in['w_v'], 'L1_xattn_w_o': _L1_xattn_in['w_o'], 'L1_xattn_alpha': _L1_xattn_in['alpha'], 'L2_xattn_q_w': _L2_xattn_in['q_w'], 'L2_xattn_q_b': _L2_xattn_in['q_b'], 'L2_xattn_kv_w': _L2_xattn_in['kv_w'], 'L2_xattn_kv_b': _L2_xattn_in['kv_b'], 'L2_xattn_out_w': _L2_xattn_in['out_w'], 'L2_xattn_out_b': _L2_xattn_in['out_b'], 'L2_xattn_postnorm_w': _L2_xattn_in['postnorm_w'], 'L2_xattn_mlp_w1': _L2_xattn_in['mlp_w1'], 'L2_xattn_mlp_b1': _L2_xattn_in['mlp_b1'], 'L2_xattn_mlp_w2': _L2_xattn_in['mlp_w2'], 'L2_xattn_mlp_b2': _L2_xattn_in['mlp_b2'], 'L3_xattn_ln1_w': _L3_xattn_in['ln1_w'], 'L3_xattn_ln1_b': _L3_xattn_in['ln1_b'], 'L3_xattn_q_w': _L3_xattn_in['q_w'], 'L3_xattn_q_b': _L3_xattn_in['q_b'], 'L3_xattn_k_w': _L3_xattn_in['k_w'], 'L3_xattn_k_b': _L3_xattn_in['k_b'], 'L3_xattn_v_w': _L3_xattn_in['v_w'], 'L3_xattn_v_b': _L3_xattn_in['v_b'], 'L3_xattn_cproj_w': _L3_xattn_in['cproj_w'], 'L3_xattn_cproj_b': _L3_xattn_in['cproj_b'], 'L3_xattn_ln2_w': _L3_xattn_in['ln2_w'], 'L3_xattn_ln2_b': _L3_xattn_in['ln2_b'], 'L3_xattn_fc_w': _L3_xattn_in['fc_w'], 'L3_xattn_fc_b': _L3_xattn_in['fc_b'], 'L3_xattn_proj_w': _L3_xattn_in['proj_w'], 'L3_xattn_proj_b': _L3_xattn_in['proj_b']}

def reference(x, ctx_2048, mask_BxS2_ik0, mask_BxS2_bf1, L0_xattn_ln1_scale, L0_xattn_ln1_offset, L0_xattn_wq1, L0_xattn_bq1, L0_xattn_wk1, L0_xattn_bk1, L0_xattn_wv1, L0_xattn_bv1, L0_xattn_wo1, L0_xattn_bo1, L0_xattn_bias_k1, L0_xattn_bias_v1, L0_xattn_ln2_scale, L0_xattn_ln2_offset, L0_xattn_wq2, L0_xattn_bq2, L0_xattn_wk2, L0_xattn_bk2, L0_xattn_wv2, L0_xattn_bv2, L0_xattn_wo2, L0_xattn_bo2, L0_xattn_bias_k2, L0_xattn_bias_v2, L0_xattn_ln_mlp_scale, L0_xattn_ln_mlp_offset, L0_xattn_w_fc1, L0_xattn_b_fc1, L0_xattn_w_fc2, L0_xattn_b_fc2, L1_xattn_w_q, L1_xattn_w_k, L1_xattn_w_v, L1_xattn_w_o, L1_xattn_alpha, L2_xattn_q_w, L2_xattn_q_b, L2_xattn_kv_w, L2_xattn_kv_b, L2_xattn_out_w, L2_xattn_out_b, L2_xattn_postnorm_w, L2_xattn_mlp_w1, L2_xattn_mlp_b1, L2_xattn_mlp_w2, L2_xattn_mlp_b2, L3_xattn_ln1_w, L3_xattn_ln1_b, L3_xattn_q_w, L3_xattn_q_b, L3_xattn_k_w, L3_xattn_k_b, L3_xattn_v_w, L3_xattn_v_b, L3_xattn_cproj_w, L3_xattn_cproj_b, L3_xattn_ln2_w, L3_xattn_ln2_b, L3_xattn_fc_w, L3_xattn_fc_b, L3_xattn_proj_w, L3_xattn_proj_b):
    import jax
    import jax.numpy as jnp

    def _L0_xattn_ref(x, xf_1, xf_2, ln1_scale, ln1_offset, wq1, bq1, wk1, bk1, wv1, bv1, wo1, bo1, bias_k1, bias_v1, ln2_scale, ln2_offset, wq2, bq2, wk2, bk2, wv2, bv2, wo2, bo2, bias_k2, bias_v2, ln_mlp_scale, ln_mlp_offset, w_fc1, b_fc1, w_fc2, b_fc2):
        import jax, jax.numpy as jnp
        import numpy as np
        B, Q, S1, S2 = (4, 64, 512, 512)
        D, H, K, F = (512, 16, 128, 2048)
        LN_EPS = 1e-05

        def _layer_norm(x, scale, offset):
            mu = jnp.mean(x, axis=-1, keepdims=True)
            var = jnp.var(x, axis=-1, keepdims=True)
            return (x - mu) * jax.lax.rsqrt(var + LN_EPS) * scale + offset

        def _cross_attention(q_in, kv_in, wq, bq, wk, bk, wv, bv, wo, bo, bias_k, bias_v):
            b, q_len, _ = q_in.shape
            t = kv_in.shape[1]
            qh = (q_in @ wq + bq).reshape(b, q_len, H, K)
            kh = (kv_in @ wk + bk).reshape(b, t, H, K)
            vh = (kv_in @ wv + bv).reshape(b, t, H, K)
            kh = jnp.concatenate([kh, jnp.broadcast_to(bias_k, (b, 1, H, K))], axis=1)
            vh = jnp.concatenate([vh, jnp.broadcast_to(bias_v, (b, 1, H, K))], axis=1)
            scale = jnp.sqrt(jnp.asarray(K, q_in.dtype))
            logits = jnp.einsum('bqhk,bthk->bhqt', qh, kh) / scale
            weights = jax.nn.softmax(logits, axis=-1)
            ctx = jnp.einsum('bhqt,bthk->bqhk', weights, vh).reshape(b, q_len, H * K)
            return ctx @ wo + bo

        def _forward(x, xf_1, xf_2, ln1_scale, ln1_offset, wq1, bq1, wk1, bk1, wv1, bv1, wo1, bo1, bias_k1, bias_v1, ln2_scale, ln2_offset, wq2, bq2, wk2, bk2, wv2, bv2, wo2, bo2, bias_k2, bias_v2, ln_mlp_scale, ln_mlp_offset, w_fc1, b_fc1, w_fc2, b_fc2):
            res = x
            h = _layer_norm(x, ln1_scale, ln1_offset)
            x = res + _cross_attention(h, xf_1, wq1, bq1, wk1, bk1, wv1, bv1, wo1, bo1, bias_k1, bias_v1)
            res = x
            h = _layer_norm(x, ln2_scale, ln2_offset)
            x = res + _cross_attention(h, xf_2, wq2, bq2, wk2, bk2, wv2, bv2, wo2, bo2, bias_k2, bias_v2)
            h = _layer_norm(x, ln_mlp_scale, ln_mlp_offset)
            h = jax.nn.gelu(h @ w_fc1 + b_fc1, approximate=False) @ w_fc2 + b_fc2
            return x + h
        return _forward(x, xf_1, xf_2, ln1_scale, ln1_offset, wq1, bq1, wk1, bk1, wv1, bv1, wo1, bo1, bias_k1, bias_v1, ln2_scale, ln2_offset, wq2, bq2, wk2, bk2, wv2, bv2, wo2, bo2, bias_k2, bias_v2, ln_mlp_scale, ln_mlp_offset, w_fc1, b_fc1, w_fc2, b_fc2)

    def _L1_xattn_ref(h_english, h_lojban, w_q, w_k, w_v, w_o, alpha):
        import jax, jax.numpy as jnp
        import numpy as np
        H = 512
        B, L, S = (4, 1024, 10)
        h = h_english.shape[-1]
        q = jnp.einsum('blh,oh->blo', h_english, w_q)
        k = jnp.einsum('bsh,oh->bso', h_lojban, w_k)
        v = jnp.einsum('bsh,oh->bso', h_lojban, w_v)
        scores = jnp.einsum('blh,bsh->bls', q, k) / jnp.sqrt(jnp.float32(h))
        probs = jax.nn.softmax(scores, axis=-1)
        context = jnp.einsum('bls,bsh->blh', probs, v)
        delta = jnp.einsum('blh,oh->blo', context, w_o)
        return h_english + alpha * delta

    def _L2_xattn_ref(x, latents, attention_mask, q_w, q_b, kv_w, kv_b, out_w, out_b, postnorm_w, mlp_w1, mlp_b1, mlp_w2, mlp_b2):
        import jax, jax.numpy as jnp
        import numpy as np
        B, P, K, H, NH = (4, 512, 64, 512, 16)
        DH = H // NH
        EPS = 1e-06

        def rmsnorm(x, w):
            var = jnp.mean(jnp.square(x), axis=-1, keepdims=True)
            return x * jax.lax.rsqrt(var + EPS) * w
        b, p, _ = x.shape
        k_len = latents.shape[1]
        residual = latents
        h = jnp.concatenate([x, latents], axis=1)
        q = (latents @ q_w + q_b).reshape(b, k_len, NH, DH)
        kv = (h @ kv_w + kv_b).reshape(b, p + k_len, NH, DH, 2)
        kmat, v = (kv[..., 0], kv[..., 1])
        attn = jnp.einsum('bkhd,bnhd->bhkn', q, kmat) / DH
        full_mask = jnp.concatenate([attention_mask.astype(bool), jnp.ones((b, k_len), bool)], axis=-1)
        attn = jnp.where(full_mask[:, None, None, :], attn, -jnp.inf)
        attn = jax.nn.softmax(attn.astype(jnp.float32), axis=-1).astype(q.dtype)
        attn_out = jnp.einsum('bhkn,bnhd->bkhd', attn, v).reshape(b, k_len, H)
        attn_out = attn_out @ out_w + out_b + residual
        out = rmsnorm(attn_out, postnorm_w)
        out = jax.nn.gelu(out @ mlp_w1 + mlp_b1) @ mlp_w2 + mlp_b2
        return out + residual

    def _L3_xattn_ref(hidden_states, encoder_hidden_states, encoder_attention_mask, ln1_w, ln1_b, q_w, q_b, k_w, k_b, v_w, v_b, cproj_w, cproj_b, ln2_w, ln2_b, fc_w, fc_b, proj_w, proj_b):
        import jax, jax.numpy as jnp
        import numpy as np
        D = 512
        H = 16
        HD = D // H
        INNER = 4 * D
        EPS = 1e-05

        def layer_norm(x, w, b):
            mu = jnp.mean(x, axis=-1, keepdims=True)
            var = jnp.mean(jnp.square(x - mu), axis=-1, keepdims=True)
            return (x - mu) * jax.lax.rsqrt(var + EPS) * w + b
        B, LQ, _ = hidden_states.shape
        LK = encoder_hidden_states.shape[1]
        residual = hidden_states
        x = layer_norm(hidden_states, ln1_w, ln1_b)
        q = (x @ q_w + q_b).reshape(B, LQ, H, HD).transpose(0, 2, 1, 3)
        k = (encoder_hidden_states @ k_w + k_b).reshape(B, LK, H, HD).transpose(0, 2, 1, 3)
        v = (encoder_hidden_states @ v_w + v_b).reshape(B, LK, H, HD).transpose(0, 2, 1, 3)
        scale = 1.0 / np.sqrt(HD).astype(np.float32)
        scores = jnp.einsum('bhqd,bhkd->bhqk', q, k) * scale
        mask = encoder_attention_mask[:, None, None, :]
        mask_value = jnp.finfo(scores.dtype).min
        scores = jnp.where(mask, scores, mask_value)
        attn = jax.nn.softmax(scores, axis=-1)
        out = jnp.einsum('bhqk,bhkd->bhqd', attn, v)
        out = out.transpose(0, 2, 1, 3).reshape(B, LQ, D)
        out = out @ cproj_w + cproj_b
        hidden = out + residual
        residual = hidden
        y = layer_norm(hidden, ln2_w, ln2_b)
        y = jax.nn.gelu(y @ fc_w + fc_b, approximate=True)
        y = y @ proj_w + proj_b
        return residual + y
    x = _L0_xattn_ref(x, ctx_2048, ctx_2048, L0_xattn_ln1_scale, L0_xattn_ln1_offset, L0_xattn_wq1, L0_xattn_bq1, L0_xattn_wk1, L0_xattn_bk1, L0_xattn_wv1, L0_xattn_bv1, L0_xattn_wo1, L0_xattn_bo1, L0_xattn_bias_k1, L0_xattn_bias_v1, L0_xattn_ln2_scale, L0_xattn_ln2_offset, L0_xattn_wq2, L0_xattn_bq2, L0_xattn_wk2, L0_xattn_bk2, L0_xattn_wv2, L0_xattn_bv2, L0_xattn_wo2, L0_xattn_bo2, L0_xattn_bias_k2, L0_xattn_bias_v2, L0_xattn_ln_mlp_scale, L0_xattn_ln_mlp_offset, L0_xattn_w_fc1, L0_xattn_b_fc1, L0_xattn_w_fc2, L0_xattn_b_fc2)
    x = _L1_xattn_ref(x, ctx_2048, L1_xattn_w_q, L1_xattn_w_k, L1_xattn_w_v, L1_xattn_w_o, L1_xattn_alpha)
    x = _L2_xattn_ref(ctx_2048, x, mask_BxS2_ik0, L2_xattn_q_w, L2_xattn_q_b, L2_xattn_kv_w, L2_xattn_kv_b, L2_xattn_out_w, L2_xattn_out_b, L2_xattn_postnorm_w, L2_xattn_mlp_w1, L2_xattn_mlp_b1, L2_xattn_mlp_w2, L2_xattn_mlp_b2)
    x = _L3_xattn_ref(x, ctx_2048, mask_BxS2_bf1, L3_xattn_ln1_w, L3_xattn_ln1_b, L3_xattn_q_w, L3_xattn_q_b, L3_xattn_k_w, L3_xattn_k_b, L3_xattn_v_w, L3_xattn_v_b, L3_xattn_cproj_w, L3_xattn_cproj_b, L3_xattn_ln2_w, L3_xattn_ln2_b, L3_xattn_fc_w, L3_xattn_fc_b, L3_xattn_proj_w, L3_xattn_proj_b)
    return x

_drawn_inputs = setup_inputs


def setup_inputs(seed=0):
    import zlib

    import numpy as np

    out = dict(_drawn_inputs(seed))
    spreads = {'L0_xattn_ln1_scale': (1.0, 0.6),
     'L0_xattn_ln1_offset': (0.0, 0.8),
     'L0_xattn_bq1': (0.0, 0.8),
     'L0_xattn_bk1': (0.0, 2.0),
     'L0_xattn_bv1': (0.0, 0.1),
     'L0_xattn_bo1': (0.0, 0.1),
     'L0_xattn_ln2_scale': (1.0, 0.6),
     'L0_xattn_ln2_offset': (0.0, 0.8),
     'L0_xattn_bq2': (0.0, 0.8),
     'L0_xattn_bk2': (0.0, 2.0),
     'L0_xattn_bv2': (0.0, 0.1),
     'L0_xattn_bo2': (0.0, 0.1),
     'L0_xattn_ln_mlp_scale': (1.0, 0.2),
     'L0_xattn_ln_mlp_offset': (0.0, 0.348),
     'L0_xattn_b_fc1': (0.0, 0.1),
     'L0_xattn_b_fc2': (0.0, 0.1),
     'L2_xattn_q_b': (0.0, 2.0),
     'L2_xattn_kv_b': (0.0, 0.8),
     'L2_xattn_out_b': (0.0, 0.409),
     'L2_xattn_postnorm_w': (1.0, 0.2),
     'L2_xattn_mlp_b1': (0.0, 0.1),
     'L2_xattn_mlp_b2': (0.0, 0.1),
     'L3_xattn_ln1_w': (1.0, 0.6),
     'L3_xattn_ln1_b': (0.0, 0.8),
     'L3_xattn_q_b': (0.0, 0.8),
     'L3_xattn_k_b': (0.0, 2.0),
     'L3_xattn_v_b': (0.0, 0.1),
     'L3_xattn_cproj_b': (0.0, 0.1),
     'L3_xattn_ln2_w': (1.0, 0.2),
     'L3_xattn_ln2_b': (0.0, 0.393),
     'L3_xattn_fc_b': (0.0, 0.1),
     'L3_xattn_proj_b': (0.0, 0.1)}
    factors = {'L0_xattn_wq1': 3.531,
     'L0_xattn_wk1': 3.432,
     'L0_xattn_bias_k1': 64.0,
     'L0_xattn_bias_v1': 40.756,
     'L0_xattn_wq2': 3.634,
     'L0_xattn_wk2': 3.551,
     'L0_xattn_bias_k2': 64.0,
     'L0_xattn_bias_v2': 64.0,
     'L1_xattn_w_k': 2.736,
     'L2_xattn_q_w': 8.0,
     'L2_xattn_kv_w': 3.916,
     'L2_xattn_out_w': 3.3,
     'L3_xattn_q_w': 7.696,
     'L3_xattn_k_w': 7.687}
    for name, (base, spread) in spreads.items():
        noise = np.random.default_rng([zlib.crc32(name.encode()), seed]).standard_normal(out[name].shape)
        drawn = base * np.exp(spread * noise) if base else spread * noise
        out[name] = jnp.asarray(drawn.astype(out[name].dtype))
    for name, factor in factors.items():
        out[name] = (out[name] * factor).astype(out[name].dtype)
    return out
```

```python
from contextlib import ExitStack

import concourse.bass as bass
from concourse import mybir

F32 = mybir.dt.float32
F32R = mybir.dt.float32r
I32 = mybir.dt.int32
U8 = mybir.dt.uint8
ALU = mybir.AluOpType
ACT = mybir.ActivationFunctionType
AX = mybir.AxisListType

P = 128
B = 4
S = 512
C = 64
D = 512
KT = D // P
TOK = B * S
TILES = TOK // P
TPB = S // P
CTOK = B * C
F = 2048
FB = F // D
H = 16
HK0 = 128
HG = 4
HD = D // H

BLOCKS = {}


def _count_blocks():
    at = 0
    for name, n in (
        ("l0a_wk", 4), ("l0a_wv", 4), ("l0a_wqT", 4), ("l0a_wo", 4),
        ("l0b_wk", 4), ("l0b_wv", 4), ("l0b_wqT", 4), ("l0b_wo", 4),
        ("l0_fc1", 4), ("l0_fc2", 4),
        ("l1_wkT", 1), ("l1_wvT", 1), ("l1_wq", 1), ("l1_woT", 1),
        ("l2_wq", 1), ("l2_wk", 1), ("l2_wv", 1), ("l2_wo", 1), ("l2_fc1", 4), ("l2_fc2", 4),
        ("l3_wq", 1), ("l3_wk", 1), ("l3_wv", 1), ("l3_wo", 1), ("l3_fc1", 4), ("l3_fc2", 4),
    ):
        BLOCKS[name] = at
        at += n
    return at


N_BLOCKS = _count_blocks()

COLUMN_SIZES = (
    ("l0a_scale", 4), ("l0a_offset", 4), ("l0b_scale", 4), ("l0b_offset", 4), ("l0m_scale", 4), ("l0m_offset", 4),
    ("l0a_bq", 16), ("l0a_bk", 16), ("l0a_bv", 16), ("l0a_bias_k", 16), ("l0a_bias_v", 16),
    ("l0b_bq", 16), ("l0b_bk", 16), ("l0b_bv", 16), ("l0b_bias_k", 16), ("l0b_bias_v", 16),
    ("l0_b1", 16), ("l2_bq", 4), ("l2_bk", 4), ("l2_scale", 4), ("l2_b1", 16),
    ("l3_scale", 4), ("l3_offset", 4), ("l3_bq", 4), ("l3_bk", 4), ("l3m_scale", 4), ("l3m_offset", 4), ("l3_b1", 16),
)
COLUMNS = {}
N_COLUMNS = 0
for _name, _n in COLUMN_SIZES:
    COLUMNS[_name] = N_COLUMNS
    N_COLUMNS += _n

ROW_NAMES = ("l0a_bo", "l0b_bo", "l0_b2", "l2_bv", "l2_bo", "l2_b2", "l3_bv", "l3_bo", "l3_b2")
ROWS = {n: i for i, n in enumerate(ROW_NAMES)}


class Net:

    def __init__(self, nc, ctx, dram):
        self.nc, self.ctx, self.dram, self.stage_sems = nc, ctx, dram, []
        self.x = self.sbuf("x", [P, TILES, D], F32)
        self.ctx_f = self.sbuf("ctx_f", [P, KT, CTOK], F32)
        self.ident = self.sbuf("ident", [P, P], F32)
        self.columns = self.sbuf("columns", [P, N_COLUMNS], F32)

    def sbuf(self, name, shape, dt, ctx=None):
        return (ctx or self.ctx).enter_context(self.nc.sbuf_tensor(name, shape, dt))

    def psum(self, name, shape, ctx):
        return ctx.enter_context(self.nc.psum_tensor(name, shape, F32))

    def sem(self, name):
        self.stage_sems.append(self.nc.alloc_semaphore(name=name))
        return self.stage_sems[-1]

    def end_stage(self):
        self.nc.clear_and_free_semaphores(self.stage_sems)
        self.nc.all_engine_barrier()
        self.stage_sems = []

    def col(self, name, j=0):
        at = COLUMNS[name] + j
        return self.columns[:, at:at + 1]

    def row_broadcast(self, name):
        return self.dram["rows"][ROWS[name]:ROWS[name] + 1, :].to_broadcast([P, D])

    def block(self, name, i=0):
        return self.dram["weights"][BLOCKS[name] + i]


def product3(pe, out, left, right, start, stop):
    (lh, ll), (rh, rl) = left, right
    pe.matmul(out, lh, rh, start=start, stop=False)
    pe.matmul(out, lh, rl, start=False, stop=False)
    return pe.matmul(out, ll, rh, start=False, stop=stop)


def load_stage(n):
    nc = n.nc
    with ExitStack() as mem:
        raw = n.sbuf("ctx_rows", [P, CTOK // P, D], F32, mem)
        turned = n.psum("ctx_turned", [P, KT, D], mem)
        x_loaded, ctx_loaded, columns_loaded = n.sem("x_loaded"), n.sem("ctx_loaded"), n.sem("columns_loaded")
        ident_ready, ctx_turned, ctx_ready = n.sem("ident_ready"), n.sem("ctx_turned"), n.sem("ctx_ready")
        block = mem.enter_context(nc.Block())

        @block.sync
        def _(sp):
            sp.dma_start(raw[:, :, :], n.dram["ctx"].rearrange("(t p) d -> p t d", p=P)).then_inc(ctx_loaded, 16)
            sp.dma_start(n.columns[:, :], n.dram["columns"]).then_inc(columns_loaded, 16)
            x_rows = n.dram["x"].rearrange("(t p) d -> p t d", p=P)
            for c in range(B):
                sp.dma_start(n.x[:, c * TPB:(c + 1) * TPB, :], x_rows[:, c * TPB:(c + 1) * TPB, :]).then_inc(x_loaded, 16)
            sp.wait_ge(x_loaded, 16 * B)
            sp.wait_ge(columns_loaded, 16)

        @block.gpsimd
        def _(pool):
            pool.memset(n.ident[:, :], 0.0).then_inc(ident_ready, 1)
            pool.wait_ge(ident_ready, 1)
            pool.affine_select(out=n.ident[:, :], in_=n.ident[:, :], compare_op=ALU.not_equal, fill=1.0, base=0,
                               pattern=[[-1, P]], channel_multiplier=1).then_inc(ident_ready, 1)

        @block.tensor
        def _(pe):
            pe.wait_ge(ident_ready, 2)
            pe.wait_ge(ctx_loaded, 16)
            for k in range(KT):
                for t in range(CTOK // P):
                    last = pe.transpose(turned[:, k, t * P:(t + 1) * P], raw[:, t, k * P:(k + 1) * P], n.ident[:, :])
            last.then_inc(ctx_turned, 1)

        @block.vector
        def _(dve):
            dve.wait_ge(ctx_turned, 1)
            dve.tensor_copy(n.ctx_f[:, :, :], turned[:, :, 0:CTOK]).then_inc(ctx_ready, 1)
            dve.wait_ge(ctx_ready, 1)


def store_stage(n):
    nc = n.nc
    with ExitStack() as mem:
        stored = n.sem("stored")
        block = mem.enter_context(nc.Block())

        @block.sync
        def _(sp):
            out_rows = n.dram["out"].rearrange("(t p) d -> p t d", p=P)
            for c in range(B):
                sp.dma_start(out_rows[:, c * TPB:(c + 1) * TPB, :], n.x[:, c * TPB:(c + 1) * TPB, :]).then_inc(stored, 16)
            sp.wait_ge(stored, 16 * B)


def normalise_stage(n, tag, src, scale, offset, row_name, kind, eps, parts=None, plain=None, first_block=None):
    nc = n.nc
    with ExitStack() as mem:
        rows = n.sbuf(f"{tag}_rows", [P, 2, TPB, D], F32, mem)
        stats = n.sbuf(f"{tag}_stats", [P, 2, TPB, 6], F32, mem)
        mean_var = n.sbuf(f"{tag}_mean_var", [P, 2, TPB, 2], F32, mem)
        second = n.sbuf(f"{tag}_second", [P, 2, TPB], F32, mem)
        deviation = n.sbuf(f"{tag}_deviation", [P, 2, TPB], F32, mem)
        inverse = n.sbuf(f"{tag}_inverse", [P, 2, TPB], F32, mem)
        bias_row = n.sbuf(f"{tag}_bias_row", [P, D], F32, mem)
        scaled = n.sbuf(f"{tag}_scaled", [P, 2, D], F32, mem)
        turned = n.psum(f"{tag}_turned", [P, 2, KT, D], mem)
        row_loaded = n.sem(f"{tag}_row_loaded")
        chain = n.sem(f"{tag}_chain")
        variance_ready, deviation_ready = n.sem(f"{tag}_variance"), n.sem(f"{tag}_deviation")
        rows_ready, tile_turned = n.sem(f"{tag}_rows_ready"), n.sem(f"{tag}_turned_ready")
        scaled_ready, split_done = n.sem(f"{tag}_scaled"), n.sem(f"{tag}_split")
        bias_added = n.sem(f"{tag}_bias_added")
        block_loaded, block_split = n.sem(f"{tag}_block_loaded"), n.sem(f"{tag}_block_split")
        block = mem.enter_context(nc.Block())

        @block.sync
        def _(sp):
            if row_name:
                sp.dma_start(bias_row[:, :], n.row_broadcast(row_name)).then_inc(row_loaded, 16)
            if first_block:
                sp.dma_start(first_block[1][:, :, :], first_block[0]).then_inc(block_loaded, 16)

        @block.gpsimd
        def _(pool):
            if first_block:
                _, raw, hi, lo = first_block
                pool.wait_ge(block_loaded, 16)
                pool.tensor_copy(hi[:, :, :], raw[:, :, :]).then_inc(block_split, 1)
                pool.wait_ge(block_split, 1)
                pool.tensor_tensor(lo[:, :, :], raw[:, :, :], hi[:, :, :].bitcast(F32), ALU.subtract).then_inc(block_split, 1)
                pool.wait_ge(block_split, 2)
            if row_name:
                pool.wait_ge(row_loaded, 16)
                for t in range(TILES):
                    pool.wait_ge(rows_ready, t // TPB + 1)
                    pool.tensor_tensor(n.x[:, t, :], n.x[:, t, :], bias_row[:, :], ALU.add).then_inc(bias_added, 1)
                pool.wait_ge(bias_added, TILES)

        @block.vector
        def _(dve):
            steps = [0]

            def link(instruction, wait=True):
                steps[0] += 1
                instruction.then_inc(chain, 1)
                if wait:
                    dve.wait_ge(chain, steps[0])

            def rows_of(c):
                half = c % 2
                if c >= 2:
                    dve.wait_ge(tile_turned, KT * (c - 1))
                if kind == "none":
                    for j in range(TPB):
                        last = dve.tensor_copy(rows[:, half, j, :], src[:, c * TPB + j, :])
                    last.then_inc(rows_ready, 1)
                    return
                for j in range(TPB):
                    link(dve.bn_stats(stats[:, half, j, :], src[:, c * TPB + j, :]), j == TPB - 1)
                for j in range(TPB):
                    link(dve.bn_aggr(mean_var[:, half, j, :], stats[:, half, j, :]), j == TPB - 1)
                if kind == "rms":
                    link(dve.tensor_tensor(second[:, half, :], mean_var[:, half, :, 0], mean_var[:, half, :, 0], ALU.mult))
                    link(dve.tensor_tensor(second[:, half, :], second[:, half, :], mean_var[:, half, :, 1], ALU.add))
                    dve.tensor_scalar(second[:, half, :], second[:, half, :], eps, None, ALU.add).then_inc(variance_ready, 1)
                else:
                    dve.tensor_scalar(second[:, half, :], mean_var[:, half, :, 1], eps, None, ALU.add).then_inc(variance_ready, 1)

            def scale_rows(c):
                half = c % 2
                dve.wait_ge(deviation_ready, c + 1)
                link(dve.reciprocal(inverse[:, half, :], deviation[:, half, :]))
                for j in range(TPB):
                    if kind == "rms":
                        last = dve.tensor_scalar(rows[:, half, j, :], src[:, c * TPB + j, :], inverse[:, half, j:j + 1],
                                                 None, ALU.mult)
                    else:
                        last = dve.tensor_scalar(rows[:, half, j, :], src[:, c * TPB + j, :], mean_var[:, half, j, 0:1],
                                                 inverse[:, half, j:j + 1], ALU.subtract, ALU.mult)
                last.then_inc(rows_ready, 1)

            def split(c):
                hi, lo = parts
                for k in range(KT):
                    i = c * KT + k
                    here = slice(c * S, (c + 1) * S)
                    dve.wait_ge(scaled_ready, i + 1)
                    link(dve.tensor_copy(hi[:, k, here], scaled[:, i % 2, :]))
                    dve.tensor_tensor(lo[:, k, here], scaled[:, i % 2, :], hi[:, k, here].bitcast(F32),
                                      ALU.subtract).then_inc(split_done, 1)

            for c in range(B):
                rows_of(c)
                if kind != "none":
                    scale_rows(c)
                if parts and c:
                    split(c - 1)
            if parts:
                split(B - 1)

        @block.tensor
        def _(pe):
            for c in range(B):
                pe.wait_ge(rows_ready, c + 1)
                for k in range(KT):
                    if c >= 2:
                        pe.wait_ge(scaled_ready, (c - 2) * KT + k + 1)
                    for j in range(TPB):
                        last = pe.transpose(turned[:, c % 2, k, j * P:(j + 1) * P], rows[:, c % 2, j, k * P:(k + 1) * P],
                                            n.ident[:, :])
                    last.then_inc(tile_turned, 1)

        @block.scalar
        def _(act):
            def roots(c):
                act.wait_ge(variance_ready, c + 1)
                act.activation(deviation[:, c % 2, :], second[:, c % 2, :], ACT.Sqrt).then_inc(deviation_ready, 1)

            if kind != "none":
                roots(0)
            for c in range(B):
                if kind != "none" and c + 1 < B:
                    roots(c + 1)
                for k in range(KT):
                    i = c * KT + k
                    act.wait_ge(tile_turned, i + 1)
                    if parts:
                        out = scaled[:, i % 2, :]
                        if i >= 2:
                            act.wait_ge(split_done, i - 1)
                    else:
                        out = plain[:, k, c * S:(c + 1) * S]
                    act.activation(out, turned[:, c % 2, k, :], ACT.Identity,
                                   bias=n.col(offset, k) if offset else 0.0, scale=n.col(scale, k) if scale else 1.0)\
                        .then_inc(scaled_ready, 1)


def l0_attention_stage(n, tag, norm):
    nc = n.nc
    K1 = C + 1
    W = HG * K1
    SCALE = float(HK0) ** -0.5
    PREP = 2 * HG + HG * (KT + 1) + 2 * HG + 1
    with ExitStack() as mem:
        wk, wv, wq, wo = (n.sbuf(f"{tag}_{w}", [P, KT, D], F32, mem) for w in ("wk", "wv", "wqT", "wo"))
        biases = n.sbuf(f"{tag}_biases", [P, 5, HG], F32, mem)
        keys = n.sbuf(f"{tag}_keys", [P, HG, CTOK + 1], F32, mem)
        values = n.sbuf(f"{tag}_values", [P, HG, CTOK], F32, mem)
        key_map = n.sbuf(f"{tag}_key_map", [P, KT, B, HG, K1], F32, mem)
        query_bias = n.sbuf(f"{tag}_query_bias", [P, B, HG, K1], F32, mem)
        value_map = n.sbuf(f"{tag}_value_map", [P, HG // 2, B, D], F32, mem)
        bq_wide = n.sbuf(f"{tag}_bq_wide", [P, HG, P], F32, mem)
        learnt_v = n.sbuf(f"{tag}_learnt_v", [P, HG, HG], F32, mem)
        learnt_out = n.sbuf(f"{tag}_learnt_out", [HG, D], F32, mem)
        learnt_map = n.sbuf(f"{tag}_learnt_map", [H, D], F32, mem)
        soft = n.sbuf(f"{tag}_soft", [P, 2, TPB, HG, K1], F32, mem)
        top = n.sbuf(f"{tag}_top", [P, 2, TPB * HG], F32, mem)
        total = n.sbuf(f"{tag}_total", [P, 2, TPB * HG], F32, mem)
        inverse = n.sbuf(f"{tag}_inverse", [P, 2, TPB * HG], F32, mem)
        probs = n.sbuf(f"{tag}_probs", [P, 2, TPB, HG, C], F32, mem)
        learnt_p = n.sbuf(f"{tag}_learnt_p", [P, TILES, HG], F32, mem)
        learnt_all = n.sbuf(f"{tag}_learnt_all", [P, TILES, H], F32, mem)
        learnt_T = n.sbuf(f"{tag}_learnt_T", [H, TILES, P], F32, mem)
        probs_T = n.sbuf(f"{tag}_probs_T", [P, 2, HG // 2, S], F32, mem)
        wide = n.psum(f"{tag}_wide", [P, TPB, 512], mem)
        turned = n.psum(f"{tag}_turned", [P, 2, S], mem)
        added = n.psum(f"{tag}_added", [P, 2, D], mem)
        scratch = n.dram[f"{tag}_scratch"]

        s = {k: n.sem(f"{tag}_{k}") for k in (
            "wk_loaded", "wv_loaded", "wq_loaded", "wo_loaded", "biases_loaded", "learnt_zeroed",
            "prep_done", "prep_out", "logits_done", "logits_read", "shifted", "exped", "chain",
            "probs_ready", "turned_done", "turned_out", "out_done", "out_added", "learnt_stored", "learnt_p_stored", "learnt_loaded")}
        block = mem.enter_context(nc.Block())
        weights = (("wk", wk, HG), ("wv", wv, 2 * HG), ("wqT", wq, 2 * HG + HG * (KT + 1)), ("wo", wo, PREP))

        def load_weights(sp, g, used_at=None):
            for i, (name, buffer, used) in enumerate(weights):
                if used_at:
                    sp.wait_ge(s["prep_done"], used_at[i])
                sp.dma_start(buffer[:, :, :], n.block(f"{tag}_{name}", g)).then_inc(s[f"{name[:2]}_loaded"], 16)

        def load_biases(sp, head):
            at = COLUMNS[f"{tag}_bq"]
            kinds = n.dram["columns"][:, at:at + 5 * H].rearrange("p (k h) -> p k h", k=5)
            sp.dma_start(biases[:, :, :], kinds[:, :, bass.ds(head, HG)]).then_inc(s["biases_loaded"], 16)

        @block.sync
        def _(sp):
            load_biases(sp, 0)
            load_weights(sp, 0)
            with sp.Fori(1, H // HG) as g:
                head, all_out = sp.snap(g * HG), sp.snap(g * PREP)
                used_at = [sp.snap(g * PREP - (PREP - used)) for _, _, used in weights]
                sp.wait_ge(s["prep_out"], all_out)
                load_biases(sp, head)
                load_weights(sp, g, used_at)

        @block.gpsimd
        def _(pool):
            pool.memset(learnt_v[:, :, :], 0.0).then_inc(s["learnt_zeroed"], 1)

        @block.tensor
        def _(pe):
            pe.sem_inc(s["turned_done"], 4)
            pe.sem_inc(s["out_done"], 8)

            def prepare(g):
                i = 0

                def bank():
                    if i == 0:
                        pe.wait_ge(s["logits_read"], g * B + 1)
                    if i >= TPB:
                        pe.wait_ge(s["prep_out"], g * PREP + i - TPB + 1)
                    return wide[:, i % TPB, :]

                for w, loaded in ((wk, "wk_loaded"), (wv, "wv_loaded")):
                    pe.wait_ge(s[loaded], 16 * (g + 1))
                    for h in range(HG):
                        out = bank()
                        for k in range(KT):
                            last = pe.matmul(out[:, 0:CTOK], w[:, k, h * P:(h + 1) * P], n.ctx_f[:, k, :],
                                             start=k == 0, stop=k == KT - 1)
                        last.then_inc(s["prep_done"], 1)
                        i += 1
                pe.wait_ge(s["wq_loaded"], 16 * (g + 1))
                pe.wait_ge(s["prep_out"], g * PREP + HG)
                for h in range(HG):
                    for k in range(KT + 1):
                        out = bank()
                        left = wq[:, h, k * P:(k + 1) * P] if k < KT else bq_wide[:, h, :]
                        pe.matmul(out[:, 0:CTOK + 1], left, keys[:, h, :], start=True, stop=True)\
                            .then_inc(s["prep_done"], 1)
                        i += 1
                pe.wait_ge(s["wo_loaded"], 16 * (g + 1))
                pe.wait_ge(s["prep_out"], g * PREP + 2 * HG)
                for h in range(HG):
                    for t in range(CTOK // P):
                        out = bank()
                        pe.matmul(out, values[:, h, t * P:(t + 1) * P], wo[:, h, :], start=True, stop=True)\
                            .then_inc(s["prep_done"], 1)
                        i += 1
                out = bank()
                for h in range(HG):
                    last = pe.matmul(out[0:HG, :], learnt_v[:, h, :], wo[:, h, :], start=h == 0, stop=h == HG - 1)
                last.then_inc(s["prep_done"], 1)
                pe.wait_ge(s["prep_out"], (g + 1) * PREP)

            def logits(g, b):
                if b:
                    pe.wait_ge(s["logits_read"], g * B + b + 1)
                for j in range(TPB):
                    at = (b * TPB + j) * P
                    for k in range(KT):
                        last = pe.matmul(wide[:, j, 0:W], norm[:, k, at:at + P],
                                         key_map[:, k, b, :, :].rearrange("p h c -> p (h c)"), start=k == 0, stop=k == KT - 1)
                last.then_inc(s["logits_done"], 1)

            def turn(g, b):
                pe.wait_ge(s["probs_ready"], g * B + b + 1)
                for pair in range(HG // 2):
                    pe.wait_ge(s["turned_out"], 2 * (g * B + b) + pair + 1)
                    for j in range(TPB):
                        last = pe.transpose(turned[:, pair, j * P:(j + 1) * P],
                                            probs[:, b % 2, j, 2 * pair:2 * pair + 2, :].rearrange("p h c -> p (h c)"),
                                            n.ident[:, :])
                    last.then_inc(s["turned_done"], 1)

            def out(g, b):
                pe.wait_ge(s["turned_out"], 2 * (g * B + b) + 4)
                for j in range(TPB):
                    pe.wait_ge(s["out_added"], TPB * (g * B + b) + j + 1)
                    for pair in range(HG // 2):
                        last = pe.matmul(added[:, j % 2, :], probs_T[:, b % 2, pair, j * P:(j + 1) * P],
                                         value_map[:, pair, b, :], start=pair == 0, stop=pair == HG // 2 - 1)
                    last.then_inc(s["out_done"], 1)

            with pe.Fori(0, H // HG) as g:
                prepare(g)
                logits(g, 0)
                for b in range(B):
                    if b + 1 < B:
                        logits(g, b + 1)
                    turn(g, b)
                    out(g, b)
            groups = H // HG * B
            pe.wait_ge(s["learnt_p_stored"], 16 * (H // HG) + 16)
            for c in range(B):
                pe.wait_ge(s["turned_out"], 2 * groups + c + 1)
                for j in range(TPB):
                    last = pe.transpose(turned[0:H, c % 2, j * P:(j + 1) * P], learnt_all[:, c * TPB + j, :], n.ident[:, :])
                last.then_inc(s["turned_done"], 1)
            pe.wait_ge(s["learnt_loaded"], 16)
            for t in range(TILES):
                if t % TPB == 0:
                    pe.wait_ge(s["turned_out"], 2 * groups + t // TPB + 3)
                pe.wait_ge(s["out_added"], TPB * groups + t + 1)
                pe.matmul(added[:, t % 2, :], learnt_T[:, t, :], learnt_map[:, :], start=True, stop=True)\
                    .then_inc(s["out_done"], 1)

        @block.scalar
        def _(act):
            act.sem_inc(s["turned_out"], 2)
            act.sem_inc(s["learnt_stored"], 16)

            def spread(out4, bank):
                act.copy(out4[:, :, 0:C], bank[:, 0:CTOK].rearrange("p (b c) -> p b c", b=B))
                return act.copy(out4[:, :, C], bank[:, CTOK:CTOK + 1].to_broadcast([P, B]))

            def prepare(g):
                i = 0

                def bank():
                    act.wait_ge(s["prep_done"], g * PREP + i + 1)
                    return wide[:, i % TPB, :]

                act.wait_ge(s["learnt_zeroed"], 1)
                act.wait_ge(s["biases_loaded"], 16 * (g + 1))
                for h in range(HG):
                    b = bank()
                    if h == 0:
                        act.copy(keys[:, :, CTOK], biases[:, 3, :])
                        act.copy(bq_wide[:, :, :], biases[:, 0, :].unsqueeze(2).to_broadcast([P, HG, P]))
                        diagonal = learnt_v[:, :, :].rearrange("p a b -> p (a b)")[:, 0:HG * HG:HG + 1]
                        act.copy(diagonal, biases[:, 4, :])
                    act.activation(keys[:, h, 0:CTOK], b[:, 0:CTOK], ACT.Identity, bias=biases[:, 1, h:h + 1])\
                        .then_inc(s["prep_out"], 1)
                    i += 1
                for h in range(HG):
                    act.activation(values[:, h, :], bank()[:, 0:CTOK], ACT.Identity, bias=biases[:, 2, h:h + 1])\
                        .then_inc(s["prep_out"], 1)
                    i += 1
                for h in range(HG):
                    for k in range(KT + 1):
                        to = key_map[:, k, :, h, :] if k < KT else query_bias[:, :, h, :]
                        spread(to, bank()).then_inc(s["prep_out"], 1)
                        i += 1
                for h in range(HG):
                    rows = slice(h % 2 * C, h % 2 * C + C)
                    for t in range(CTOK // P):
                        b = bank()
                        act.copy(value_map[rows, h // 2, 2 * t, :], b[0:C, :])
                        act.copy(value_map[rows, h // 2, 2 * t + 1, :], b[C:2 * C, :]).then_inc(s["prep_out"], 1)
                        i += 1
                b = bank()
                act.wait_ge(s["learnt_stored"], 16 * g + 16)
                act.copy(learnt_out[:, :], b[0:HG, :]).then_inc(s["prep_out"], 1)

            def exps(g, b):
                act.wait_ge(s["shifted"], g * B + b + 1)
                act.activation(soft[:, b % 2, :, :, :], soft[:, b % 2, :, :, :], ACT.Exp, scale=SCALE)\
                    .then_inc(s["exped"], 1)

            def turned_copies(g, b):
                act.wait_ge(s["out_done"], TPB * (g * B + b) + 4)
                for pair in range(HG // 2):
                    act.wait_ge(s["turned_done"], 2 * (g * B + b) + pair + 5)
                    act.copy(probs_T[:, b % 2, pair, :], turned[:, pair, :]).then_inc(s["turned_out"], 1)

            with act.Fori(0, H // HG) as g:
                prepare(g)
                exps(g, 0)
                for b in range(B):
                    turned_copies(g, b)
                    if b + 1 < B:
                        exps(g, b + 1)
                act.wait_ge(s["prep_out"], (g + 1) * PREP)
                act.dma_start(scratch[bass.ds(g * HG, HG), :], learnt_out[:, :]).then_inc(s["learnt_stored"], 16)
                act.wait_ge(s["probs_ready"], (g + 1) * B)
                act.dma_start(learnt_all[:, :, bass.ds(g * HG, HG)], learnt_p[:, :, :]).then_inc(s["learnt_p_stored"], 16)
            act.wait_ge(s["learnt_stored"], 16 * (H // HG) + 16)
            act.dma_start(learnt_map[:, :], scratch).then_inc(s["learnt_loaded"], 16)
            for c in range(B):
                act.wait_ge(s["turned_done"], 2 * (H // HG) * B + c + 5)
                act.copy(learnt_T[:, c * TPB:(c + 1) * TPB, :],
                         turned[0:H, c % 2, :].rearrange("p (t q) -> p t q", t=TPB)).then_inc(s["turned_out"], 1)

        @block.vector
        def _(dve):
            dve.sem_inc(s["logits_read"], 1)
            dve.sem_inc(s["out_added"], 2)
            dve.sem_inc(s["learnt_p_stored"], 16)
            LINKS = 3

            def shift(g, b):
                dve.wait_ge(s["logits_done"], g * B + b + 1)
                flat = soft[:, b % 2, :, :, :].rearrange("p t h c -> p t (h c)")
                add = query_bias[:, b, :, :].rearrange("p h c -> p (h c)").unsqueeze(1).to_broadcast([P, TPB, W])
                dve.tensor_tensor(flat, wide[:, :, 0:W], add, ALU.add).then_inc(s["logits_read"], 1)
                dve.wait_ge(s["logits_read"], g * B + b + 2)
                rows = soft[:, b % 2, :, :, :].rearrange("p t h c -> p (t h) c")
                dve.tensor_reduce(top[:, b % 2, :], rows, AX.X, ALU.max).then_inc(s["chain"], 1)
                dve.wait_ge(s["chain"], LINKS * (g * B + b) + 1)
                dve.tensor_tensor(rows, rows, top[:, b % 2, :].unsqueeze(2).to_broadcast([P, TPB * HG, K1]),
                                  ALU.subtract).then_inc(s["shifted"], 1)

            def normalise(g, b):
                rows = soft[:, b % 2, :, :, :].rearrange("p t h c -> p (t h) c")
                dve.wait_ge(s["exped"], g * B + b + 1)
                dve.tensor_reduce(total[:, b % 2, :], rows, AX.X, ALU.add).then_inc(s["chain"], 1)
                dve.wait_ge(s["chain"], LINKS * (g * B + b) + 2)
                dve.reciprocal(inverse[:, b % 2, :], total[:, b % 2, :]).then_inc(s["chain"], 1)
                dve.wait_ge(s["chain"], LINKS * (g * B + b) + 3)
                dve.wait_ge(s["turned_done"], 2 * (g * B + b) + 2)
                if b == 0:
                    dve.wait_ge(s["learnt_p_stored"], 16 * g + 16)
                dve.tensor_tensor(learnt_p[:, b * TPB:(b + 1) * TPB, :].rearrange("p t h -> p (t h)"), rows[:, :, C],
                                  inverse[:, b % 2, :], ALU.mult)
                dve.tensor_tensor(probs[:, b % 2, :, :, :].rearrange("p t h c -> p (t h) c"), rows[:, :, 0:C],
                                  inverse[:, b % 2, :].unsqueeze(2).to_broadcast([P, TPB * HG, C]),
                                  ALU.mult).then_inc(s["probs_ready"], 1)

            def add_out(at, t):
                dve.wait_ge(s["out_done"], at + 9)
                dve.tensor_tensor(n.x[:, t, :], added[:, t % 2, :], n.x[:, t, :], ALU.add).then_inc(s["out_added"], 1)

            with dve.Fori(0, H // HG) as g:
                shift(g, 0)
                for b in range(B):
                    normalise(g, b)
                    if b + 1 < B:
                        shift(g, b + 1)
                    for j in range(TPB):
                        add_out(TPB * (g * B + b) + j, b * TPB + j)
            for t in range(TILES):
                add_out(TPB * (H // HG) * B + t, t)


def l1_attention_stage(n, tag, turned_x):
    nc = n.nc
    SCALE = float(D) ** -0.5
    with ExitStack() as mem:
        names = ("wkT", "wvT", "wq", "woT")
        weights = [n.sbuf(f"{tag}_{w}", [P, KT, D], F32, mem) for w in names]
        wk, wv, wq, wo = weights
        alpha = n.sbuf(f"{tag}_alpha", [P, 1], F32, mem)
        keys = n.sbuf(f"{tag}_keys", [P, KT, CTOK], F32, mem)
        values = n.sbuf(f"{tag}_values", [P, KT, CTOK], F32, mem)
        key_map = n.sbuf(f"{tag}_key_map", [P, KT, CTOK], F32, mem)
        value_map = n.sbuf(f"{tag}_value_map", [C, B, D], F32, mem)
        soft = n.sbuf(f"{tag}_soft", [P, 2, TPB, C], F32, mem)
        top, total, inverse = (n.sbuf(f"{tag}_{w}", [P, 2, TPB], F32, mem) for w in ("top", "total", "inverse"))
        probs = n.sbuf(f"{tag}_probs", [P, 2, TPB, C], F32, mem)
        probs_T = n.sbuf(f"{tag}_probs_T", [C, 2, S], F32, mem)
        work = n.psum(f"{tag}_work", [P, 2, 512], mem)
        score = n.psum(f"{tag}_score", [P, 2, TPB, 2 * C], mem)
        turned = n.psum(f"{tag}_turned", [P, 2, S], mem)
        added = n.psum(f"{tag}_added", [P, 2, D], mem)
        loaded = [n.sem(f"{tag}_{w}_loaded") for w in names]
        alpha_loaded = n.sem(f"{tag}_alpha_loaded")
        s = {k: n.sem(f"{tag}_{k}") for k in ("prep_done", "prep_out", "logits_done", "chain", "shifted", "exped",
                                              "probs_ready", "turned_done", "turned_out", "out_done", "out_added")}
        block = mem.enter_context(nc.Block())

        @block.sync
        def _(sp):
            for name, w, l in zip(names, weights, loaded):
                sp.dma_start(w[:, :, :], n.block(f"{tag}_{name}")).then_inc(l, 16)
            sp.dma_start(alpha[:, :], n.dram["alpha"].to_broadcast([P, 1])).then_inc(alpha_loaded, 16)

        @block.tensor
        def _(pe):
            i = 0

            def bank():
                if i >= 2:
                    pe.wait_ge(s["prep_out"], i - 1)
                return work[:, i % 2, :]

            for w, l in ((wk, loaded[0]), (wv, loaded[1])):
                pe.wait_ge(l, 16)
                for m in range(KT):
                    out = bank()
                    for k in range(KT):
                        last = pe.matmul(out[:, 0:CTOK], w[:, k, m * P:(m + 1) * P], n.ctx_f[:, k, :], start=k == 0, stop=k == KT - 1)
                    last.then_inc(s["prep_done"], 1)
                    i += 1
            pe.wait_ge(loaded[2], 16)
            pe.wait_ge(s["prep_out"], KT)
            for m in range(KT):
                out = bank()
                for k in range(KT):
                    last = pe.matmul(out[:, 0:CTOK], wq[:, k, m * P:(m + 1) * P], keys[:, k, :], start=k == 0, stop=k == KT - 1)
                last.then_inc(s["prep_done"], 1)
                i += 1
            pe.wait_ge(loaded[3], 16)
            pe.wait_ge(s["prep_out"], 2 * KT)
            for b in range(B):
                out = bank()
                for k in range(KT):
                    last = pe.matmul(out[0:C, :], values[:, k, b * C:(b + 1) * C], wo[:, k, :], start=k == 0, stop=k == KT - 1)
                last.then_inc(s["prep_done"], 1)
                i += 1
            pe.wait_ge(s["prep_out"], 4 * KT)

            def logits(b):
                if b >= 2:
                    pe.wait_ge(s["shifted"], b - 1)
                for j in range(TPB):
                    at = (b * TPB + j) * P
                    for k in range(KT):
                        last = pe.matmul(score[:, b % 2, j, :], turned_x[:, k, at:at + P],
                                         key_map[:, k, b // 2 * 2 * C:(b // 2 + 1) * 2 * C], start=k == 0, stop=k == KT - 1)
                last.then_inc(s["logits_done"], 1)

            logits(0)
            for b in range(B):
                if b + 1 < B:
                    logits(b + 1)
                pe.wait_ge(s["probs_ready"], b + 1)
                if b >= 2:
                    pe.wait_ge(s["turned_out"], b - 1)
                for j in range(TPB):
                    last = pe.transpose(turned[0:C, b % 2, j * P:(j + 1) * P], probs[:, b % 2, j, :], n.ident[:, :])
                last.then_inc(s["turned_done"], 1)
                pe.wait_ge(s["turned_out"], b + 1)
                for j in range(TPB):
                    t = b * TPB + j
                    if t >= 2:
                        pe.wait_ge(s["out_added"], t - 1)
                    pe.matmul(added[:, t % 2, :], probs_T[:, b % 2, j * P:(j + 1) * P], value_map[:, b, :], start=True, stop=True)\
                        .then_inc(s["out_done"], 1)

        @block.scalar
        def _(act):
            act.wait_ge(alpha_loaded, 16)
            for i in range(4 * KT):
                act.wait_ge(s["prep_done"], i + 1)
                if i < 3 * KT:
                    to = (keys, values, key_map)[i // KT]
                    act.copy(to[:, i % KT, :], work[:, i % 2, 0:CTOK]).then_inc(s["prep_out"], 1)
                else:
                    act.activation(value_map[:, i % KT, :], work[0:C, i % 2, :], ACT.Identity, scale=alpha[0:C, :])\
                        .then_inc(s["prep_out"], 1)
            for b in range(B):
                act.wait_ge(s["shifted"], b + 1)
                act.activation(soft[:, b % 2, :, :], soft[:, b % 2, :, :], ACT.Exp, scale=SCALE).then_inc(s["exped"], 1)
                act.wait_ge(s["turned_done"], b + 1)
                if b >= 2:
                    act.wait_ge(s["out_done"], (b - 1) * TPB)
                act.copy(probs_T[:, b % 2, :], turned[0:C, b % 2, :]).then_inc(s["turned_out"], 1)

        @block.vector
        def _(dve):
            def softmax(b):
                u = b % 2
                mine = score[:, u, :, b % 2 * C:(b % 2 + 1) * C]
                dve.wait_ge(s["logits_done"], b + 1)
                dve.tensor_reduce(top[:, u, :], mine, AX.X, ALU.max).then_inc(s["chain"], 1)
                dve.wait_ge(s["chain"], 3 * b + 1)
                dve.tensor_tensor(soft[:, u, :, :], mine, top[:, u, :].unsqueeze(2).to_broadcast([P, TPB, C]),
                                  ALU.subtract).then_inc(s["shifted"], 1)
                dve.wait_ge(s["exped"], b + 1)
                dve.tensor_reduce(total[:, u, :], soft[:, u, :, :], AX.X, ALU.add).then_inc(s["chain"], 1)
                dve.wait_ge(s["chain"], 3 * b + 2)
                dve.reciprocal(inverse[:, u, :], total[:, u, :]).then_inc(s["chain"], 1)
                dve.wait_ge(s["chain"], 3 * b + 3)
                if b >= 2:
                    dve.wait_ge(s["turned_done"], b - 1)
                dve.tensor_tensor(probs[:, u, :, :], soft[:, u, :, :], inverse[:, u, :].unsqueeze(2).to_broadcast([P, TPB, C]),
                                  ALU.mult).then_inc(s["probs_ready"], 1)

            softmax(0)
            for b in range(B):
                for j in range(TPB):
                    t = b * TPB + j
                    dve.wait_ge(s["out_done"], t + 1)
                    dve.tensor_tensor(n.x[:, t, :], added[:, t % 2, :], n.x[:, t, :], ALU.add).then_inc(s["out_added"], 1)
                if b + 1 < B:
                    softmax(b + 1)


def l2_attention_stage(n, tag):
    nc = n.nc
    KEYS = S + C
    HALF = KEYS // 2
    CHUNKS = S // P + 1
    GROUPS = H // 4
    INV = 1.0 / HD
    with ExitStack() as mem:
        names = ("wq", "wk", "wv", "wo")
        weights = [n.sbuf(f"{tag}_{w}", [P, KT, D], F32, mem) for w in names]
        wq, wk, wv, wo = weights
        bq_scaled = n.sbuf(f"{tag}_bq_scaled", [P, GROUPS], F32, mem)
        bv_row, bo_row = n.sbuf(f"{tag}_bv_row", [P, D], F32, mem), n.sbuf(f"{tag}_bo_row", [P, D], F32, mem)
        keep = n.sbuf(f"{tag}_keep", [1, CTOK], I32, mem)
        mask = n.sbuf(f"{tag}_mask", [1, CTOK], F32R, mem)
        latents = n.sbuf(f"{tag}_latents", [P, TPB, D], F32, mem)
        rows = n.sbuf(f"{tag}_rows", [P, TPB, D], F32, mem)
        source = n.sbuf(f"{tag}_source", [P, KT, KEYS], F32, mem)
        projected = n.sbuf(f"{tag}_projected", [P, 2, KEYS], F32, mem)
        q_parts = n.sbuf(f"{tag}_q_parts", [P, 2, S], F32R, mem)
        k_parts = n.sbuf(f"{tag}_k_parts", [P, 2, KEYS], F32R, mem)
        q_stack = n.sbuf(f"{tag}_q_stack", [P, 4, S], F32R, mem)
        k_stack = n.sbuf(f"{tag}_k_stack", [P, 4, KEYS], F32R, mem)
        values = n.sbuf(f"{tag}_values", [P, CHUNKS, D], F32, mem)
        padded_v = n.sbuf(f"{tag}_padded_v", [P, CHUNKS, 4, P], F32, mem)
        top = n.sbuf(f"{tag}_top", [P, 2, TPB], F32, mem)
        total = n.sbuf(f"{tag}_total", [P, 2, TPB, 4], F32, mem)
        inverse = n.sbuf(f"{tag}_inverse", [P, TPB, 4], F32, mem)
        wide_inverse = n.sbuf(f"{tag}_wide_inverse", [P, TPB, 4, HD], F32, mem)
        inverse_T = n.sbuf(f"{tag}_inverse_T", [P, S], F32, mem)
        probs = n.sbuf(f"{tag}_probs", [P, 2, TPB, KEYS], F32, mem)
        probs_T = n.sbuf(f"{tag}_probs_T", [P, 2, CHUNKS, S], F32, mem)
        mixed = n.sbuf(f"{tag}_mixed", [P, GROUPS, S], F32, mem)
        slot = n.psum(f"{tag}_slot", [P, 2, 2, 512], mem)
        turned = n.psum(f"{tag}_turned", [P, 2, S], mem)
        gathered = n.psum(f"{tag}_gathered", [P, 2, S], mem)

        loaded = [n.sem(f"{tag}_{w}_loaded") for w in names]
        stack_loaded = [n.sem(f"{tag}_stack{j}_loaded") for j in range(4)]
        s = {k: n.sem(f"{tag}_{k}") for k in (
            "consts_loaded", "setup", "latents_loaded", "ctx_loaded", "rows_loaded", "rows_stored", "zeroed",
            "projected_done", "slot_read", "parts_chain", "parts_ready", "logits_done", "top_ready", "padded_ready",
            "turned0_done", "turned0_out", "turned1_done", "turned1_out", "inverse_ready", "gathered_done",
            "gathered_read", "chain")}
        PROJ = 2 + CHUNKS + 2 * GROUPS
        SLOTS = PROJ + H * TPB
        T0, T1 = 3 * H, 2 * H + GROUPS
        GATHERED = GROUPS + TPB
        STACKED = 16 + 6 * 16 * GROUPS
        LOGITS = H * TPB

        def slot_of_logits(i, t):
            groups_before = 0 if i == 0 else min(GROUPS - 1, (i - 1) // 4 + 1)
            return 2 + CHUNKS + 2 + 4 * i + 2 * groups_before + t

        def slot_of_q(m):
            return 2 if m == 0 else slot_of_logits(4 * (m - 1) + 1, 0) - 2

        block = mem.enter_context(nc.Block())

        @block.sync
        def _(sp):
            def load_latents(tile, token):
                sp.dma_start(latents[:, :, :], n.x[:, bass.ds(tile, TPB), :]).then_inc(s["latents_loaded"], 16)
                sp.dma_start(source[:, :, S:KEYS], n.ctx_f[:, :, bass.ds(token, C)]).then_inc(s["ctx_loaded"], 16)

            sp.dma_start(keep[:, :], n.dram["keep_l2"]).then_inc(s["consts_loaded"], 16)
            load_latents(0, 0)
            for name, w, l in zip(names[:3], weights[:3], loaded[:3]):
                sp.dma_start(w[:, :, :], n.block(f"{tag}_{name}")).then_inc(l, 16)
            sp.dma_start(bv_row[:, :], n.row_broadcast(f"{tag}_bv")).then_inc(s["consts_loaded"], 16)
            sp.dma_start(bo_row[:, :], n.row_broadcast(f"{tag}_bo")).then_inc(s["consts_loaded"], 16)
            sp.dma_start(wo[:, :, :], n.block(f"{tag}_wo")).then_inc(loaded[3], 16)
            sp.wait_ge(s["setup"], 2)
            sp.wait_ge(s["zeroed"], 4)

            def batch(b, more):
                tile, token, stored_at = b * TPB, b * C, 16 * b + 16
                next_tile, next_token = b * TPB + TPB, b * C + C
                all_projected, all_gathered = b * PROJ + 2 * PROJ, b * GATHERED + GATHERED + 2
                parts_at = [b * GROUPS + m + 2 for m in range(GROUPS)]
                slot_free = [b * LOGITS + TPB * (i + 1) for i in range(H)]
                if more:
                    tile, token, stored_at, next_tile, next_token, all_projected, all_gathered = (
                        sp.snap(v) for v in (tile, token, stored_at, next_tile, next_token, all_projected, all_gathered))
                    parts_at, slot_free = [sp.snap(v) for v in parts_at], [sp.snap(v) for v in slot_free]
                x_b, rows_b = n.x[:, bass.ds(tile, TPB), :], n.dram["l2_rows"][:, bass.ds(tile, TPB), :]
                for m in range(GROUPS):
                    sp.wait_ge(s["parts_ready"], parts_at[m])
                    for j in range(4):
                        if m and j >= 2:
                            sp.wait_ge(s["logits_done"], slot_free[4 * m + j])
                        mine = slice(32 * j, 32 * j + 32)
                        for c in range(3):
                            quarter = slice(32 * c, 32 * c + 32)
                            sp.dma_start(q_stack[quarter, j, :].bitcast(F32),
                                         q_parts[mine, c // 2, :].bitcast(F32)).then_inc(stack_loaded[j], 16)
                            sp.dma_start(k_stack[quarter, j, :].bitcast(F32),
                                         k_parts[mine, c % 2, :].bitcast(F32)).then_inc(stack_loaded[j], 16)
                        if m == 0:
                            sp.dma_start(k_stack[96:97, j, S:KEYS].bitcast(F32),
                                         mask[:, bass.ds(token, C)].bitcast(F32)).then_inc(stack_loaded[j], 16)
                    if m == 0:
                        sp.wait_ge(s["rows_stored"], stored_at)
                        sp.dma_start(rows[:, :, :], x_b).then_inc(s["rows_loaded"], 16)
                if more:
                    sp.wait_ge(s["projected_done"], all_projected)
                    load_latents(next_tile, next_token)
                sp.wait_ge(s["gathered_read"], all_gathered)
                sp.dma_start(rows_b, rows[:, :, :]).then_inc(s["rows_stored"], 16)

            with sp.Fori(0, B - 1) as b:
                batch(b, True)
            batch(B - 1, False)
            sp.wait_ge(s["rows_stored"], 16 * B + 16)

        @block.gpsimd
        def _(pool):
            pool.memset(q_stack[96:128, :, :].bitcast(F32), 0.0).then_inc(s["zeroed"], 1)
            pool.memset(k_stack[96:128, :, :].bitcast(F32), 0.0).then_inc(s["zeroed"], 1)
            pool.wait_ge(s["zeroed"], 2)
            pool.memset(padded_v[:, :, :, :], 0.0).then_inc(s["zeroed"], 1)
            pool.wait_ge(s["zeroed"], 3)
            pool.memset(q_stack[96:97, :, :].bitcast(F32), 1.0).then_inc(s["zeroed"], 1)

        @block.tensor
        def _(pe):
            pe.sem_inc(s["projected_done"], PROJ)
            pe.sem_inc(s["logits_done"], 4 * TPB)

            def take_slot(b, u):
                pe.wait_ge(s["slot_read"], b * SLOTS + u + 1)
                return slot[:, u % 2, :, :]

            def turn_input(b):
                pe.wait_ge(s["latents_loaded"], 16 * (b + 1))
                for half in range(2):
                    out = take_slot(b, half)
                    for k in range(2):
                        kt = 2 * half + k
                        for j in range(TPB):
                            last = pe.transpose(out[:, k, j * P:(j + 1) * P], latents[:, j, kt * P:(kt + 1) * P], n.ident[:, :])
                    last.then_inc(s["projected_done"], 1)

            def project_values(b):
                pe.wait_ge(loaded[2], 16)
                for c in range(CHUNKS):
                    out = take_slot(b, 4 + c)
                    at = min(c * P, KEYS - P)
                    for k in range(KT):
                        last = pe.matmul(out[:, 0, :], source[:, k, at:at + P], wv[:, k, :],
                                         start=k == 0, stop=k == KT - 1)
                    last.then_inc(s["projected_done"], 1)

            def project(b, m):
                if m == 0:
                    pe.wait_ge(s["slot_read"], b * SLOTS + 2 + 2)
                    pe.wait_ge(s["ctx_loaded"], 16 * (b + 1))
                out = take_slot(b, slot_of_q(m))
                for k in range(KT):
                    last = pe.matmul(out[:, 0, :], wq[:, k, m * P:(m + 1) * P], source[:, k, 0:S], start=k == 0, stop=k == KT - 1)
                last.then_inc(s["projected_done"], 1)
                out = take_slot(b, slot_of_q(m) + 1)
                for half in range(2):
                    for k in range(KT):
                        last = pe.matmul(out[:, half, 0:HALF], wk[:, k, m * P:(m + 1) * P],
                                         source[:, k, half * HALF:(half + 1) * HALF], start=k == 0, stop=k == KT - 1)
                last.then_inc(s["projected_done"], 1)

            def logits(b, i, t):
                m, j = i // 4, i % 4
                if t == 0:
                    pe.wait_ge(stack_loaded[j], b * STACKED + 16 + 96 * (m + 1) + 1)
                out = take_slot(b, slot_of_logits(i, t))
                for half in range(2):
                    last = pe.matmul(out[:, half, 0:HALF], q_stack[:, j, t * P:(t + 1) * P],
                                     k_stack[:, j, half * HALF:(half + 1) * HALF], start=True, stop=True)
                last.then_inc(s["logits_done"], 1)

            def turn(b, i, c):
                bank = c % 2
                if c == 0:
                    pe.wait_ge(s["slot_read"], b * SLOTS + slot_of_logits(i, TPB - 1) + 3)
                at = b * T1 + 2 * i + max(0, (i - 1) // 4) + c // 2 if bank else b * T0 + 3 * i + c // 2
                pe.wait_ge(s[f"turned{bank}_out"], at + 1)
                first = min(c * P, KEYS - P)
                for t in range(TPB):
                    last = pe.transpose(turned[:, bank, t * P:(t + 1) * P], probs[:, i % 2, t, first:first + P],
                                        n.ident[:, :])
                last.then_inc(s[f"turned{bank}_done"], 1)

            def mix(b, i, c):
                m, j = i // 4, i % 4
                if c == 0:
                    pe.wait_ge(s["padded_ready"], b * H + i + 1)
                    pe.wait_ge(s["turned0_out"], b * T0 + 3 * i + 4)
                    pe.wait_ge(s["turned1_out"], b * T1 + 2 * i + max(0, (i - 1) // 4) + 3)
                    if j == 0:
                        pe.wait_ge(s["gathered_read"], b * GATHERED + m + 1)
                last = pe.matmul(gathered[:, m % 2, :], padded_v[:, c, j, :], probs_T[:, i % 2, c, :],
                                 start=(j == 0 and c == 0), stop=(j == 3 and c == CHUNKS - 1))
                if c == CHUNKS - 1:
                    last.then_inc(s["gathered_done"], 1)

            def turn_inverse(b, m):
                pe.wait_ge(s["inverse_ready"], b * GROUPS + m + 1)
                pe.wait_ge(s["turned1_out"], b * T1 + 2 * min(4 * m + 5, H) + m + 1)
                for t in range(TPB):
                    last = pe.transpose(turned[:, 1, t * P:(t + 1) * P],
                                        wide_inverse[:, t, :, :].rearrange("p h d -> p (h d)"), n.ident[:, :])
                last.then_inc(s["turned1_done"], 1)

            def project_out(b):
                pe.wait_ge(loaded[3], 16)
                pe.wait_ge(s["gathered_read"], b * GATHERED + GROUPS + 2)
                for t in range(TPB):
                    pe.wait_ge(s["gathered_read"], b * GATHERED + GROUPS + t + 1)
                    for m in range(GROUPS):
                        last = pe.matmul(gathered[:, t % 2, :], mixed[:, m, t * P:(t + 1) * P], wo[:, m, :],
                                         start=m == 0, stop=m == GROUPS - 1)
                    last.then_inc(s["gathered_done"], 1)

            pe.wait_ge(loaded[0], 16)
            pe.wait_ge(loaded[1], 16)
            pe.wait_ge(s["zeroed"], 4)
            with pe.Fori(0, B) as b:
                turn_input(b)
                project(b, 0)
                project_values(b)
                for t in range(TPB):
                    logits(b, 0, t)
                for i in range(H + 1):
                    if i % 4 == 0 and i // 4 + 1 < GROUPS:
                        project(b, i // 4 + 1)
                    for c in range(CHUNKS):
                        if c < TPB and i + 1 < H:
                            logits(b, i + 1, c)
                        if i < H:
                            turn(b, i, c)
                        if i >= 1:
                            mix(b, i - 1, c)
                    if i >= 4 and i % 4 == 0:
                        turn_inverse(b, i // 4 - 1)
                project_out(b)

        @block.scalar
        def _(act):
            act.sem_inc(s["slot_read"], 2)
            act.sem_inc(s["turned0_out"], 1)
            act.mul(bq_scaled[:, :], n.columns[:, COLUMNS[f"{tag}_bq"]:COLUMNS[f"{tag}_bq"] + GROUPS], INV).then_inc(s["setup"], 1)
            act.wait_ge(s["setup"], 2)

            def projections(b, m):
                u = slot_of_q(m)
                done = b * PROJ + PROJ + (2 if m == 0 else 2 + CHUNKS + 2 * m)
                act.wait_ge(s["projected_done"], done + 1)
                act.wait_ge(s["parts_ready"], b * GROUPS + m + 1)
                act.activation(projected[:, 0, 0:S], slot[:, u % 2, 0, :], ACT.Identity, bias=bq_scaled[:, m:m + 1],
                               scale=INV).then_inc(s["slot_read"], 1)
                act.wait_ge(s["projected_done"], done + 2)
                act.activation(projected[:, 1, :].rearrange("p (a k) -> p a k", a=2), slot[:, (u + 1) % 2, :, 0:HALF],
                               ACT.Identity, bias=n.col(f"{tag}_bk", m)).then_inc(s["slot_read"], 1)

            def exps(b, i, t):
                if i >= 2:
                    act.wait_ge(s["turned0_done"], b * T0 + 3 * (i - 1))
                act.wait_ge(s["top_ready"], b * LOGITS + TPB * i + t + 1)
                u = slot_of_logits(i, t)
                act.activation(probs[:, i % 2, t, :].rearrange("p (a k) -> p a k", a=2), slot[:, u % 2, :, 0:HALF], ACT.Exp,
                               bias=top[:, i % 2, t:t + 1], accum_out=total[:, i // 4 % 2, t, i % 4:i % 4 + 1])\
                    .then_inc(s["slot_read"], 1)

            with act.Fori(0, B) as b:
                for half in range(2):
                    act.wait_ge(s["projected_done"], b * PROJ + PROJ + half + 1)
                    act.copy(source[:, 2 * half:2 * half + 2, 0:S], slot[:, half, :, :]).then_inc(s["slot_read"], 1)
                projections(b, 0)
                for c in range(CHUNKS):
                    act.wait_ge(s["projected_done"], b * PROJ + PROJ + 4 + c + 1)
                    new = slice(0, P) if c < CHUNKS - 1 else slice(C, P)
                    act.copy(values[new, c, :], slot[new, (4 + c) % 2, 0, :]).then_inc(s["slot_read"], 1)
                for t in range(TPB):
                    exps(b, 0, t)
                for i in range(H):
                    if i % 4 == 0 and i // 4 + 1 < GROUPS:
                        projections(b, i // 4 + 1)
                    for c in range(CHUNKS):
                        if c < TPB and i + 1 < H:
                            exps(b, i + 1, c)
                        if c % 2 == 0:
                            act.wait_ge(s["turned0_done"], b * T0 + 3 * i + c // 2 + 1)
                            act.copy(probs_T[:, i % 2, c, :], turned[:, 0, :]).then_inc(s["turned0_out"], 1)

        @block.vector
        def _(dve):
            dve.sem_inc(s["turned1_out"], 1)
            dve.sem_inc(s["gathered_read"], 2)
            dve.sem_inc(s["rows_stored"], 16)
            dve.sem_inc(s["parts_ready"], 1)
            for j in range(4):
                dve.sem_inc(stack_loaded[j], 1)
            dve.wait_ge(s["consts_loaded"], 16 * 3)
            dve.tensor_scalar(mask[:, :], keep[:, :], 0.0, -1e30, ALU.is_equal, ALU.mult).then_inc(s["setup"], 1)
            dve.wait_ge(s["zeroed"], 4)
            CHAIN = GROUPS + 1

            def split(b, m):
                dve.wait_ge(s["slot_read"], b * SLOTS + slot_of_q(m) + 2 + 2)
                for j in range(4):
                    dve.wait_ge(stack_loaded[j], b * STACKED + (16 + 96 * m if m else 0) + 1)
                dve.tensor_copy(q_parts[:, 0, :], projected[:, 0, 0:S])
                dve.tensor_copy(k_parts[:, 0, :], projected[:, 1, :]).then_inc(s["parts_chain"], 1)
                dve.wait_ge(s["parts_chain"], b * GROUPS + m + 1)
                dve.tensor_tensor(q_parts[:, 1, :], projected[:, 0, 0:S], q_parts[:, 0, :].bitcast(F32), ALU.subtract)
                dve.tensor_tensor(k_parts[:, 1, :], projected[:, 1, :], k_parts[:, 0, :].bitcast(F32),
                                  ALU.subtract).then_inc(s["parts_ready"], 1)

            def maximum(b, i, t):
                dve.wait_ge(s["logits_done"], b * LOGITS + TPB * i + t + 1 + 4 * TPB)
                u = slot_of_logits(i, t)
                dve.tensor_reduce(top[:, i % 2, t:t + 1], slot[:, u % 2, :, 0:HALF], AX.XY, ALU.max,
                                  negate=True).then_inc(s["top_ready"], 1)

            def pad_values(b, i):
                j = i % 4
                if i >= 4:
                    dve.wait_ge(s["gathered_done"], b * (H + TPB) + i - 3)
                if i == 0:
                    dve.wait_ge(s["slot_read"], b * SLOTS + 4 + CHUNKS + 2)
                mine = slice(i * HD, (i + 1) * HD)
                dve.tensor_tensor(padded_v[:, 0:TPB, j, j * HD:(j + 1) * HD], values[:, 0:TPB, mine],
                                  bv_row[:, mine].unsqueeze(1).to_broadcast([P, TPB, HD]), ALU.add)
                dve.tensor_tensor(padded_v[C:P, TPB, j, j * HD:(j + 1) * HD], values[C:P, TPB, mine], bv_row[C:P, mine],
                                  ALU.add).then_inc(s["padded_ready"], 1)

            def invert(b, m):
                dve.wait_ge(s["slot_read"], b * SLOTS + slot_of_logits(4 * m + 3, TPB - 1) + 3)
                dve.reciprocal(inverse[:, :, :], total[:, m % 2, :, :]).then_inc(s["chain"], 1)
                dve.wait_ge(s["chain"], b * CHAIN + m + 1)
                dve.tensor_copy(wide_inverse[:, :, :, :].rearrange("p t h d -> p (t h) d"),
                                inverse[:, :, :].rearrange("p t h -> p (t h)").unsqueeze(2).to_broadcast([P, 4 * TPB, HD]))\
                    .then_inc(s["inverse_ready"], 1)

            def normalise(b, m):
                dve.wait_ge(s["turned1_done"], b * T1 + 2 * min(4 * m + 5, H) + m + 1)
                dve.tensor_copy(inverse_T[:, :], turned[:, 1, :]).then_inc(s["turned1_out"], 1)
                dve.wait_ge(s["turned1_out"], b * T1 + 2 * min(4 * m + 5, H) + m + 2)
                dve.wait_ge(s["gathered_done"], b * (H + TPB) + 4 * m + 4)
                dve.tensor_tensor(mixed[:, m, :], gathered[:, m % 2, :], inverse_T[:, :], ALU.mult).then_inc(s["gathered_read"], 1)

            with dve.Fori(0, B) as b:
                split(b, 0)
                for t in range(TPB):
                    maximum(b, 0, t)
                for i in range(H + 1):
                    if i < H:
                        pad_values(b, i)
                    for c in range(CHUNKS):
                        if c < TPB and i + 1 < H:
                            maximum(b, i + 1, c)
                        if i < H and c % 2:
                            at = b * T1 + 2 * i + max(0, (i - 1) // 4) + c // 2 + 1
                            dve.wait_ge(s["turned1_done"], at)
                            dve.tensor_copy(probs_T[:, i % 2, c, :], turned[:, 1, :]).then_inc(s["turned1_out"], 1)
                    if i % 4 == 0 and i // 4 + 1 < GROUPS:
                        split(b, i // 4 + 1)
                    if i >= 4 and i % 4 == 0:
                        normalise(b, i // 4 - 1)
                    if i % 4 == 3:
                        invert(b, i // 4)
                dve.wait_ge(s["rows_loaded"], 16 * (b + 1))
                dve.tensor_tensor(rows[:, :, :], rows[:, :, :], bo_row[:, :].unsqueeze(1).to_broadcast([P, TPB, D]),
                                  ALU.add).then_inc(s["chain"], 1)
                dve.wait_ge(s["chain"], b * CHAIN + CHAIN)
                for t in range(TPB):
                    dve.wait_ge(s["gathered_done"], b * (H + TPB) + H + t + 1)
                    dve.tensor_tensor(rows[:, t, :], gathered[:, t % 2, :], rows[:, t, :], ALU.add).then_inc(s["gathered_read"], 1)


def l3_attention_stage(n, tag, norm):
    nc = n.nc
    SCALE = float(HD) ** -0.5
    LEAST = -3.4028234663852886e38
    GROUPS, PAIRS = H // 4, H // 2
    PREP = GROUPS + B
    with ExitStack() as mem:
        names = ("wq", "wk", "wv", "wo")
        weights = [n.sbuf(f"{tag}_{w}", [P, KT, D], F32, mem) for w in names]
        wq, wk, wv, wo = weights
        bv_row = n.sbuf(f"{tag}_bv_row", [P, D], F32, mem)
        keep_raw = n.sbuf(f"{tag}_keep_raw", [P, CTOK], U8, mem)
        keep = n.sbuf(f"{tag}_keep", [P, CTOK], F32, mem)
        dropped = n.sbuf(f"{tag}_dropped", [P, CTOK], F32, mem)
        least = n.sbuf(f"{tag}_least", [P, CTOK], F32, mem)
        least_b = n.sbuf(f"{tag}_least_b", [P, C], F32, mem)
        keys = n.sbuf(f"{tag}_keys", [P, GROUPS, B, 4, C], F32, mem)
        all_values = n.sbuf(f"{tag}_all_values", [P, B, PAIRS, P], F32, mem)
        values = n.sbuf(f"{tag}_values", [P, PAIRS, P], F32, mem)
        queries = n.sbuf(f"{tag}_queries", [P, GROUPS, S], F32, mem)
        probs = n.sbuf(f"{tag}_probs", [P, TPB, H, C], F32, mem)
        top, total, inverse = (n.sbuf(f"{tag}_{w}", [P, TPB, H], F32, mem) for w in ("top", "total", "inverse"))
        probs_T = n.sbuf(f"{tag}_probs_T", [P, PAIRS, S], F32, mem)
        mixed = n.sbuf(f"{tag}_mixed", [P, GROUPS, S], F32, mem)
        rows = n.sbuf(f"{tag}_rows", [P, TPB, D], F32, mem)
        work = n.psum(f"{tag}_work", [P, 2, 512], mem)
        score = n.psum(f"{tag}_score", [P, 2, H * C], mem)
        turned = n.psum(f"{tag}_turned", [P, 2, S], mem)

        loaded = [n.sem(f"{tag}_{w}_loaded") for w in names]
        s = {k: n.sem(f"{tag}_{k}") for k in (
            "bv_loaded", "keep_loaded", "zeroed", "mask_ready", "prep_done", "prep_read", "least_b_loaded", "values_loaded",
            "rows_loaded", "rows_stored", "work_done", "work_read", "logits_done", "logits_read", "chain", "shifted",
            "exped", "probs_ready", "turned_done", "turned_out", "projected_done", "rows_added")}
        WORK = 2 * GROUPS
        block = mem.enter_context(nc.Block())

        @block.sync
        def _(sp):
            sp.dma_start(keep_raw[:, :], n.dram["keep_l3"].to_broadcast([P, CTOK])).then_inc(s["keep_loaded"], 16)
            for name, w, l in ((names[i], weights[i], loaded[i]) for i in (1, 2, 0, 3)):
                sp.dma_start(w[:, :, :], n.block(f"{tag}_{name}")).then_inc(l, 16)
            sp.dma_start(bv_row[:, :], n.row_broadcast(f"{tag}_bv")).then_inc(s["bv_loaded"], 16)
            sp.wait_ge(s["mask_ready"], 1)
            sp.wait_ge(s["prep_read"], 4 * GROUPS + 2 * B)
            with sp.Fori(0, B) as b:
                tile = sp.snap(b * TPB)
                x_b = n.x[:, bass.ds(tile, TPB), :]
                sp.wait_ge(s["rows_added"], b * TPB + TPB + 2)
                sp.dma_start(values[:, :, :], all_values[:, bass.ds(b, 1), :, :]).then_inc(s["values_loaded"], 16)
                sp.dma_start(least_b[:, :], least[:, bass.ds(b * C, C)]).then_inc(s["least_b_loaded"], 16)
                sp.wait_ge(s["rows_stored"], 16 * b + 16)
                sp.dma_start(rows[:, :, :], x_b).then_inc(s["rows_loaded"], 16)
                sp.wait_ge(s["rows_added"], b * TPB + 2 * TPB + 2)
                sp.dma_start(x_b, rows[:, :, :]).then_inc(s["rows_stored"], 16)
            sp.wait_ge(s["rows_stored"], 16 * B + 16)

        @block.gpsimd
        def _(pool):
            pool.memset(keys[:, :, :, :, :], 0.0).then_inc(s["zeroed"], 1)
            pool.wait_ge(s["zeroed"], 1)
            pool.memset(all_values[:, :, :, :], 0.0).then_inc(s["zeroed"], 1)

        @block.tensor
        def _(pe):
            pe.sem_inc(s["projected_done"], TPB)
            i = 0
            pe.wait_ge(loaded[1], 16)
            for m in range(GROUPS):
                if i >= 2:
                    pe.wait_ge(s["prep_read"], 4 * (i - 1))
                for k in range(KT):
                    last = pe.matmul(work[:, i % 2, 0:CTOK], wk[:, k, m * P:(m + 1) * P], n.ctx_f[:, k, :], start=k == 0, stop=k == KT - 1)
                last.then_inc(s["prep_done"], 1)
                i += 1
            pe.wait_ge(loaded[2], 16)
            for b in range(B):
                pe.wait_ge(s["prep_read"], 4 * (i - 1) if i - 2 < GROUPS else 4 * GROUPS + 2 * (i - 1 - GROUPS))
                for k in range(KT):
                    last = pe.matmul(work[0:C, i % 2, :], n.ctx_f[:, k, b * C:(b + 1) * C], wv[:, k, :], start=k == 0, stop=k == KT - 1)
                last.then_inc(s["prep_done"], 1)
                i += 1
            pe.wait_ge(s["prep_read"], 4 * GROUPS + 2 * B)
            pe.wait_ge(loaded[0], 16)
            pe.wait_ge(loaded[3], 16)

            def queries_of(b, at):
                for m in range(GROUPS):
                    pe.wait_ge(s["work_read"], at + m + 1)
                    for k in range(KT):
                        last = pe.matmul(work[:, m % 2, :], wq[:, k, m * P:(m + 1) * P], norm[:, k, bass.ds(b * S, S)],
                                         start=k == 0, stop=k == KT - 1)
                    last.then_inc(s["work_done"], 1)

            def logits(b, t):
                if t == 0:
                    pe.wait_ge(s["work_read"], b * WORK + GROUPS + 2)
                if t == 0:
                    pe.wait_ge(s["rows_added"], b * TPB + TPB + 2)
                pe.wait_ge(s["logits_read"], b * TPB + t + 1)
                for m in range(GROUPS):
                    last = pe.matmul(score[:, t % 2, m * 4 * C:(m + 1) * 4 * C], queries[:, m, t * P:(t + 1) * P],
                                     keys[:, m, bass.ds(b, 1), :, :].rearrange("p a h c -> p (a h c)"), start=True, stop=True)
                last.then_inc(s["logits_done"], 1)

            def turn(b, pair):
                if pair == 0:
                    pe.wait_ge(s["probs_ready"], (b + 1) * TPB)
                pe.wait_ge(s["turned_out"], b * PAIRS + pair + 1)
                for t in range(TPB):
                    last = pe.transpose(turned[:, pair % 2, t * P:(t + 1) * P],
                                        probs[:, t, 2 * pair:2 * pair + 2, :].rearrange("p h c -> p (h c)"), n.ident[:, :])
                last.then_inc(s["turned_done"], 1)

            def mix(b, m, at):
                pe.wait_ge(s["turned_out"], b * PAIRS + 2 * m + 4)
                if m == 0:
                    pe.wait_ge(s["values_loaded"], 16 * (b + 1))
                pe.wait_ge(s["work_read"], at + m + 1)
                for half in range(2):
                    last = pe.matmul(work[:, m % 2, :], values[:, 2 * m + half, :], probs_T[:, 2 * m + half, :],
                                     start=half == 0, stop=half == 1)
                last.then_inc(s["work_done"], 1)

            def project(b, t, at):
                if t == 0:
                    pe.wait_ge(s["work_read"], at + GROUPS + 2)
                pe.wait_ge(s["rows_added"], b * TPB + t + 1 + TPB)
                for m in range(GROUPS):
                    last = pe.matmul(score[:, t % 2, 0:D], mixed[:, m, t * P:(t + 1) * P], wo[:, m, :],
                                     start=m == 0, stop=m == GROUPS - 1)
                last.then_inc(s["projected_done"], 1)

            def batch(b, more):
                for t in range(TPB):
                    logits(b, t)
                at = b * WORK + GROUPS
                if more:
                    queries_of(b + 1, at)
                    at = at + GROUPS
                for m in range(GROUPS):
                    turn(b, 2 * m)
                    turn(b, 2 * m + 1)
                    if m:
                        mix(b, m - 1, at)
                mix(b, GROUPS - 1, at)
                for t in range(TPB):
                    project(b, t, at)

            queries_of(0, 0)
            with pe.Fori(0, B - 1) as b:
                batch(b, True)
            batch(B - 1, False)

        @block.scalar
        def _(act):
            act.sem_inc(s["work_read"], 2)
            act.sem_inc(s["turned_out"], 2)
            act.wait_ge(s["prep_read"], 4 * GROUPS + 2 * B)

            def queries_of(at):
                for m in range(GROUPS):
                    act.wait_ge(s["work_done"], at + m + 1)
                    act.activation(queries[:, m, :], work[:, m % 2, :], ACT.Identity, bias=n.col(f"{tag}_bq", m))\
                        .then_inc(s["work_read"], 1)

            def exps(b, t):
                act.wait_ge(s["shifted"], b * TPB + t + 1)
                act.activation(probs[:, t, :, :], probs[:, t, :, :], ACT.Exp, scale=SCALE).then_inc(s["exped"], 1)

            def mixed_of(m, at):
                act.wait_ge(s["work_done"], at + m + 1)
                act.copy(mixed[:, m, :], work[:, m % 2, :]).then_inc(s["work_read"], 1)

            def batch(b, more):
                at = b * WORK + GROUPS
                exps(b, 0)
                exps(b, 1)
                if more:
                    queries_of(at)
                    at = at + GROUPS
                exps(b, 2)
                exps(b, 3)
                for m in range(GROUPS):
                    for half in range(2):
                        pair = 2 * m + half
                        act.wait_ge(s["turned_done"], b * PAIRS + pair + 1)
                        act.copy(probs_T[:, pair, :], turned[:, half, :]).then_inc(s["turned_out"], 1)
                    if m:
                        mixed_of(m - 1, at)
                mixed_of(GROUPS - 1, at)

            queries_of(0)
            with act.Fori(0, B - 1) as b:
                batch(b, True)
            batch(B - 1, False)

        @block.vector
        def _(dve):
            dve.sem_inc(s["logits_read"], 2)
            dve.sem_inc(s["rows_added"], 2 + TPB)
            dve.sem_inc(s["rows_stored"], 16)
            dve.wait_ge(s["keep_loaded"], 16)
            dve.tensor_scalar(dropped[:, :], keep_raw[:, :], 0.0, None, ALU.is_equal).then_inc(s["chain"], 1)
            dve.wait_ge(s["chain"], 1)
            dve.tensor_scalar(keep[:, :], dropped[:, :], -1.0, 1.0, ALU.mult, ALU.add).then_inc(s["chain"], 1)
            dve.tensor_scalar(least[:, :], dropped[:, :], LEAST, None, ALU.mult).then_inc(s["mask_ready"], 1)
            dve.wait_ge(s["chain"], 2)
            dve.wait_ge(s["zeroed"], 2)
            for m in range(GROUPS):
                dve.wait_ge(s["prep_done"], m + 1)
                for j in range(4):
                    mine = slice(32 * j, 32 * j + 32)
                    dve.scalar_tensor_tensor(keys[mine, m, :, j, :], work[mine, m % 2, 0:CTOK].rearrange("p (b c) -> p b c", b=B),
                                             n.col(f"{tag}_bk", m)[mine, :], keep[mine, :].rearrange("p (b c) -> p b c", b=B),
                                             ALU.add, ALU.mult).then_inc(s["prep_read"], 1)
            dve.wait_ge(s["bv_loaded"], 16)
            for b in range(B):
                dve.wait_ge(s["prep_done"], GROUPS + b + 1)
                for odd in range(2):
                    pick = "p (a c o d) -> p a c o d"
                    out = all_values[odd * C:(odd + 1) * C, b, :, :].rearrange("p (a c) n -> p a (c n)", c=2)
                    source = work[0:C, (GROUPS + b) % 2, :].rearrange(pick, a=4, c=2, o=2)
                    bias = bv_row[0:C, :].rearrange(pick, a=4, c=2, o=2)
                    for c in range(2):
                        at = c * P + (2 * c + odd) * HD
                        instruction = dve.tensor_tensor(out[:, :, at:at + HD], source[:, :, c, odd, :], bias[:, :, c, odd, :],
                                                        ALU.add)
                    instruction.then_inc(s["prep_read"], 1)
            BEFORE = 2
            LINKS = 3 * TPB

            def shift(b, t):
                u = t % 2
                dve.wait_ge(s["logits_done"], b * TPB + t + 1)
                if t == 0:
                    dve.wait_ge(s["least_b_loaded"], 16 * (b + 1))
                dve.tensor_tensor(probs[:, t, :, :], score[:, u, :].rearrange("p (h c) -> p h c", h=H),
                                  least_b[:, :].unsqueeze(1).to_broadcast([P, H, C]), ALU.add).then_inc(s["logits_read"], 1)
                dve.wait_ge(s["logits_read"], b * TPB + t + 3)
                dve.tensor_reduce(top[:, t, :], probs[:, t, :, :], AX.X, ALU.max).then_inc(s["chain"], 1)
                dve.wait_ge(s["chain"], b * LINKS + BEFORE + (1 if t == 0 else 3 * t - 1))
                dve.tensor_tensor(probs[:, t, :, :], probs[:, t, :, :], top[:, t, :].unsqueeze(2).to_broadcast([P, H, C]),
                                  ALU.subtract).then_inc(s["shifted"], 1)

            def normalise(b, t):
                before = min(3 * t + 2, 3 * TPB - 2)
                dve.wait_ge(s["exped"], b * TPB + t + 1)
                dve.tensor_reduce(total[:, t, :], probs[:, t, :, :], AX.X, ALU.add).then_inc(s["chain"], 1)
                dve.wait_ge(s["chain"], b * LINKS + BEFORE + before + 1)
                dve.reciprocal(inverse[:, t, :], total[:, t, :]).then_inc(s["chain"], 1)
                dve.wait_ge(s["chain"], b * LINKS + BEFORE + before + 2)
                dve.tensor_tensor(probs[:, t, :, :], probs[:, t, :, :], inverse[:, t, :].unsqueeze(2).to_broadcast([P, H, C]),
                                  ALU.mult).then_inc(s["probs_ready"], 1)

            with dve.Fori(0, B) as b:
                shift(b, 0)
                for t in range(TPB):
                    if t + 1 < TPB:
                        shift(b, t + 1)
                    normalise(b, t)
                dve.wait_ge(s["rows_loaded"], 16 * (b + 1))
                for t in range(TPB):
                    dve.wait_ge(s["projected_done"], b * TPB + t + 1 + TPB)
                    dve.tensor_tensor(rows[:, t, :], score[:, t % 2, 0:D], rows[:, t, :], ALU.add).then_inc(s["rows_added"], 1)


def mlp_stage(n, tag, first, second, bias, activation, parts, first_block):
    nc = n.nc
    norm_hi, norm_lo = parts
    with ExitStack() as mem:
        raw1, w1h, w1l = first_block
        raw2 = n.sbuf(f"{tag}_raw2", [P, KT, D], F32, mem)
        w2h, w2l = n.sbuf(f"{tag}_w2h", [P, KT, D], F32R, mem), n.sbuf(f"{tag}_w2l", [P, KT, D], F32R, mem)
        bias_block = n.sbuf(f"{tag}_bias_block", [P, KT], F32, mem)
        bias_loaded = n.sem(f"{tag}_bias_loaded")
        hidden = n.sbuf(f"{tag}_hidden", [P, 2, S], F32, mem)
        hh, hl = n.sbuf(f"{tag}_hh", [P, 2, KT, S], F32R, mem), n.sbuf(f"{tag}_hl", [P, 2, KT, S], F32R, mem)
        up, down = n.psum(f"{tag}_up", [P, KT, S], mem), n.psum(f"{tag}_down", [P, TPB, D], mem)

        raw1_loaded, raw2_loaded = n.sem(f"{tag}_raw1_loaded"), n.sem(f"{tag}_raw2_loaded")
        w1_ready, w2_ready = n.sem(f"{tag}_w1_ready"), n.sem(f"{tag}_w2_ready")
        split_hi = n.sem(f"{tag}_split_hi")
        up_done = n.sem(f"{tag}_up_done")
        hidden_ready = n.sem(f"{tag}_hidden_ready")
        hidden_split = n.sem(f"{tag}_hidden_split")
        down_done, down_free = n.sem(f"{tag}_down_done"), n.sem(f"{tag}_down_free")
        UPS, DOWNS = B * KT, B * TPB
        block = mem.enter_context(nc.Block())

        @block.sync
        def _(sp):
            def loads(f):
                sp.wait_ge(w2_ready, f + 1)
                sp.dma_start(raw2[:, :, :], n.block(second, f)).then_inc(raw2_loaded, 16)
                sp.wait_ge(hidden_ready, f * UPS + KT)
                at = COLUMNS[bias]
                sp.dma_start(bias_block[:, :], n.dram["columns"][:, bass.ds(f * KT + at, KT)]).then_inc(bias_loaded, 16)

            loads(0)
            with sp.Fori(1, FB) as f:
                sp.wait_ge(w1_ready, f + 1)
                sp.dma_start(raw1[:, :, :], n.block(first, f)).then_inc(raw1_loaded, 16)
                loads(f)

        @block.tensor
        def _(pe):
            def ups(f, c):
                for m in range(KT):
                    pe.wait_ge(hidden_ready, f * UPS + c * KT + m + 1)
                    for k in range(KT):
                        last = product3(pe, up[:, m, :],
                                        (w1h[:, k, m * P:(m + 1) * P], w1l[:, k, m * P:(m + 1) * P]),
                                        (norm_hi[:, k, c * S:(c + 1) * S], norm_lo[:, k, c * S:(c + 1) * S]),
                                        k == 0, k == KT - 1)
                    last.then_inc(up_done, 1)

            def downs(f, c):
                pe.wait_ge(hidden_split, f * UPS + (c + 1) * KT + 2)
                for j in range(TPB):
                    pe.wait_ge(down_free, f * DOWNS + c * TPB + j + 1)
                    for m in range(KT):
                        last = product3(pe, down[:, j, :],
                                        (hh[:, c % 2, m, j * P:(j + 1) * P], hl[:, c % 2, m, j * P:(j + 1) * P]),
                                        (w2h[:, m, :], w2l[:, m, :]), m == 0, m == KT - 1)
                    last.then_inc(down_done, 1)

            with pe.Fori(0, FB) as f:
                pe.wait_ge(w1_ready, f + 2)
                ups(f, 0)
                pe.wait_ge(w2_ready, f + 2)
                for c in range(B):
                    if c + 1 < B:
                        ups(f, c + 1)
                    downs(f, c)

        @block.scalar
        def _(act):
            act.sem_inc(hidden_ready, KT)
            with act.Fori(0, FB) as f:
                act.wait_ge(bias_loaded, 16 * (f + 1))
                for i in range(UPS):
                    act.wait_ge(up_done, f * UPS + i + 1)
                    act.wait_ge(hidden_split, f * UPS + i + 1)
                    act.activation(hidden[:, i % 2, :], up[:, i % KT, :], activation,
                                   bias=bias_block[:, i % KT:i % KT + 1])\
                        .then_inc(hidden_ready, 1)

        @block.vector
        def _(dve):
            dve.sem_inc(hidden_split, 2)
            dve.sem_inc(w1_ready, 2)
            dve.sem_inc(w2_ready, 1)
            dve.sem_inc(down_free, TPB)
            SPLITS = 2 + UPS

            def split_weights(f, raw, loaded, hi, lo, ready, at):
                dve.wait_ge(loaded, 16 * (f + 1) if ready is w2_ready else 16 * f)
                dve.tensor_copy(hi[:, :, :], raw[:, :, :]).then_inc(split_hi, 1)
                dve.wait_ge(split_hi, at)
                dve.tensor_tensor(lo[:, :, :], raw[:, :, :], hi[:, :, :].bitcast(F32), ALU.subtract).then_inc(ready, 1)

            def split_hidden(f, c):
                for m in range(KT):
                    i = c * KT + m
                    dve.wait_ge(hidden_ready, f * UPS + KT + i + 1)
                    if m == 0 and c >= 2:
                        dve.wait_ge(down_done, f * DOWNS + (c - 1) * TPB)
                    dve.tensor_copy(hh[:, c % 2, m, :], hidden[:, i % 2, :]).then_inc(split_hi, 1)
                    dve.wait_ge(split_hi, f * SPLITS + 2 + i)
                    dve.tensor_tensor(hl[:, c % 2, m, :], hidden[:, i % 2, :], hh[:, c % 2, m, :].bitcast(F32),
                                      ALU.subtract).then_inc(hidden_split, 1)

            def add_downs(f, c):
                for j in range(TPB):
                    dve.wait_ge(down_done, f * DOWNS + c * TPB + j + 1)
                    dve.tensor_tensor(n.x[:, c * TPB + j, :], down[:, j, :], n.x[:, c * TPB + j, :],
                                      ALU.add).then_inc(down_free, 1)

            def one_block(f, more):
                split_weights(f, raw2, raw2_loaded, w2h, w2l, w2_ready, f * SPLITS + 1)
                split_hidden(f, 0)
                for c in range(B):
                    if c + 1 < B:
                        split_hidden(f, c + 1)
                    if more and c == B - 2:
                        split_weights(f + 1, raw1, raw1_loaded, w1h, w1l, w1_ready, (f + 1) * SPLITS)
                    add_downs(f, c)

            with dve.Fori(0, FB - 1) as f:
                one_block(f, True)
            one_block(FB - 1, False)


def build(nc, dram):
    with ExitStack() as ctx:
        n = Net(nc, ctx, dram)
        for stage in (load_stage, *STAGES, store_stage):
            stage(n)
            n.end_stage()


def mlp_operands(n, tag, mem):
    parts = (n.sbuf(f"{tag}_norm_hi", [P, KT, TOK], F32R, mem), n.sbuf(f"{tag}_norm_lo", [P, KT, TOK], F32R, mem))
    return parts, (n.sbuf(f"{tag}_raw1", [P, KT, D], F32, mem), n.sbuf(f"{tag}_w1h", [P, KT, D], F32R, mem),
                   n.sbuf(f"{tag}_w1l", [P, KT, D], F32R, mem))


def stage_mlp(n, tag, norm_kind, src, eps, scale, offset, row, first, second, bias, activation):
    with ExitStack() as mem:
        parts, first_block = mlp_operands(n, tag, mem)
        normalise_stage(n, f"{tag}_norm", src, scale, offset, row, norm_kind, eps, parts=parts,
                        first_block=(n.block(first), *first_block))
        mlp_stage(n, tag, first, second, bias, activation, parts, first_block)


def l0_mlp(n):
    stage_mlp(n, "l0m", "layer", n.x, 1e-5, "l0m_scale", "l0m_offset", "l0_b2", "l0_fc1", "l0_fc2", "l0_b1", ACT.Gelu)


def l0_attention(tag, row):
    def stage(n):
        with ExitStack() as mem:
            norm = n.sbuf(f"{tag}_norm", [P, KT, TOK], F32, mem)
            normalise_stage(n, f"{tag}_norm", n.x, f"{tag}_scale", f"{tag}_offset", row, "layer", 1e-5, plain=norm)
            l0_attention_stage(n, tag, norm)
    return stage


def l1_attention(n):
    with ExitStack() as mem:
        turned_x = n.sbuf("l1_turned_x", [P, KT, TOK], F32, mem)
        normalise_stage(n, "l1_turn", n.x, None, None, None, "none", 0.0, plain=turned_x)
        l1_attention_stage(n, "l1", turned_x)


def l2_attention(n):
    l2_attention_stage(n, "l2")


def l2_mlp(n):
    with ExitStack() as mem:
        parts, first_block = mlp_operands(n, "l2m", mem)
        with ExitStack() as inner:
            rows = n.sbuf("l2m_rows", [P, TILES, D], F32, inner)
            rows_loaded = n.sem("l2m_rows_loaded")
            with n.nc.Block() as block:
                @block.sync
                def _(sp):
                    sp.dma_start(rows[:, :, :], n.dram["l2_rows"]).then_inc(rows_loaded, 16)
                    sp.wait_ge(rows_loaded, 16)
            normalise_stage(n, "l2m_norm", rows, "l2_scale", None, "l2_b2", "rms", 1e-6, parts=parts,
                            first_block=(n.block("l2_fc1"), *first_block))
        mlp_stage(n, "l2m", "l2_fc1", "l2_fc2", "l2_b1", ACT.Gelu_apprx_tanh, parts, first_block)


def l3_attention(n):
    with ExitStack() as mem:
        norm = n.sbuf("l3_norm", [P, KT, TOK], F32, mem)
        normalise_stage(n, "l3_norm", n.x, "l3_scale", "l3_offset", "l3_bo", "layer", 1e-5, plain=norm)
        l3_attention_stage(n, "l3", norm)


def l3_mlp(n):
    stage_mlp(n, "l3m", "layer", n.x, 1e-5, "l3m_scale", "l3m_offset", "l3_b2", "l3_fc1", "l3_fc2", "l3_b1",
              ACT.Gelu_apprx_tanh)


STAGES = (l0_attention("l0a", "l0a_bo"), l0_attention("l0b", "l0b_bo"), l0_mlp, l1_attention, l2_attention, l2_mlp,
          l3_attention, l3_mlp)


def kernel(**inputs):
    import numpy as _np
    import concourse.bacc as _bacc
    from concourse.bass_utils import run_bass_kernel_spmd as _run

    a = {k: _np.asarray(v) for k, v in inputs.items()}

    def blocks(w):
        r, c = w.shape[0] // 512, w.shape[1] // 512
        w = w.reshape(r, 4, 128, c, 512).transpose(0, 3, 2, 1, 4)
        return w.reshape(r * c, 128, 2048)

    l0, l1, l2, l3 = "L0_xattn_", "L1_xattn_", "L2_xattn_", "L3_xattn_"
    w = []
    for i in "12":
        w += [a[l0 + "wk" + i], a[l0 + "wv" + i], a[l0 + "wq" + i].T, a[l0 + "wo" + i]]
    w += [a[l0 + "w_fc1"], a[l0 + "w_fc2"]]
    w += [a[l1 + "w_k"].T, a[l1 + "w_v"].T, a[l1 + "w_q"], a[l1 + "w_o"].T]
    w += [a[l2 + "q_w"], a[l2 + "kv_w"][:, 0::2], a[l2 + "kv_w"][:, 1::2], a[l2 + "out_w"], a[l2 + "mlp_w1"], a[l2 + "mlp_w2"]]
    w += [a[l3 + "q_w"], a[l3 + "k_w"], a[l3 + "v_w"], a[l3 + "cproj_w"], a[l3 + "fc_w"], a[l3 + "proj_w"]]
    weights = _np.ascontiguousarray(_np.concatenate([blocks(m) for m in w], axis=0))

    c = [a[l0 + "ln1_scale"], a[l0 + "ln1_offset"], a[l0 + "ln2_scale"], a[l0 + "ln2_offset"],
         a[l0 + "ln_mlp_scale"], a[l0 + "ln_mlp_offset"]]
    for i in "12":
        c += [a[l0 + v + i] for v in ("bq", "bk", "bv", "bias_k", "bias_v")]
    c += [a[l0 + "b_fc1"], a[l2 + "q_b"], a[l2 + "kv_b"][0::2], a[l2 + "postnorm_w"], a[l2 + "mlp_b1"]]
    c += [a[l3 + "ln1_w"], a[l3 + "ln1_b"], a[l3 + "q_b"], a[l3 + "k_b"], a[l3 + "ln2_w"], a[l3 + "ln2_b"], a[l3 + "fc_b"]]
    columns = _np.ascontiguousarray(_np.concatenate([v.reshape(-1, 128) for v in c], axis=0).T)

    rows = _np.stack([a[l0 + "bo1"], a[l0 + "bo2"], a[l0 + "b_fc2"], a[l2 + "kv_b"][1::2], a[l2 + "out_b"],
                      a[l2 + "mlp_b2"], a[l3 + "v_b"], a[l3 + "cproj_b"], a[l3 + "proj_b"]])
    arrays = {
        "x": _np.ascontiguousarray(a["x"].reshape(TOK, D)), "ctx": _np.ascontiguousarray(a["ctx_2048"].reshape(CTOK, D)),
        "weights": weights, "columns": columns, "rows": rows,
        "keep_l2": a["mask_BxS2_ik0"].reshape(1, CTOK), "keep_l3": a["mask_BxS2_bf1"].view(_np.uint8).reshape(1, CTOK),
        "alpha": a[l1 + "alpha"].reshape(1, 1),
    }
    nc = _bacc.Bacc("TRN2", target_bir_lowering=False, num_devices=1)
    types = {"float32": F32, "int32": I32, "uint8": U8}
    dram = {k: nc.dram_tensor(f"in_{k}", v.shape, types[str(v.dtype)], kind="ExternalInput").ap() for k, v in arrays.items()}
    dram["out"] = nc.dram_tensor("out_0", (TOK, D), F32, kind="ExternalOutput").ap()
    for tag in ("l0a", "l0b"):
        dram[f"{tag}_scratch"] = nc.dram_tensor(f"{tag}_scratch", (H, D), F32).ap()
    dram["l2_rows"] = nc.dram_tensor("l2_rows_dram", (P, TILES, D), F32).ap()
    build(nc, dram)
    r = _run(nc, [{f"in_{k}": v for k, v in arrays.items()}], core_ids=[0])
    return r.results[0]["out_0"].reshape(B, S, D)
```

```python
from contextlib import ExitStack

import concourse.bass as bass
from concourse import mybir

F32 = mybir.dt.float32
F32R = mybir.dt.float32r
I32 = mybir.dt.int32
U8 = mybir.dt.uint8
ALU = mybir.AluOpType
ACT = mybir.ActivationFunctionType
AX = mybir.AxisListType

P = 128
B = 4
S = 512
C = 64
D = 512
KT = D // P
TOK = B * S
TILES = TOK // P
TPB = S // P
CTOK = B * C
F = 2048
FB = F // D
H = 16
HK0 = 128
HG = 4
HD = D // H

BLOCKS = {}


def _count_blocks():
    at = 0
    for name, n in (
        ("l0a_wk", 4), ("l0a_wv", 4), ("l0a_wqT", 4), ("l0a_wo", 4),
        ("l0b_wk", 4), ("l0b_wv", 4), ("l0b_wqT", 4), ("l0b_wo", 4),
        ("l0_fc1", 4), ("l0_fc2", 4),
        ("l1_wkT", 1), ("l1_wvT", 1), ("l1_wq", 1), ("l1_woT", 1),
        ("l2_wq", 1), ("l2_wk", 1), ("l2_wv", 1), ("l2_wo", 1), ("l2_fc1", 4), ("l2_fc2", 4),
        ("l3_wq", 1), ("l3_wk", 1), ("l3_wv", 1), ("l3_wo", 1), ("l3_fc1", 4), ("l3_fc2", 4),
    ):
        BLOCKS[name] = at
        at += n
    return at


N_BLOCKS = _count_blocks()

COLUMN_SIZES = (
    ("l0a_scale", 4), ("l0a_offset", 4), ("l0b_scale", 4), ("l0b_offset", 4), ("l0m_scale", 4), ("l0m_offset", 4),
    ("l0a_bq", 16), ("l0a_bk", 16), ("l0a_bv", 16), ("l0a_bias_k", 16), ("l0a_bias_v", 16),
    ("l0b_bq", 16), ("l0b_bk", 16), ("l0b_bv", 16), ("l0b_bias_k", 16), ("l0b_bias_v", 16),
    ("l0_b1", 16), ("l2_bq", 4), ("l2_bk", 4), ("l2_scale", 4), ("l2_b1", 16),
    ("l3_scale", 4), ("l3_offset", 4), ("l3_bq", 4), ("l3_bk", 4), ("l3m_scale", 4), ("l3m_offset", 4), ("l3_b1", 16),
)
COLUMNS = {}
N_COLUMNS = 0
for _name, _n in COLUMN_SIZES:
    COLUMNS[_name] = N_COLUMNS
    N_COLUMNS += _n

ROW_NAMES = ("l0a_bo", "l0b_bo", "l0_b2", "l2_bv", "l2_bo", "l2_b2", "l3_bv", "l3_bo", "l3_b2")
ROWS = {n: i for i, n in enumerate(ROW_NAMES)}


class Net:

    def __init__(self, nc, ctx, dram):
        self.nc, self.ctx, self.dram, self.stage_sems = nc, ctx, dram, []
        self.x = self.sbuf("x", [P, TILES, D], F32)
        self.ctx_f = self.sbuf("ctx_f", [P, KT, CTOK], F32)
        self.ident = self.sbuf("ident", [P, P], F32)
        self.columns = self.sbuf("columns", [P, N_COLUMNS], F32)

    def sbuf(self, name, shape, dt, ctx=None):
        return (ctx or self.ctx).enter_context(self.nc.sbuf_tensor(name, shape, dt))

    def psum(self, name, shape, ctx):
        return ctx.enter_context(self.nc.psum_tensor(name, shape, F32))

    def sem(self, name):
        self.stage_sems.append(self.nc.alloc_semaphore(name=name))
        return self.stage_sems[-1]

    def end_stage(self):
        self.nc.clear_and_free_semaphores(self.stage_sems)
        self.nc.all_engine_barrier()
        self.stage_sems = []

    def col(self, name, j=0):
        at = COLUMNS[name] + j
        return self.columns[:, at:at + 1]

    def row_broadcast(self, name):
        return self.dram["rows"][ROWS[name]:ROWS[name] + 1, :].to_broadcast([P, D])

    def block(self, name, i=0):
        return self.dram["weights"][BLOCKS[name] + i]


def product3(pe, out, left, right, start, stop):
    (lh, ll), (rh, rl) = left, right
    pe.matmul(out, lh, rh, start=start, stop=False)
    pe.matmul(out, lh, rl, start=False, stop=False)
    return pe.matmul(out, ll, rh, start=False, stop=stop)


def load_stage(n):
    nc = n.nc
    with ExitStack() as mem:
        raw = n.sbuf("ctx_rows", [P, CTOK // P, D], F32, mem)
        turned = n.psum("ctx_turned", [P, KT, D], mem)
        ctx_loaded, columns_loaded = n.sem("ctx_loaded"), n.sem("columns_loaded")
        ident_ready, ctx_turned, ctx_ready = n.sem("ident_ready"), n.sem("ctx_turned"), n.sem("ctx_ready")
        block = mem.enter_context(nc.Block())

        @block.sync
        def _(sp):
            sp.dma_start(raw[:, :, :], n.dram["ctx"].rearrange("(t p) d -> p t d", p=P)).then_inc(ctx_loaded, 16)
            sp.dma_start(n.columns[:, :], n.dram["columns"]).then_inc(columns_loaded, 16)
            sp.wait_ge(columns_loaded, 16)

        @block.gpsimd
        def _(pool):
            pool.memset(n.ident[:, :], 0.0).then_inc(ident_ready, 1)
            pool.wait_ge(ident_ready, 1)
            pool.affine_select(out=n.ident[:, :], in_=n.ident[:, :], compare_op=ALU.not_equal, fill=1.0, base=0,
                               pattern=[[-1, P]], channel_multiplier=1).then_inc(ident_ready, 1)

        @block.tensor
        def _(pe):
            pe.wait_ge(ident_ready, 2)
            pe.wait_ge(ctx_loaded, 16)
            for k in range(KT):
                for t in range(CTOK // P):
                    last = pe.transpose(turned[:, k, t * P:(t + 1) * P], raw[:, t, k * P:(k + 1) * P], n.ident[:, :])
            last.then_inc(ctx_turned, 1)

        @block.vector
        def _(dve):
            dve.wait_ge(ctx_turned, 1)
            dve.tensor_copy(n.ctx_f[:, :, :], turned[:, :, 0:CTOK]).then_inc(ctx_ready, 1)
            dve.wait_ge(ctx_ready, 1)


def store_stage(n):
    nc = n.nc
    with ExitStack() as mem:
        stored = n.sem("stored")
        block = mem.enter_context(nc.Block())

        @block.sync
        def _(sp):
            out_rows = n.dram["out"].rearrange("(t p) d -> p t d", p=P)
            for c in range(B):
                sp.dma_start(out_rows[:, c * TPB:(c + 1) * TPB, :], n.x[:, c * TPB:(c + 1) * TPB, :]).then_inc(stored, 16)
            sp.wait_ge(stored, 16 * B)


def normalise_stage(n, tag, src, scale, offset, kind, eps, parts=None, plain=None, first_block=None, src_dram=None, preload=()):
    nc = n.nc
    RING = 2 * KT
    with ExitStack() as mem:
        rows = n.sbuf(f"{tag}_rows", [P, 2, TPB, D], F32, mem)
        stats = n.sbuf(f"{tag}_stats", [P, 2, TPB, 6], F32, mem)
        mean_var = n.sbuf(f"{tag}_mean_var", [P, 2, TPB, 2], F32, mem)
        second = n.sbuf(f"{tag}_second", [P, 2, TPB], F32, mem)
        deviation = n.sbuf(f"{tag}_deviation", [P, 2, TPB], F32, mem)
        inverse = n.sbuf(f"{tag}_inverse", [P, 2, TPB], F32, mem)
        scaled = n.sbuf(f"{tag}_scaled", [P, RING if parts else 1, D], F32, mem)
        turned = n.psum(f"{tag}_turned", [P, 2, KT, D], mem)
        src_loaded = [n.sem(f"{tag}_src_loaded{c}") for c in range(B)]
        chain = n.sem(f"{tag}_chain")
        variance_ready, deviation_ready = n.sem(f"{tag}_variance"), n.sem(f"{tag}_deviation")
        rows_ready, tile_turned = n.sem(f"{tag}_rows_ready"), n.sem(f"{tag}_turned_ready")
        scaled_ready, split_done = n.sem(f"{tag}_scaled"), n.sem(f"{tag}_split")
        preloaded = n.sem(f"{tag}_preloaded")
        block_loaded, block_split = n.sem(f"{tag}_block_loaded"), n.sem(f"{tag}_block_split")
        block = mem.enter_context(nc.Block())

        @block.sync
        def _(sp):
            if src_dram is not None:
                for c in range(B):
                    sp.dma_start(src[:, c * TPB:(c + 1) * TPB, :], src_dram[:, c * TPB:(c + 1) * TPB, :])\
                        .then_inc(src_loaded[c], 16)
            if first_block:
                sp.dma_start(first_block[1][:, :, :], first_block[0]).then_inc(block_loaded, 16)
            for buffer, weights in preload:
                sp.dma_start(buffer, weights).then_inc(preloaded, 16)
            if preload:
                sp.wait_ge(preloaded, 16 * len(preload))

        @block.gpsimd
        def _(pool):
            if first_block:
                _, raw, hi, lo = first_block
                pool.wait_ge(block_loaded, 16)
                pool.tensor_copy(hi[:, :, :], raw[:, :, :]).then_inc(block_split, 1)
                pool.wait_ge(block_split, 1)
                pool.tensor_tensor(lo[:, :, :], raw[:, :, :], hi[:, :, :].bitcast(F32), ALU.subtract).then_inc(block_split, 1)
                pool.wait_ge(block_split, 2)

        @block.vector
        def _(dve):
            steps = [0]

            def link(instruction, wait=True):
                steps[0] += 1
                instruction.then_inc(chain, 1)
                if wait:
                    dve.wait_ge(chain, steps[0])

            def rows_of(c):
                half = c % 2
                if src_dram is not None:
                    dve.wait_ge(src_loaded[c], 16)
                if kind == "none":
                    if c >= 2:
                        dve.wait_ge(tile_turned, KT * (c - 1))
                    for j in range(TPB):
                        last = dve.tensor_copy(rows[:, half, j, :], src[:, c * TPB + j, :])
                    last.then_inc(rows_ready, 1)
                    return
                for j in range(TPB):
                    link(dve.bn_stats(stats[:, half, j, :], src[:, c * TPB + j, :]), j == TPB - 1)
                for j in range(TPB):
                    link(dve.bn_aggr(mean_var[:, half, j, :], stats[:, half, j, :]), j == TPB - 1)
                if kind == "rms":
                    link(dve.tensor_tensor(second[:, half, :], mean_var[:, half, :, 0], mean_var[:, half, :, 0], ALU.mult))
                    link(dve.tensor_tensor(second[:, half, :], second[:, half, :], mean_var[:, half, :, 1], ALU.add))
                    dve.tensor_scalar(second[:, half, :], second[:, half, :], eps, None, ALU.add).then_inc(variance_ready, 1)
                else:
                    dve.tensor_scalar(second[:, half, :], mean_var[:, half, :, 1], eps, None, ALU.add).then_inc(variance_ready, 1)

            def scale_rows(c):
                half = c % 2
                dve.wait_ge(deviation_ready, c + 1)
                link(dve.reciprocal(inverse[:, half, :], deviation[:, half, :]))
                if c >= 2:
                    dve.wait_ge(tile_turned, KT * (c - 1))
                for j in range(TPB):
                    if kind == "rms":
                        last = dve.tensor_scalar(rows[:, half, j, :], src[:, c * TPB + j, :], inverse[:, half, j:j + 1],
                                                 None, ALU.mult)
                    else:
                        last = dve.tensor_scalar(rows[:, half, j, :], src[:, c * TPB + j, :], mean_var[:, half, j, 0:1],
                                                 inverse[:, half, j:j + 1], ALU.subtract, ALU.mult)
                last.then_inc(rows_ready, 1)

            def split(c):
                hi, lo = parts
                for k in range(KT):
                    i = c * KT + k
                    here = slice(c * S, (c + 1) * S)
                    dve.wait_ge(scaled_ready, i + 1)
                    dve.tensor_tensor(lo[:, k, here], scaled[:, i % RING, :], hi[:, k, here].bitcast(F32),
                                      ALU.subtract).then_inc(split_done, 1)

            rows_of(0)
            for c in range(B):
                if kind != "none" and c < 2:
                    scale_rows(c)
                if c + 1 < B:
                    rows_of(c + 1)
                if parts and c:
                    split(c - 1)
                if kind != "none" and 2 <= c + 1 < B:
                    scale_rows(c + 1)
            if parts:
                split(B - 1)

        @block.tensor
        def _(pe):
            for c in range(B):
                pe.wait_ge(rows_ready, c + 1)
                for k in range(KT):
                    if c >= 2:
                        pe.wait_ge(scaled_ready, (c - 2) * KT + k + 1)
                    for j in range(TPB):
                        last = pe.transpose(turned[:, c % 2, k, j * P:(j + 1) * P], rows[:, c % 2, j, k * P:(k + 1) * P],
                                            n.ident[:, :])
                    last.then_inc(tile_turned, 1)

        @block.scalar
        def _(act):
            def roots(c):
                act.wait_ge(variance_ready, c + 1)
                act.activation(deviation[:, c % 2, :], second[:, c % 2, :], ACT.Sqrt).then_inc(deviation_ready, 1)

            def turned_out(c):
                for k in range(KT):
                    i = c * KT + k
                    act.wait_ge(tile_turned, i + 1)
                    here = slice(c * S, (c + 1) * S)
                    outs = [plain[:, k, here]] if plain is not None else [parts[0][:, k, here], scaled[:, i % RING, :]]
                    if parts and i >= RING:
                        act.wait_ge(split_done, i - RING + 1)
                    for out in outs:
                        last = act.activation(out, turned[:, c % 2, k, :], ACT.Identity,
                                              bias=n.col(offset, k) if offset else 0.0, scale=n.col(scale, k) if scale else 1.0)
                    last.then_inc(scaled_ready, 1)

            if kind != "none":
                roots(0)
            for c in range(B):
                if kind != "none" and c + 1 < B:
                    roots(c + 1)
                turned_out(c)


def add_bias(n, pool, row, added):
    for t in range(TILES):
        pool.tensor_tensor(n.x[:, t, :], n.x[:, t, :], row[:, :], ALU.add).then_inc(added, 1)


def l0_attention_stage(n, tag, norm, blocks, bias_row):
    nc = n.nc
    K1 = C + 1
    W = HG * K1
    SCALE = float(HK0) ** -0.5
    PREP = 2 * HG + HG * (KT + 1) + 2 * HG + 1
    with ExitStack() as mem:
        wk, wv, wq, wo = blocks
        biases = n.sbuf(f"{tag}_biases", [P, 5, HG], F32, mem)
        keys = n.sbuf(f"{tag}_keys", [P, HG, CTOK + 1], F32, mem)
        values = n.sbuf(f"{tag}_values", [P, HG, CTOK], F32, mem)
        key_map = n.sbuf(f"{tag}_key_map", [P, KT, B, HG, K1], F32, mem)
        query_bias = n.sbuf(f"{tag}_query_bias", [P, B, HG, K1], F32, mem)
        map_hi, map_lo = (n.sbuf(f"{tag}_value_map_{w}", [P, HG // 2, B, D], F32R, mem) for w in ("hi", "lo"))
        bq_wide = n.sbuf(f"{tag}_bq_wide", [P, HG, P], F32, mem)
        learnt_v = n.sbuf(f"{tag}_learnt_v", [P, HG, HG], F32, mem)
        learnt_out = n.sbuf(f"{tag}_learnt_out", [HG, D], F32, mem)
        learnt_map = n.sbuf(f"{tag}_learnt_map", [H, D], F32, mem)
        soft = n.sbuf(f"{tag}_soft", [P, 2, TPB, HG, K1], F32, mem)
        top = n.sbuf(f"{tag}_top", [P, 2, TPB * HG], F32, mem)
        total = n.sbuf(f"{tag}_total", [P, 2, TPB * HG], F32, mem)
        inverse = n.sbuf(f"{tag}_inverse", [P, 2, TPB * HG], F32, mem)
        probs = n.sbuf(f"{tag}_probs", [P, 2, TPB, HG, C], F32, mem)
        learnt_p = n.sbuf(f"{tag}_learnt_p", [P, TILES, HG], F32, mem)
        learnt_all = n.sbuf(f"{tag}_learnt_all", [P, TILES, H], F32, mem)
        whole_map = [a.rearrange(f"p {w} -> p ({w})")[:, 0:B * D].rearrange("p (b d) -> p b d", b=B)
                     for a, w in ((soft[:, :, :, :, :], "a t h c"), (probs[:, :, :, :, :], "a t h c"))]
        learnt_T = soft[0:H, :, :, :, :].rearrange("p a t h c -> p (a t h c)")[:, 0:TILES * P]\
            .rearrange("p (t q) -> p t q", t=TILES)
        probs_hi, probs_lo = (n.sbuf(f"{tag}_probs_T_{w}", [P, 2, HG // 2, S], F32R, mem) for w in ("hi", "lo"))
        wide = n.psum(f"{tag}_wide", [P, TPB, 512], mem)
        turned = n.psum(f"{tag}_turned", [P, 2, S], mem)
        added = n.psum(f"{tag}_added", [P, 2, D], mem)
        scratch = n.dram[f"{tag}_scratch"]

        s = {k: n.sem(f"{tag}_{k}") for k in (
            "wk_loaded", "wv_loaded", "wq_loaded", "wo_loaded", "biases_loaded", "learnt_zeroed", "bias_added",
            "prep_done", "prep_out", "logits_done", "logits_read", "shifted", "exped", "chain",
            "probs_ready", "turned_done", "turned_out", "turned_hi", "map_hi", "map_split", "out_done", "out_added", "learnt_stored", "learnt_p_stored", "learnt_loaded")}
        block = mem.enter_context(nc.Block())
        MAPS = 2 * HG
        QUERY_MAPS = MAPS + HG * (CTOK // P) + 1
        weights = (("wk", wk, HG), ("wv", wv, 2 * HG), ("wo", wo, QUERY_MAPS), ("wqT", wq, PREP))

        def load_weights(sp, g, used_at):
            for i, (name, buffer, _) in enumerate(weights):
                sp.wait_ge(s["prep_done"], used_at[i])
                sp.dma_start(buffer[:, :, :], n.block(f"{tag}_{name}", g)).then_inc(s[f"{name[:2]}_loaded"], 16)

        def load_biases(sp, head):
            at = COLUMNS[f"{tag}_bq"]
            kinds = n.dram["columns"][:, at:at + 5 * H].rearrange("p (k h) -> p k h", k=5)
            sp.dma_start(biases[:, :, :], kinds[:, :, bass.ds(head, HG)]).then_inc(s["biases_loaded"], 16)

        @block.sync
        def _(sp):
            load_biases(sp, 0)
            for name, _, _ in weights:
                sp.sem_inc(s[f"{name[:2]}_loaded"], 16)
            with sp.Fori(1, H // HG) as g:
                head, all_out = sp.snap(g * HG), sp.snap(g * PREP)
                used_at = [sp.snap(g * PREP - (PREP - used)) for _, _, used in weights]
                sp.wait_ge(s["prep_out"], all_out)
                load_biases(sp, head)
                load_weights(sp, g, used_at)

        @block.gpsimd
        def _(pool):
            pool.memset(learnt_v[:, :, :], 0.0).then_inc(s["learnt_zeroed"], 1)
            add_bias(n, pool, bias_row, s["bias_added"])

        @block.tensor
        def _(pe):
            pe.sem_inc(s["turned_done"], 4)
            pe.sem_inc(s["out_done"], 8)

            def prepare(g):
                i = 0

                def bank():
                    if i == 0:
                        pe.wait_ge(s["logits_read"], g * B + 1)
                    if i >= TPB:
                        pe.wait_ge(s["prep_out"], g * PREP + i - TPB + 1)
                    return wide[:, i % TPB, :]

                for w, loaded in ((wk, "wk_loaded"), (wv, "wv_loaded")):
                    pe.wait_ge(s[loaded], 16 * (g + 1))
                    for h in range(HG):
                        out = bank()
                        for k in range(KT):
                            last = pe.matmul(out[:, 0:CTOK], w[:, k, h * P:(h + 1) * P], n.ctx_f[:, k, :],
                                             start=k == 0, stop=k == KT - 1)
                        last.then_inc(s["prep_done"], 1)
                        i += 1
                pe.wait_ge(s["wo_loaded"], 16 * (g + 1))
                pe.wait_ge(s["prep_out"], g * PREP + 2 * HG)
                for h in range(HG):
                    for t in range(CTOK // P):
                        out = bank()
                        pe.matmul(out, values[:, h, t * P:(t + 1) * P], wo[:, h, :], start=True, stop=True)\
                            .then_inc(s["prep_done"], 1)
                        i += 1
                out = bank()
                for h in range(HG):
                    last = pe.matmul(out[0:HG, :], learnt_v[:, h, :], wo[:, h, :], start=h == 0, stop=h == HG - 1)
                last.then_inc(s["prep_done"], 1)
                i += 1
                pe.wait_ge(s["wq_loaded"], 16 * (g + 1))
                for h in range(HG):
                    for k in range(KT + 1):
                        out = bank()
                        left = wq[:, h, k * P:(k + 1) * P] if k < KT else bq_wide[:, h, :]
                        pe.matmul(out[:, 0:CTOK + 1], left, keys[:, h, :], start=True, stop=True)\
                            .then_inc(s["prep_done"], 1)
                        i += 1
                pe.wait_ge(s["prep_out"], (g + 1) * PREP)

            def logits_tile(g, b, j):
                if b and j == 0:
                    pe.wait_ge(s["logits_read"], g * B + b + 1)
                at = (b * TPB + j) * P
                for k in range(KT):
                    last = pe.matmul(wide[:, j, 0:W], norm[:, k, at:at + P],
                                     key_map[:, k, b, :, :].rearrange("p h c -> p (h c)"), start=k == 0, stop=k == KT - 1)
                if j == TPB - 1:
                    last.then_inc(s["logits_done"], 1)

            def turn(g, b):
                pe.wait_ge(s["probs_ready"], g * B + b + 1)
                for pair in range(HG // 2):
                    pe.wait_ge(s["turned_out"], 2 * (g * B + b) + pair + 1)
                    for j in range(TPB):
                        last = pe.transpose(turned[:, pair, j * P:(j + 1) * P],
                                            probs[:, b % 2, j, 2 * pair:2 * pair + 2, :].rearrange("p h c -> p (h c)"),
                                            n.ident[:, :])
                    last.then_inc(s["turned_done"], 1)

            def out_tile(g, b, j):
                if b == 0 and j == 0:
                    pe.wait_ge(s["map_split"], (g + 1) * (HG // 2))
                if j == 0:
                    pe.wait_ge(s["turned_out"], 2 * (g * B + b) + 4)
                pe.wait_ge(s["out_added"], TPB * (g * B + b) + j + 1)
                tokens = slice(j * P, (j + 1) * P)
                for pair in range(HG // 2):
                    last = product3(pe, added[:, j % 2, :],
                                    (probs_hi[:, b % 2, pair, tokens], probs_lo[:, b % 2, pair, tokens]),
                                    (map_hi[:, pair, b, :], map_lo[:, pair, b, :]), pair == 0, pair == HG // 2 - 1)
                last.then_inc(s["out_done"], 1)

            with pe.Fori(0, H // HG) as g:
                prepare(g)
                for b in range(B):
                    for j in range(TPB):
                        if b >= 2 and j == TPB - 1:
                            turn(g, b - 1)
                        logits_tile(g, b, j)
                        if b >= 2 and j:
                            out_tile(g, b - 2, j - 1)
                    if b >= 2:
                        out_tile(g, b - 2, TPB - 1)
                    if b == 1:
                        turn(g, 0)
                for j in range(TPB):
                    out_tile(g, B - 2, j)
                turn(g, B - 1)
                for j in range(TPB):
                    out_tile(g, B - 1, j)
            groups = H // HG * B
            pe.wait_ge(s["learnt_p_stored"], 16 * (H // HG) + 16)
            for c in range(B):
                pe.wait_ge(s["turned_out"], 2 * groups + c + 1)
                for j in range(TPB):
                    last = pe.transpose(turned[0:H, c % 2, j * P:(j + 1) * P], learnt_all[:, c * TPB + j, :], n.ident[:, :])
                last.then_inc(s["turned_done"], 1)
            pe.wait_ge(s["learnt_loaded"], 16)
            for t in range(TILES):
                if t % TPB == 0:
                    pe.wait_ge(s["turned_out"], 2 * groups + t // TPB + 3)
                pe.wait_ge(s["out_added"], TPB * groups + t + 1)
                pe.matmul(added[:, t % 2, :], learnt_T[:, t, :], learnt_map[:, :], start=True, stop=True)\
                    .then_inc(s["out_done"], 1)

        @block.scalar
        def _(act):
            act.sem_inc(s["turned_out"], 2)
            act.sem_inc(s["learnt_stored"], 16)

            def spread(out4, bank):
                act.copy(out4[:, :, 0:C], bank[:, 0:CTOK].rearrange("p (b c) -> p b c", b=B))
                return act.copy(out4[:, :, C], bank[:, CTOK:CTOK + 1].to_broadcast([P, B]))

            def prepare(g):
                i = 0

                def bank():
                    act.wait_ge(s["prep_done"], g * PREP + i + 1)
                    return wide[:, i % TPB, :]

                act.wait_ge(s["learnt_zeroed"], 1)
                act.wait_ge(s["biases_loaded"], 16 * (g + 1))
                for h in range(HG):
                    b = bank()
                    if h == 0:
                        act.copy(keys[:, :, CTOK], biases[:, 3, :])
                        act.copy(bq_wide[:, :, :], biases[:, 0, :].unsqueeze(2).to_broadcast([P, HG, P]))
                        diagonal = learnt_v[:, :, :].rearrange("p a b -> p (a b)")[:, 0:HG * HG:HG + 1]
                        act.copy(diagonal, biases[:, 4, :])
                    act.activation(keys[:, h, 0:CTOK], b[:, 0:CTOK], ACT.Identity, bias=biases[:, 1, h:h + 1])\
                        .then_inc(s["prep_out"], 1)
                    i += 1
                for h in range(HG):
                    act.activation(values[:, h, :], bank()[:, 0:CTOK], ACT.Identity, bias=biases[:, 2, h:h + 1])\
                        .then_inc(s["prep_out"], 1)
                    i += 1
                for h in range(HG):
                    rows = slice(h % 2 * C, h % 2 * C + C)
                    for t in range(CTOK // P):
                        b = bank()
                        act.copy(whole_map[h // 2][rows, 2 * t, :], b[0:C, :])
                        act.copy(whole_map[h // 2][rows, 2 * t + 1, :], b[C:2 * C, :]).then_inc(s["prep_out"], 1)
                        i += 1
                b = bank()
                act.wait_ge(s["learnt_stored"], 16 * g + 16)
                act.copy(learnt_out[:, :], b[0:HG, :]).then_inc(s["prep_out"], 1)
                i += 1
                for h in range(HG):
                    for k in range(KT + 1):
                        to = key_map[:, k, :, h, :] if k < KT else query_bias[:, :, h, :]
                        spread(to, bank()).then_inc(s["prep_out"], 1)
                        i += 1

            def exps(g, b):
                act.wait_ge(s["shifted"], g * B + b + 1)
                act.activation(soft[:, b % 2, :, :, :], soft[:, b % 2, :, :, :], ACT.Exp, scale=SCALE)\
                    .then_inc(s["exped"], 1)

            def turned_copies(g, b):
                act.wait_ge(s["out_done"], TPB * (g * B + b) + 4)
                for pair in range(HG // 2):
                    act.wait_ge(s["turned_done"], 2 * (g * B + b) + pair + 5)
                    act.copy(probs_hi[:, b % 2, pair, :], turned[:, pair, :]).then_inc(s["turned_hi"], 1)

            with act.Fori(0, H // HG) as g:
                prepare(g)
                exps(g, 0)
                for b in range(B):
                    turned_copies(g, b)
                    if b + 1 < B:
                        exps(g, b + 1)
                act.wait_ge(s["prep_out"], (g + 1) * PREP)
                act.dma_start(scratch[bass.ds(g * HG, HG), :], learnt_out[:, :]).then_inc(s["learnt_stored"], 16)
                act.wait_ge(s["probs_ready"], (g + 1) * B)
                act.dma_start(learnt_all[:, :, bass.ds(g * HG, HG)], learnt_p[:, :, :]).then_inc(s["learnt_p_stored"], 16)
            act.wait_ge(s["learnt_stored"], 16 * (H // HG) + 16)
            act.dma_start(learnt_map[:, :], scratch).then_inc(s["learnt_loaded"], 16)
            for c in range(B):
                act.wait_ge(s["turned_done"], 2 * (H // HG) * B + c + 5)
                act.copy(learnt_T[:, c * TPB:(c + 1) * TPB, :],
                         turned[0:H, c % 2, :].rearrange("p (t q) -> p t q", t=TPB)).then_inc(s["turned_out"], 1)

        @block.vector
        def _(dve):
            dve.sem_inc(s["logits_read"], 1)
            dve.sem_inc(s["out_added"], 2)
            dve.sem_inc(s["learnt_p_stored"], 16)
            LINKS = 3

            def shift(g, b, between=lambda step: None):
                dve.wait_ge(s["logits_done"], g * B + b + 1)
                flat = soft[:, b % 2, :, :, :].rearrange("p t h c -> p t (h c)")
                add = query_bias[:, b, :, :].rearrange("p h c -> p (h c)").unsqueeze(1).to_broadcast([P, TPB, W])
                dve.tensor_tensor(flat, wide[:, :, 0:W], add, ALU.add).then_inc(s["logits_read"], 1)
                between(0)
                dve.wait_ge(s["logits_read"], g * B + b + 2)
                rows = soft[:, b % 2, :, :, :].rearrange("p t h c -> p (t h) c")
                dve.tensor_reduce(top[:, b % 2, :], rows, AX.X, ALU.max).then_inc(s["chain"], 1)
                between(1)
                dve.wait_ge(s["chain"], LINKS * (g * B + b) + 1)
                dve.tensor_tensor(rows, rows, top[:, b % 2, :].unsqueeze(2).to_broadcast([P, TPB * HG, K1]),
                                  ALU.subtract).then_inc(s["shifted"], 1)

            def normalise(g, b):
                rows = soft[:, b % 2, :, :, :].rearrange("p t h c -> p (t h) c")
                dve.wait_ge(s["exped"], g * B + b + 1)
                dve.tensor_reduce(total[:, b % 2, :], rows, AX.X, ALU.add).then_inc(s["chain"], 1)
                dve.wait_ge(s["chain"], LINKS * (g * B + b) + 2)
                dve.reciprocal(inverse[:, b % 2, :], total[:, b % 2, :]).then_inc(s["chain"], 1)
                dve.wait_ge(s["chain"], LINKS * (g * B + b) + 3)
                dve.wait_ge(s["turned_done"], 2 * (g * B + b) + 2)
                if b == 0:
                    dve.wait_ge(s["learnt_p_stored"], 16 * g + 16)
                dve.tensor_tensor(learnt_p[:, b * TPB:(b + 1) * TPB, :].rearrange("p t h -> p (t h)"), rows[:, :, C],
                                  inverse[:, b % 2, :], ALU.mult)
                dve.tensor_tensor(probs[:, b % 2, :, :, :].rearrange("p t h c -> p (t h) c"), rows[:, :, 0:C],
                                  inverse[:, b % 2, :].unsqueeze(2).to_broadcast([P, TPB * HG, C]),
                                  ALU.mult).then_inc(s["probs_ready"], 1)

            def split_map(g):
                for pair in range(HG // 2):
                    dve.wait_ge(s["prep_out"], g * PREP + MAPS + (pair + 1) * CTOK // C)
                    whole = whole_map[pair]
                    dve.tensor_copy(map_hi[:, pair, :, :], whole).then_inc(s["map_hi"], 1)
                    dve.wait_ge(s["map_hi"], g * (HG // 2) + pair + 1)
                    dve.tensor_tensor(map_lo[:, pair, :, :], whole, map_hi[:, pair, :, :].bitcast(F32), ALU.subtract)\
                        .then_inc(s["map_split"], 1)

            def split_probs(g, b):
                for pair in range(HG // 2):
                    dve.wait_ge(s["turned_hi"], 2 * (g * B + b) + pair + 1)
                    dve.tensor_tensor(probs_lo[:, b % 2, pair, :], turned[:, pair, :], probs_hi[:, b % 2, pair, :].bitcast(F32),
                                      ALU.subtract).then_inc(s["turned_out"], 1)

            def add_out(at, t):
                dve.wait_ge(s["bias_added"], t + 1)
                dve.wait_ge(s["out_done"], at + 9)
                dve.tensor_tensor(n.x[:, t, :], added[:, t % 2, :], n.x[:, t, :], ALU.add).then_inc(s["out_added"], 1)

            def add_outs(g, b, first, end):
                for j in range(first, end):
                    add_out(TPB * (g * B + b) + j, b * TPB + j)

            with dve.Fori(0, H // HG) as g:
                split_map(g)
                shift(g, 0)
                for b in range(B):
                    if b == 0:
                        normalise(g, b)
                        shift(g, b + 1)
                        split_probs(g, b)
                    elif b + 1 < B:
                        normalise(g, b)
                        add_outs(g, b - 1, 0, 2)
                        split_probs(g, b)
                        shift(g, b + 1, lambda step: add_outs(g, b - 1, 2 + step, 3 + step))
                    else:
                        add_outs(g, b - 1, 0, 2)
                        normalise(g, b)
                        split_probs(g, b)
                        add_outs(g, b - 1, 2, TPB)
                add_outs(g, B - 1, 0, TPB)
            for t in range(TILES):
                add_out(TPB * (H // HG) * B + t, t)


def l1_attention_stage(n, tag, turned_x, weights, preload):
    nc = n.nc
    SCALE = float(D) ** -0.5
    with ExitStack() as mem:
        wk, wv, wq, wo = weights
        alpha = n.sbuf(f"{tag}_alpha", [P, 1], F32, mem)
        keys = n.sbuf(f"{tag}_keys", [P, KT, CTOK], F32, mem)
        values = n.sbuf(f"{tag}_values", [P, KT, CTOK], F32, mem)
        key_map = n.sbuf(f"{tag}_key_map", [P, KT, CTOK], F32, mem)
        value_map = n.sbuf(f"{tag}_value_map", [C, B, D], F32, mem)
        soft = n.sbuf(f"{tag}_soft", [P, 2, TPB, C], F32, mem)
        top, total, inverse = (n.sbuf(f"{tag}_{w}", [P, 2, TPB], F32, mem) for w in ("top", "total", "inverse"))
        probs = n.sbuf(f"{tag}_probs", [P, 2, TPB, C], F32, mem)
        probs_T = n.sbuf(f"{tag}_probs_T", [C, 2, S], F32, mem)
        work = n.psum(f"{tag}_work", [P, 2, 512], mem)
        score = n.psum(f"{tag}_score", [P, 2, TPB, 2 * C], mem)
        turned = n.psum(f"{tag}_turned", [P, 2, S], mem)
        added = n.psum(f"{tag}_added", [P, 2, D], mem)
        alpha_loaded, preloaded = n.sem(f"{tag}_alpha_loaded"), n.sem(f"{tag}_preloaded")
        s = {k: n.sem(f"{tag}_{k}") for k in ("prep_done", "prep_out", "logits_done", "chain", "shifted", "exped",
                                              "probs_ready", "turned_done", "turned_out", "out_done", "out_added")}
        block = mem.enter_context(nc.Block())

        @block.sync
        def _(sp):
            sp.dma_start(alpha[:, :], n.dram["alpha"].to_broadcast([P, 1])).then_inc(alpha_loaded, 16)
            for buffer, dram in preload:
                sp.dma_start(buffer, dram).then_inc(preloaded, 16)
            sp.wait_ge(preloaded, 16 * len(preload))

        @block.tensor
        def _(pe):
            i = 0

            def bank():
                if i >= 2:
                    pe.wait_ge(s["prep_out"], i - 1)
                return work[:, i % 2, :]

            for w in (wk, wv):
                for m in range(KT):
                    out = bank()
                    for k in range(KT):
                        last = pe.matmul(out[:, 0:CTOK], w[:, k, m * P:(m + 1) * P], n.ctx_f[:, k, :], start=k == 0, stop=k == KT - 1)
                    last.then_inc(s["prep_done"], 1)
                    i += 1
            pe.wait_ge(s["prep_out"], KT)
            for m in range(KT):
                out = bank()
                for k in range(KT):
                    last = pe.matmul(out[:, 0:CTOK], wq[:, k, m * P:(m + 1) * P], keys[:, k, :], start=k == 0, stop=k == KT - 1)
                last.then_inc(s["prep_done"], 1)
                i += 1
            pe.wait_ge(s["prep_out"], 2 * KT)
            for b in range(B):
                out = bank()
                for k in range(KT):
                    last = pe.matmul(out[0:C, :], values[:, k, b * C:(b + 1) * C], wo[:, k, :], start=k == 0, stop=k == KT - 1)
                last.then_inc(s["prep_done"], 1)
                i += 1
            pe.wait_ge(s["prep_out"], 4 * KT)

            def logits(b):
                if b >= 2:
                    pe.wait_ge(s["shifted"], b - 1)
                for j in range(TPB):
                    at = (b * TPB + j) * P
                    for k in range(KT):
                        last = pe.matmul(score[:, b % 2, j, :], turned_x[:, k, at:at + P],
                                         key_map[:, k, b // 2 * 2 * C:(b // 2 + 1) * 2 * C], start=k == 0, stop=k == KT - 1)
                last.then_inc(s["logits_done"], 1)

            logits(0)
            for b in range(B):
                if b + 1 < B:
                    logits(b + 1)
                pe.wait_ge(s["probs_ready"], b + 1)
                if b >= 2:
                    pe.wait_ge(s["turned_out"], b - 1)
                for j in range(TPB):
                    last = pe.transpose(turned[0:C, b % 2, j * P:(j + 1) * P], probs[:, b % 2, j, :], n.ident[:, :])
                last.then_inc(s["turned_done"], 1)
                pe.wait_ge(s["turned_out"], b + 1)
                for j in range(TPB):
                    t = b * TPB + j
                    if t >= 2:
                        pe.wait_ge(s["out_added"], t - 1)
                    pe.matmul(added[:, t % 2, :], probs_T[:, b % 2, j * P:(j + 1) * P], value_map[:, b, :], start=True, stop=True)\
                        .then_inc(s["out_done"], 1)

        @block.scalar
        def _(act):
            act.wait_ge(alpha_loaded, 16)
            for i in range(4 * KT):
                act.wait_ge(s["prep_done"], i + 1)
                if i < 3 * KT:
                    to = (keys, values, key_map)[i // KT]
                    act.copy(to[:, i % KT, :], work[:, i % 2, 0:CTOK]).then_inc(s["prep_out"], 1)
                else:
                    act.activation(value_map[:, i % KT, :], work[0:C, i % 2, :], ACT.Identity, scale=alpha[0:C, :])\
                        .then_inc(s["prep_out"], 1)
            for b in range(B):
                act.wait_ge(s["shifted"], b + 1)
                act.activation(soft[:, b % 2, :, :], soft[:, b % 2, :, :], ACT.Exp, scale=SCALE).then_inc(s["exped"], 1)
                act.wait_ge(s["turned_done"], b + 1)
                if b >= 2:
                    act.wait_ge(s["out_done"], (b - 1) * TPB)
                act.copy(probs_T[:, b % 2, :], turned[0:C, b % 2, :]).then_inc(s["turned_out"], 1)

        @block.vector
        def _(dve):
            def softmax(b):
                u = b % 2
                mine = score[:, u, :, b % 2 * C:(b % 2 + 1) * C]
                dve.wait_ge(s["logits_done"], b + 1)
                dve.tensor_reduce(top[:, u, :], mine, AX.X, ALU.max).then_inc(s["chain"], 1)
                dve.wait_ge(s["chain"], 3 * b + 1)
                dve.tensor_tensor(soft[:, u, :, :], mine, top[:, u, :].unsqueeze(2).to_broadcast([P, TPB, C]),
                                  ALU.subtract).then_inc(s["shifted"], 1)
                dve.wait_ge(s["exped"], b + 1)
                dve.tensor_reduce(total[:, u, :], soft[:, u, :, :], AX.X, ALU.add).then_inc(s["chain"], 1)
                dve.wait_ge(s["chain"], 3 * b + 2)
                dve.reciprocal(inverse[:, u, :], total[:, u, :]).then_inc(s["chain"], 1)
                dve.wait_ge(s["chain"], 3 * b + 3)
                if b >= 2:
                    dve.wait_ge(s["turned_done"], b - 1)
                dve.tensor_tensor(probs[:, u, :, :], soft[:, u, :, :], inverse[:, u, :].unsqueeze(2).to_broadcast([P, TPB, C]),
                                  ALU.mult).then_inc(s["probs_ready"], 1)

            softmax(0)
            for b in range(B):
                for j in range(TPB):
                    t = b * TPB + j
                    dve.wait_ge(s["out_done"], t + 1)
                    dve.tensor_tensor(n.x[:, t, :], added[:, t % 2, :], n.x[:, t, :], ALU.add).then_inc(s["out_added"], 1)
                if b + 1 < B:
                    softmax(b + 1)


def l2_attention_stage(n, tag, weights):
    nc = n.nc
    KEYS = S + C
    HALF = KEYS // 2
    CHUNKS = S // P + 1
    GROUPS = H // 4
    INV = 1.0 / HD
    with ExitStack() as mem:
        wq, wk, wv, wo = weights
        bq_scaled = n.sbuf(f"{tag}_bq_scaled", [P, GROUPS], F32, mem)
        bv_row, bo_row = n.sbuf(f"{tag}_bv_row", [P, D], F32, mem), n.sbuf(f"{tag}_bo_row", [P, D], F32, mem)
        keep = n.sbuf(f"{tag}_keep", [1, CTOK], I32, mem)
        mask = n.sbuf(f"{tag}_mask", [1, CTOK], F32R, mem)
        latents = n.sbuf(f"{tag}_latents", [P, TPB, D], F32, mem)
        rows = n.sbuf(f"{tag}_rows", [P, TPB, D], F32, mem)
        source = n.sbuf(f"{tag}_source", [P, KT, KEYS], F32, mem)
        projected = n.sbuf(f"{tag}_projected", [P, 2, KEYS], F32, mem)
        q_parts = n.sbuf(f"{tag}_q_parts", [P, 2, S], F32R, mem)
        k_parts = n.sbuf(f"{tag}_k_parts", [P, 2, KEYS], F32R, mem)
        q_stack = n.sbuf(f"{tag}_q_stack", [P, 4, S], F32R, mem)
        k_stack = n.sbuf(f"{tag}_k_stack", [P, 4, KEYS], F32R, mem)
        values = n.sbuf(f"{tag}_values", [P, CHUNKS, D], F32, mem)
        padded_v = n.sbuf(f"{tag}_padded_v", [P, CHUNKS, 4, P], F32, mem)
        top = n.sbuf(f"{tag}_top", [P, 2, TPB], F32, mem)
        total = n.sbuf(f"{tag}_total", [P, 2, TPB, 4], F32, mem)
        inverse = n.sbuf(f"{tag}_inverse", [P, TPB, 4], F32, mem)
        wide_inverse = n.sbuf(f"{tag}_wide_inverse", [P, TPB, 4, HD], F32, mem)
        inverse_T = n.sbuf(f"{tag}_inverse_T", [P, S], F32, mem)
        probs = n.sbuf(f"{tag}_probs", [P, 2, TPB, KEYS], F32, mem)
        probs_T = n.sbuf(f"{tag}_probs_T", [P, 2, CHUNKS, S], F32, mem)
        mixed = n.sbuf(f"{tag}_mixed", [P, GROUPS, S], F32, mem)
        slot = n.psum(f"{tag}_slot", [P, 2, 2, 512], mem)
        turned = n.psum(f"{tag}_turned", [P, 2, S], mem)
        gathered = n.psum(f"{tag}_gathered", [P, 2, S], mem)

        stack_loaded = [n.sem(f"{tag}_stack{j}_loaded") for j in range(4)]
        s = {k: n.sem(f"{tag}_{k}") for k in (
            "consts_loaded", "setup", "latents_loaded", "ctx_loaded", "rows_loaded", "rows_stored", "zeroed",
            "projected_done", "slot_read", "parts_chain", "parts_ready", "logits_done", "top_ready", "padded_ready",
            "turned0_done", "turned0_out", "turned1_done", "turned1_out", "inverse_ready", "gathered_done",
            "gathered_read", "chain")}
        PROJ = 2 + CHUNKS + 2 * GROUPS
        SLOTS = PROJ + H * TPB
        T0, T1 = 3 * H, 2 * H + GROUPS
        GATHERED = GROUPS + TPB
        STACKED = 16 + 6 * 16 * GROUPS
        LOGITS = H * TPB

        def slot_of_logits(i, t):
            groups_before = 0 if i == 0 else min(GROUPS - 1, (i - 1) // 4 + 1)
            return 2 + CHUNKS + 2 + 4 * i + 2 * groups_before + t

        def slot_of_q(m):
            return 2 if m == 0 else slot_of_logits(4 * (m - 1) + 1, 0) - 2

        block = mem.enter_context(nc.Block())

        @block.sync
        def _(sp):
            def load_latents(tile, token):
                sp.dma_start(latents[:, :, :], n.x[:, bass.ds(tile, TPB), :]).then_inc(s["latents_loaded"], 16)
                sp.dma_start(source[:, :, S:KEYS], n.ctx_f[:, :, bass.ds(token, C)]).then_inc(s["ctx_loaded"], 16)

            sp.dma_start(keep[:, :], n.dram["keep_l2"]).then_inc(s["consts_loaded"], 16)
            load_latents(0, 0)
            sp.dma_start(bv_row[:, :], n.row_broadcast(f"{tag}_bv")).then_inc(s["consts_loaded"], 16)
            sp.dma_start(bo_row[:, :], n.row_broadcast(f"{tag}_bo")).then_inc(s["consts_loaded"], 16)
            sp.wait_ge(s["setup"], 2)
            sp.wait_ge(s["zeroed"], 4)

            def batch(b, more):
                tile, token, stored_at = b * TPB, b * C, 16 * b + 16
                next_tile, next_token = b * TPB + TPB, b * C + C
                all_projected, all_gathered = b * PROJ + 2 * PROJ, b * GATHERED + GATHERED + 2
                parts_at = [b * GROUPS + m + 2 for m in range(GROUPS)]
                slot_free = [b * LOGITS + TPB * (i + 1) for i in range(H)]
                if more:
                    tile, token, stored_at, next_tile, next_token, all_projected, all_gathered = (
                        sp.snap(v) for v in (tile, token, stored_at, next_tile, next_token, all_projected, all_gathered))
                    parts_at, slot_free = [sp.snap(v) for v in parts_at], [sp.snap(v) for v in slot_free]
                x_b, rows_b = n.x[:, bass.ds(tile, TPB), :], n.dram["l2_rows"][:, bass.ds(tile, TPB), :]
                for m in range(GROUPS):
                    sp.wait_ge(s["parts_ready"], parts_at[m])
                    for j in range(4):
                        if m and j >= 2:
                            sp.wait_ge(s["logits_done"], slot_free[4 * m + j])
                        mine = slice(32 * j, 32 * j + 32)
                        for c in range(3):
                            quarter = slice(32 * c, 32 * c + 32)
                            sp.dma_start(q_stack[quarter, j, :].bitcast(F32),
                                         q_parts[mine, c // 2, :].bitcast(F32)).then_inc(stack_loaded[j], 16)
                            sp.dma_start(k_stack[quarter, j, :].bitcast(F32),
                                         k_parts[mine, c % 2, :].bitcast(F32)).then_inc(stack_loaded[j], 16)
                        if m == 0:
                            sp.dma_start(k_stack[96:97, j, S:KEYS].bitcast(F32),
                                         mask[:, bass.ds(token, C)].bitcast(F32)).then_inc(stack_loaded[j], 16)
                    if m == 0:
                        sp.wait_ge(s["rows_stored"], stored_at)
                        sp.dma_start(rows[:, :, :], x_b).then_inc(s["rows_loaded"], 16)
                if more:
                    sp.wait_ge(s["projected_done"], all_projected)
                    load_latents(next_tile, next_token)
                sp.wait_ge(s["gathered_read"], all_gathered)
                sp.dma_start(rows_b, rows[:, :, :]).then_inc(s["rows_stored"], 16)

            with sp.Fori(0, B - 1) as b:
                batch(b, True)
            batch(B - 1, False)
            sp.wait_ge(s["rows_stored"], 16 * B + 16)

        @block.gpsimd
        def _(pool):
            pool.memset(q_stack[96:128, :, :].bitcast(F32), 0.0).then_inc(s["zeroed"], 1)
            pool.memset(k_stack[96:128, :, :].bitcast(F32), 0.0).then_inc(s["zeroed"], 1)
            pool.wait_ge(s["zeroed"], 2)
            pool.memset(padded_v[:, :, :, :], 0.0).then_inc(s["zeroed"], 1)
            pool.wait_ge(s["zeroed"], 3)
            pool.memset(q_stack[96:97, :, :].bitcast(F32), 1.0).then_inc(s["zeroed"], 1)

        @block.tensor
        def _(pe):
            pe.sem_inc(s["projected_done"], PROJ)
            pe.sem_inc(s["logits_done"], 4 * TPB)

            def take_slot(b, u):
                pe.wait_ge(s["slot_read"], b * SLOTS + u + 1)
                return slot[:, u % 2, :, :]

            def turn_input(b):
                pe.wait_ge(s["latents_loaded"], 16 * (b + 1))
                for half in range(2):
                    out = take_slot(b, half)
                    for k in range(2):
                        kt = 2 * half + k
                        for j in range(TPB):
                            last = pe.transpose(out[:, k, j * P:(j + 1) * P], latents[:, j, kt * P:(kt + 1) * P], n.ident[:, :])
                    last.then_inc(s["projected_done"], 1)

            def project_values(b):
                for c in range(CHUNKS):
                    out = take_slot(b, 4 + c)
                    at = min(c * P, KEYS - P)
                    for k in range(KT):
                        last = pe.matmul(out[:, 0, :], source[:, k, at:at + P], wv[:, k, :],
                                         start=k == 0, stop=k == KT - 1)
                    last.then_inc(s["projected_done"], 1)

            def project(b, m):
                if m == 0:
                    pe.wait_ge(s["slot_read"], b * SLOTS + 2 + 2)
                    pe.wait_ge(s["ctx_loaded"], 16 * (b + 1))
                out = take_slot(b, slot_of_q(m))
                for k in range(KT):
                    last = pe.matmul(out[:, 0, :], wq[:, k, m * P:(m + 1) * P], source[:, k, 0:S], start=k == 0, stop=k == KT - 1)
                last.then_inc(s["projected_done"], 1)
                out = take_slot(b, slot_of_q(m) + 1)
                for half in range(2):
                    for k in range(KT):
                        last = pe.matmul(out[:, half, 0:HALF], wk[:, k, m * P:(m + 1) * P],
                                         source[:, k, half * HALF:(half + 1) * HALF], start=k == 0, stop=k == KT - 1)
                last.then_inc(s["projected_done"], 1)

            def logits(b, i, t):
                m, j = i // 4, i % 4
                if i == 0 and t == 0:
                    pe.wait_ge(s["zeroed"], 4)
                if t == 0:
                    pe.wait_ge(stack_loaded[j], b * STACKED + 16 + 96 * (m + 1) + 1)
                out = take_slot(b, slot_of_logits(i, t))
                for half in range(2):
                    last = pe.matmul(out[:, half, 0:HALF], q_stack[:, j, t * P:(t + 1) * P],
                                     k_stack[:, j, half * HALF:(half + 1) * HALF], start=True, stop=True)
                last.then_inc(s["logits_done"], 1)

            def turn(b, i, c):
                bank = c % 2
                if c == 0:
                    pe.wait_ge(s["slot_read"], b * SLOTS + slot_of_logits(i, TPB - 1) + 3)
                at = b * T1 + 2 * i + max(0, (i - 1) // 4) + c // 2 if bank else b * T0 + 3 * i + c // 2
                pe.wait_ge(s[f"turned{bank}_out"], at + 1)
                first = min(c * P, KEYS - P)
                for t in range(TPB):
                    last = pe.transpose(turned[:, bank, t * P:(t + 1) * P], probs[:, i % 2, t, first:first + P],
                                        n.ident[:, :])
                last.then_inc(s[f"turned{bank}_done"], 1)

            def mix(b, i, c):
                m, j = i // 4, i % 4
                if c == 0:
                    pe.wait_ge(s["padded_ready"], b * H + i + 1)
                    pe.wait_ge(s["turned0_out"], b * T0 + 3 * i + 4)
                    pe.wait_ge(s["turned1_out"], b * T1 + 2 * i + max(0, (i - 1) // 4) + 3)
                    if j == 0:
                        pe.wait_ge(s["gathered_read"], b * GATHERED + m + 1)
                last = pe.matmul(gathered[:, m % 2, :], padded_v[:, c, j, :], probs_T[:, i % 2, c, :],
                                 start=(j == 0 and c == 0), stop=(j == 3 and c == CHUNKS - 1))
                if c == CHUNKS - 1:
                    last.then_inc(s["gathered_done"], 1)

            def turn_inverse(b, m):
                pe.wait_ge(s["inverse_ready"], b * GROUPS + m + 1)
                pe.wait_ge(s["turned1_out"], b * T1 + 2 * min(4 * m + 5, H) + m + 1)
                for t in range(TPB):
                    last = pe.transpose(turned[:, 1, t * P:(t + 1) * P],
                                        wide_inverse[:, t, :, :].rearrange("p h d -> p (h d)"), n.ident[:, :])
                last.then_inc(s["turned1_done"], 1)

            def project_out(b):
                pe.wait_ge(s["gathered_read"], b * GATHERED + GROUPS + 2)
                for t in range(TPB):
                    pe.wait_ge(s["gathered_read"], b * GATHERED + GROUPS + t + 1)
                    for m in range(GROUPS):
                        last = pe.matmul(gathered[:, t % 2, :], mixed[:, m, t * P:(t + 1) * P], wo[:, m, :],
                                         start=m == 0, stop=m == GROUPS - 1)
                    last.then_inc(s["gathered_done"], 1)

            with pe.Fori(0, B) as b:
                turn_input(b)
                project(b, 0)
                project_values(b)
                for t in range(TPB):
                    logits(b, 0, t)
                for i in range(H + 1):
                    if i % 4 == 0 and i // 4 + 1 < GROUPS:
                        project(b, i // 4 + 1)
                    for c in range(CHUNKS):
                        if c < TPB and i + 1 < H:
                            logits(b, i + 1, c)
                        if i < H:
                            turn(b, i, c)
                        if i >= 1:
                            mix(b, i - 1, c)
                    if i >= 4 and i % 4 == 0:
                        turn_inverse(b, i // 4 - 1)
                project_out(b)

        @block.scalar
        def _(act):
            act.sem_inc(s["slot_read"], 2)
            act.sem_inc(s["turned0_out"], 1)
            act.mul(bq_scaled[:, :], n.columns[:, COLUMNS[f"{tag}_bq"]:COLUMNS[f"{tag}_bq"] + GROUPS], INV).then_inc(s["setup"], 1)
            act.wait_ge(s["setup"], 2)

            def projections(b, m):
                u = slot_of_q(m)
                done = b * PROJ + PROJ + (2 if m == 0 else 2 + CHUNKS + 2 * m)
                act.wait_ge(s["projected_done"], done + 1)
                act.wait_ge(s["parts_ready"], b * GROUPS + m + 1)
                act.activation(projected[:, 0, 0:S], slot[:, u % 2, 0, :], ACT.Identity, bias=bq_scaled[:, m:m + 1],
                               scale=INV).then_inc(s["slot_read"], 1)
                act.wait_ge(s["projected_done"], done + 2)
                act.activation(projected[:, 1, :].rearrange("p (a k) -> p a k", a=2), slot[:, (u + 1) % 2, :, 0:HALF],
                               ACT.Identity, bias=n.col(f"{tag}_bk", m)).then_inc(s["slot_read"], 1)

            def exps(b, i, t):
                if i >= 2:
                    act.wait_ge(s["turned0_done"], b * T0 + 3 * (i - 1))
                act.wait_ge(s["top_ready"], b * LOGITS + TPB * i + t + 1)
                u = slot_of_logits(i, t)
                act.activation(probs[:, i % 2, t, :].rearrange("p (a k) -> p a k", a=2), slot[:, u % 2, :, 0:HALF], ACT.Exp,
                               bias=top[:, i % 2, t:t + 1], accum_out=total[:, i // 4 % 2, t, i % 4:i % 4 + 1])\
                    .then_inc(s["slot_read"], 1)

            with act.Fori(0, B) as b:
                for half in range(2):
                    act.wait_ge(s["projected_done"], b * PROJ + PROJ + half + 1)
                    act.copy(source[:, 2 * half:2 * half + 2, 0:S], slot[:, half, :, :]).then_inc(s["slot_read"], 1)
                projections(b, 0)
                for c in range(CHUNKS):
                    act.wait_ge(s["projected_done"], b * PROJ + PROJ + 4 + c + 1)
                    new = slice(0, P) if c < CHUNKS - 1 else slice(C, P)
                    act.copy(values[new, c, :], slot[new, (4 + c) % 2, 0, :]).then_inc(s["slot_read"], 1)
                for t in range(TPB):
                    exps(b, 0, t)
                for i in range(H):
                    if i % 4 == 0 and i // 4 + 1 < GROUPS:
                        projections(b, i // 4 + 1)
                    for c in range(CHUNKS):
                        if c < TPB and i + 1 < H:
                            exps(b, i + 1, c)
                        if c % 2 == 0:
                            act.wait_ge(s["turned0_done"], b * T0 + 3 * i + c // 2 + 1)
                            act.copy(probs_T[:, i % 2, c, :], turned[:, 0, :]).then_inc(s["turned0_out"], 1)

        @block.vector
        def _(dve):
            dve.sem_inc(s["turned1_out"], 1)
            dve.sem_inc(s["gathered_read"], 2)
            dve.sem_inc(s["rows_stored"], 16)
            dve.sem_inc(s["parts_ready"], 1)
            for j in range(4):
                dve.sem_inc(stack_loaded[j], 1)
            dve.wait_ge(s["consts_loaded"], 16 * 3)
            dve.tensor_scalar(mask[:, :], keep[:, :], 0.0, -1e30, ALU.is_equal, ALU.mult).then_inc(s["setup"], 1)
            dve.wait_ge(s["zeroed"], 4)
            CHAIN = GROUPS + 1

            def split(b, m):
                dve.wait_ge(s["slot_read"], b * SLOTS + slot_of_q(m) + 2 + 2)
                for j in range(4):
                    dve.wait_ge(stack_loaded[j], b * STACKED + (16 + 96 * m if m else 0) + 1)
                dve.tensor_copy(q_parts[:, 0, :], projected[:, 0, 0:S])
                dve.tensor_copy(k_parts[:, 0, :], projected[:, 1, :]).then_inc(s["parts_chain"], 1)
                dve.wait_ge(s["parts_chain"], b * GROUPS + m + 1)
                dve.tensor_tensor(q_parts[:, 1, :], projected[:, 0, 0:S], q_parts[:, 0, :].bitcast(F32), ALU.subtract)
                dve.tensor_tensor(k_parts[:, 1, :], projected[:, 1, :], k_parts[:, 0, :].bitcast(F32),
                                  ALU.subtract).then_inc(s["parts_ready"], 1)

            def maximum(b, i, t):
                dve.wait_ge(s["logits_done"], b * LOGITS + TPB * i + t + 1 + 4 * TPB)
                u = slot_of_logits(i, t)
                dve.tensor_reduce(top[:, i % 2, t:t + 1], slot[:, u % 2, :, 0:HALF], AX.XY, ALU.max,
                                  negate=True).then_inc(s["top_ready"], 1)

            def pad_values(b, i):
                j = i % 4
                if i >= 4:
                    dve.wait_ge(s["gathered_done"], b * (H + TPB) + i - 3)
                if i == 0:
                    dve.wait_ge(s["slot_read"], b * SLOTS + 4 + CHUNKS + 2)
                mine = slice(i * HD, (i + 1) * HD)
                dve.tensor_tensor(padded_v[:, 0:TPB, j, j * HD:(j + 1) * HD], values[:, 0:TPB, mine],
                                  bv_row[:, mine].unsqueeze(1).to_broadcast([P, TPB, HD]), ALU.add)
                dve.tensor_tensor(padded_v[C:P, TPB, j, j * HD:(j + 1) * HD], values[C:P, TPB, mine], bv_row[C:P, mine],
                                  ALU.add).then_inc(s["padded_ready"], 1)

            def invert(b, m):
                dve.wait_ge(s["slot_read"], b * SLOTS + slot_of_logits(4 * m + 3, TPB - 1) + 3)
                dve.reciprocal(inverse[:, :, :], total[:, m % 2, :, :]).then_inc(s["chain"], 1)
                dve.wait_ge(s["chain"], b * CHAIN + m + 1)
                dve.tensor_copy(wide_inverse[:, :, :, :].rearrange("p t h d -> p (t h) d"),
                                inverse[:, :, :].rearrange("p t h -> p (t h)").unsqueeze(2).to_broadcast([P, 4 * TPB, HD]))\
                    .then_inc(s["inverse_ready"], 1)

            def normalise(b, m):
                dve.wait_ge(s["turned1_done"], b * T1 + 2 * min(4 * m + 5, H) + m + 1)
                dve.tensor_copy(inverse_T[:, :], turned[:, 1, :]).then_inc(s["turned1_out"], 1)
                dve.wait_ge(s["turned1_out"], b * T1 + 2 * min(4 * m + 5, H) + m + 2)
                dve.wait_ge(s["gathered_done"], b * (H + TPB) + 4 * m + 4)
                dve.tensor_tensor(mixed[:, m, :], gathered[:, m % 2, :], inverse_T[:, :], ALU.mult).then_inc(s["gathered_read"], 1)

            with dve.Fori(0, B) as b:
                split(b, 0)
                for t in range(TPB):
                    maximum(b, 0, t)
                for i in range(H + 1):
                    if i < H:
                        pad_values(b, i)
                    for c in range(CHUNKS):
                        if c < TPB and i + 1 < H:
                            maximum(b, i + 1, c)
                        if i < H and c % 2:
                            at = b * T1 + 2 * i + max(0, (i - 1) // 4) + c // 2 + 1
                            dve.wait_ge(s["turned1_done"], at)
                            dve.tensor_copy(probs_T[:, i % 2, c, :], turned[:, 1, :]).then_inc(s["turned1_out"], 1)
                    if i % 4 == 0 and i // 4 + 1 < GROUPS:
                        split(b, i // 4 + 1)
                    if i >= 4 and i % 4 == 0:
                        normalise(b, i // 4 - 1)
                    if i % 4 == 3:
                        invert(b, i // 4)
                dve.wait_ge(s["rows_loaded"], 16 * (b + 1))
                dve.tensor_tensor(rows[:, :, :], rows[:, :, :], bo_row[:, :].unsqueeze(1).to_broadcast([P, TPB, D]),
                                  ALU.add).then_inc(s["chain"], 1)
                dve.wait_ge(s["chain"], b * CHAIN + CHAIN)
                for t in range(TPB):
                    dve.wait_ge(s["gathered_done"], b * (H + TPB) + H + t + 1)
                    dve.tensor_tensor(rows[:, t, :], gathered[:, t % 2, :], rows[:, t, :], ALU.add).then_inc(s["gathered_read"], 1)


def l3_attention_stage(n, tag, norm, weights, bias_row):
    nc = n.nc
    SCALE = float(HD) ** -0.5
    LEAST = -3.4028234663852886e38
    GROUPS, PAIRS = H // 4, H // 2
    PREP = GROUPS + B
    with ExitStack() as mem:
        wq, wk, wv, wo = weights
        bv_row = n.sbuf(f"{tag}_bv_row", [P, D], F32, mem)
        keep_raw = n.sbuf(f"{tag}_keep_raw", [P, CTOK], U8, mem)
        keep = n.sbuf(f"{tag}_keep", [P, CTOK], F32, mem)
        dropped = n.sbuf(f"{tag}_dropped", [P, CTOK], F32, mem)
        least = n.sbuf(f"{tag}_least", [P, CTOK], F32, mem)
        least_b = n.sbuf(f"{tag}_least_b", [P, C], F32, mem)
        keys = n.sbuf(f"{tag}_keys", [P, GROUPS, B, 4, C], F32, mem)
        all_values = n.sbuf(f"{tag}_all_values", [P, B, PAIRS, P], F32, mem)
        values = n.sbuf(f"{tag}_values", [P, PAIRS, P], F32, mem)
        queries = n.sbuf(f"{tag}_queries", [P, GROUPS, S], F32, mem)
        probs = n.sbuf(f"{tag}_probs", [P, TPB, H, C], F32, mem)
        top, total, inverse = (n.sbuf(f"{tag}_{w}", [P, TPB, H], F32, mem) for w in ("top", "total", "inverse"))
        probs_T = n.sbuf(f"{tag}_probs_T", [P, PAIRS, S], F32, mem)
        mixed = n.sbuf(f"{tag}_mixed", [P, GROUPS, S], F32, mem)
        rows = n.sbuf(f"{tag}_rows", [P, TPB, D], F32, mem)
        work = n.psum(f"{tag}_work", [P, 2, 512], mem)
        score = n.psum(f"{tag}_score", [P, 2, H * C], mem)
        turned = n.psum(f"{tag}_turned", [P, 2, S], mem)

        s = {k: n.sem(f"{tag}_{k}") for k in (
            "bv_loaded", "keep_loaded", "zeroed", "bias_added", "mask_ready", "prep_done", "prep_read", "least_b_loaded", "values_loaded",
            "rows_loaded", "rows_stored", "work_done", "work_read", "logits_done", "logits_read", "chain", "shifted",
            "exped", "probs_ready", "turned_done", "turned_out", "projected_done", "rows_added")}
        WORK = 2 * GROUPS
        block = mem.enter_context(nc.Block())

        @block.sync
        def _(sp):
            sp.dma_start(keep_raw[:, :], n.dram["keep_l3"].to_broadcast([P, CTOK])).then_inc(s["keep_loaded"], 16)
            sp.dma_start(bv_row[:, :], n.row_broadcast(f"{tag}_bv")).then_inc(s["bv_loaded"], 16)
            sp.wait_ge(s["mask_ready"], 1)
            sp.wait_ge(s["bias_added"], TILES)
            sp.wait_ge(s["prep_read"], 4 * GROUPS + 2 * B)

            def load_mask(b):
                sp.dma_start(least_b[:, :], least[:, bass.ds(b * C, C)]).then_inc(s["least_b_loaded"], 16)

            def load_values(b):
                sp.dma_start(values[:, :, :], all_values[:, bass.ds(b, 1), :, :]).then_inc(s["values_loaded"], 16)

            def batch(b, more):
                x_b = n.x[:, bass.ds(sp.snap(b * TPB) if more else b * TPB, TPB), :]
                sp.wait_ge(s["rows_stored"], 16 * b + 16)
                sp.dma_start(rows[:, :, :], x_b).then_inc(s["rows_loaded"], 16)
                if more:
                    following = sp.snap(b + 1)
                    sp.wait_ge(s["logits_read"], b * TPB + TPB + 2)
                    load_mask(following)
                    sp.wait_ge(s["work_done"], b * WORK + 3 * GROUPS)
                    load_values(following)
                sp.wait_ge(s["rows_added"], b * TPB + 2 * TPB + 2)
                sp.dma_start(x_b, rows[:, :, :]).then_inc(s["rows_stored"], 16)

            load_mask(0)
            load_values(0)
            with sp.Fori(0, B - 1) as b:
                batch(b, True)
            batch(B - 1, False)
            sp.wait_ge(s["rows_stored"], 16 * B + 16)

        @block.gpsimd
        def _(pool):
            pool.memset(keys[:, :, :, :, :], 0.0).then_inc(s["zeroed"], 1)
            pool.wait_ge(s["zeroed"], 1)
            pool.memset(all_values[:, :, :, :], 0.0).then_inc(s["zeroed"], 1)
            add_bias(n, pool, bias_row, s["bias_added"])

        @block.tensor
        def _(pe):
            pe.sem_inc(s["projected_done"], TPB)
            i = 0
            for m in range(GROUPS):
                if i >= 2:
                    pe.wait_ge(s["prep_read"], 4 * (i - 1))
                for k in range(KT):
                    last = pe.matmul(work[:, i % 2, 0:CTOK], wk[:, k, m * P:(m + 1) * P], n.ctx_f[:, k, :], start=k == 0, stop=k == KT - 1)
                last.then_inc(s["prep_done"], 1)
                i += 1
            for b in range(B):
                pe.wait_ge(s["prep_read"], 4 * (i - 1) if i - 2 < GROUPS else 4 * GROUPS + 2 * (i - 1 - GROUPS))
                for k in range(KT):
                    last = pe.matmul(work[0:C, i % 2, :], n.ctx_f[:, k, b * C:(b + 1) * C], wv[:, k, :], start=k == 0, stop=k == KT - 1)
                last.then_inc(s["prep_done"], 1)
                i += 1
            pe.wait_ge(s["prep_read"], 4 * GROUPS + 2 * B)

            def queries_of(b, at, added):
                for m in range(GROUPS):
                    pe.wait_ge(s["work_read"], at + m + 1)
                    if m == 0:
                        pe.wait_ge(s["rows_added"], added)
                    for k in range(KT):
                        last = pe.matmul(work[:, m % 2, :], wq[:, k, m * P:(m + 1) * P], norm[:, k, bass.ds(b * S, S)],
                                         start=k == 0, stop=k == KT - 1)
                    last.then_inc(s["work_done"], 1)

            def logits(b, t):
                if t == 0:
                    pe.wait_ge(s["work_read"], b * WORK + GROUPS + 2)
                pe.wait_ge(s["logits_read"], b * TPB + t + 1)
                for m in range(GROUPS):
                    last = pe.matmul(score[:, t % 2, m * 4 * C:(m + 1) * 4 * C], queries[:, m, t * P:(t + 1) * P],
                                     keys[:, m, bass.ds(b, 1), :, :].rearrange("p a h c -> p (a h c)"), start=True, stop=True)
                last.then_inc(s["logits_done"], 1)

            def turn(b, pair):
                if pair == 0:
                    pe.wait_ge(s["probs_ready"], (b + 1) * TPB)
                pe.wait_ge(s["turned_out"], b * PAIRS + pair + 1)
                for t in range(TPB):
                    last = pe.transpose(turned[:, pair % 2, t * P:(t + 1) * P],
                                        probs[:, t, 2 * pair:2 * pair + 2, :].rearrange("p h c -> p (h c)"), n.ident[:, :])
                last.then_inc(s["turned_done"], 1)

            def mix(b, m, at):
                pe.wait_ge(s["turned_out"], b * PAIRS + 2 * m + 4)
                if m == 0:
                    pe.wait_ge(s["values_loaded"], 16 * (b + 1))
                pe.wait_ge(s["work_read"], at + m + 1)
                for half in range(2):
                    last = pe.matmul(work[:, m % 2, :], values[:, 2 * m + half, :], probs_T[:, 2 * m + half, :],
                                     start=half == 0, stop=half == 1)
                last.then_inc(s["work_done"], 1)

            def project(b, t, at):
                if t == 0:
                    pe.wait_ge(s["work_read"], at + GROUPS + 2)
                pe.wait_ge(s["rows_added"], b * TPB + t + 1 + TPB)
                for m in range(GROUPS):
                    last = pe.matmul(work[:, t % 2, :], mixed[:, m, t * P:(t + 1) * P], wo[:, m, :],
                                     start=m == 0, stop=m == GROUPS - 1)
                last.then_inc(s["projected_done"], 1)

            def batch(b, more):
                at = b * WORK + GROUPS
                if more:
                    queries_of(b + 1, at, b * TPB + TPB + 2)
                    at = at + GROUPS
                for m in range(GROUPS):
                    turn(b, 2 * m)
                    turn(b, 2 * m + 1)
                    if m:
                        mix(b, m - 1, at)
                mix(b, GROUPS - 1, at)
                for t in range(TPB):
                    project(b, t, at)
                    if more:
                        logits(b + 1, t)

            queries_of(0, 0, TPB + 2)
            for t in range(TPB):
                logits(0, t)
            with pe.Fori(0, B - 1) as b:
                batch(b, True)
            batch(B - 1, False)

        @block.scalar
        def _(act):
            act.sem_inc(s["work_read"], 2)
            act.sem_inc(s["turned_out"], 2)
            act.wait_ge(s["prep_read"], 4 * GROUPS + 2 * B)

            def queries_of(at):
                for m in range(GROUPS):
                    act.wait_ge(s["work_done"], at + m + 1)
                    act.activation(queries[:, m, :], work[:, m % 2, :], ACT.Identity, bias=n.col(f"{tag}_bq", m))\
                        .then_inc(s["work_read"], 1)

            def exps(b, t):
                act.wait_ge(s["shifted"], b * TPB + t + 1)
                act.activation(probs[:, t, :, :], probs[:, t, :, :], ACT.Exp, scale=SCALE).then_inc(s["exped"], 1)

            def mixed_of(m, at):
                act.wait_ge(s["work_done"], at + m + 1)
                act.copy(mixed[:, m, :], work[:, m % 2, :]).then_inc(s["work_read"], 1)

            def batch(b, more):
                at = b * WORK + GROUPS
                for t in range(TPB):
                    exps(b, t)
                if more:
                    queries_of(at)
                    at = at + GROUPS
                for m in range(GROUPS):
                    for half in range(2):
                        pair = 2 * m + half
                        act.wait_ge(s["turned_done"], b * PAIRS + pair + 1)
                        act.copy(probs_T[:, pair, :], turned[:, half, :]).then_inc(s["turned_out"], 1)
                    if m:
                        mixed_of(m - 1, at)
                mixed_of(GROUPS - 1, at)

            queries_of(0)
            with act.Fori(0, B - 1) as b:
                batch(b, True)
            batch(B - 1, False)

        @block.vector
        def _(dve):
            dve.sem_inc(s["logits_read"], 2)
            dve.sem_inc(s["rows_added"], 2 + TPB)
            dve.sem_inc(s["rows_stored"], 16)
            dve.wait_ge(s["keep_loaded"], 16)
            dve.tensor_scalar(dropped[:, :], keep_raw[:, :], 0.0, None, ALU.is_equal).then_inc(s["chain"], 1)
            dve.wait_ge(s["chain"], 1)
            dve.tensor_scalar(keep[:, :], dropped[:, :], -1.0, 1.0, ALU.mult, ALU.add).then_inc(s["chain"], 1)
            dve.tensor_scalar(least[:, :], dropped[:, :], LEAST, None, ALU.mult).then_inc(s["mask_ready"], 1)
            dve.wait_ge(s["chain"], 2)
            dve.wait_ge(s["zeroed"], 2)
            for m in range(GROUPS):
                dve.wait_ge(s["prep_done"], m + 1)
                for j in range(4):
                    mine = slice(32 * j, 32 * j + 32)
                    dve.scalar_tensor_tensor(keys[mine, m, :, j, :], work[mine, m % 2, 0:CTOK].rearrange("p (b c) -> p b c", b=B),
                                             n.col(f"{tag}_bk", m)[mine, :], keep[mine, :].rearrange("p (b c) -> p b c", b=B),
                                             ALU.add, ALU.mult).then_inc(s["prep_read"], 1)
            dve.wait_ge(s["bv_loaded"], 16)
            for b in range(B):
                dve.wait_ge(s["prep_done"], GROUPS + b + 1)
                for odd in range(2):
                    pick = "p (a c o d) -> p a c o d"
                    out = all_values[odd * C:(odd + 1) * C, b, :, :].rearrange("p (a c) n -> p a (c n)", c=2)
                    source = work[0:C, (GROUPS + b) % 2, :].rearrange(pick, a=4, c=2, o=2)
                    bias = bv_row[0:C, :].rearrange(pick, a=4, c=2, o=2)
                    for c in range(2):
                        at = c * P + (2 * c + odd) * HD
                        instruction = dve.tensor_tensor(out[:, :, at:at + HD], source[:, :, c, odd, :], bias[:, :, c, odd, :],
                                                        ALU.add)
                    instruction.then_inc(s["prep_read"], 1)
            BEFORE = 2
            LINKS = 3 * TPB

            def shift(b, t):
                u = t % 2
                dve.wait_ge(s["logits_done"], b * TPB + t + 1)
                if t == 0:
                    dve.wait_ge(s["least_b_loaded"], 16 * (b + 1))
                dve.tensor_tensor(probs[:, t, :, :], score[:, u, :].rearrange("p (h c) -> p h c", h=H),
                                  least_b[:, :].unsqueeze(1).to_broadcast([P, H, C]), ALU.add).then_inc(s["logits_read"], 1)
                dve.wait_ge(s["logits_read"], b * TPB + t + 3)
                dve.tensor_reduce(top[:, t, :], probs[:, t, :, :], AX.X, ALU.max).then_inc(s["chain"], 1)
                dve.wait_ge(s["chain"], b * LINKS + BEFORE + (1 if t == 0 else 3 * t - 1))
                dve.tensor_tensor(probs[:, t, :, :], probs[:, t, :, :], top[:, t, :].unsqueeze(2).to_broadcast([P, H, C]),
                                  ALU.subtract).then_inc(s["shifted"], 1)

            def normalise(b, t):
                before = min(3 * t + 2, 3 * TPB - 2)
                dve.wait_ge(s["exped"], b * TPB + t + 1)
                dve.tensor_reduce(total[:, t, :], probs[:, t, :, :], AX.X, ALU.add).then_inc(s["chain"], 1)
                dve.wait_ge(s["chain"], b * LINKS + BEFORE + before + 1)
                dve.reciprocal(inverse[:, t, :], total[:, t, :]).then_inc(s["chain"], 1)
                dve.wait_ge(s["chain"], b * LINKS + BEFORE + before + 2)
                dve.tensor_tensor(probs[:, t, :, :], probs[:, t, :, :], inverse[:, t, :].unsqueeze(2).to_broadcast([P, H, C]),
                                  ALU.mult).then_inc(s["probs_ready"], 1)

            def add(b, t):
                if t == 0:
                    dve.wait_ge(s["rows_loaded"], 16 * (b + 1))
                dve.wait_ge(s["projected_done"], b * TPB + t + 1 + TPB)
                dve.tensor_tensor(rows[:, t, :], work[:, t % 2, :], rows[:, t, :], ALU.add).then_inc(s["rows_added"], 1)

            def softmax(b, between):
                between(0)
                shift(b, 0)
                for t in range(TPB):
                    if t + 1 < TPB:
                        between(t + 1)
                        shift(b, t + 1)
                    normalise(b, t)

            softmax(0, lambda t: None)
            with dve.Fori(0, B - 1) as b:
                softmax(b + 1, lambda t: add(b, t))
            for t in range(TPB):
                add(B - 1, t)


def mlp_stage(n, tag, first, second, bias, activation, parts, first_block, bias_row):
    nc = n.nc
    norm_hi, norm_lo = parts
    with ExitStack() as mem:
        raw1, w1h, w1l = first_block
        raw2 = n.sbuf(f"{tag}_raw2", [P, KT, D], F32, mem)
        w2h, w2l = n.sbuf(f"{tag}_w2h", [P, KT, D], F32R, mem), n.sbuf(f"{tag}_w2l", [P, KT, D], F32R, mem)
        bias_block = n.sbuf(f"{tag}_bias_block", [P, KT], F32, mem)
        bias_loaded = n.sem(f"{tag}_bias_loaded")
        hidden = n.sbuf(f"{tag}_hidden", [P, 2, S], F32, mem)
        hh, hl = n.sbuf(f"{tag}_hh", [P, 2, KT, S], F32R, mem), n.sbuf(f"{tag}_hl", [P, 2, KT, S], F32R, mem)
        up, down = n.psum(f"{tag}_up", [P, KT, S], mem), n.psum(f"{tag}_down", [P, TPB, D], mem)

        raw1_loaded, raw2_loaded = n.sem(f"{tag}_raw1_loaded"), n.sem(f"{tag}_raw2_loaded")
        w1_ready, w2_ready = n.sem(f"{tag}_w1_ready"), n.sem(f"{tag}_w2_ready")
        split_hi = n.sem(f"{tag}_split_hi")
        up_done = n.sem(f"{tag}_up_done")
        hidden_ready = n.sem(f"{tag}_hidden_ready")
        hidden_split = n.sem(f"{tag}_hidden_split")
        down_done, down_free = n.sem(f"{tag}_down_done"), n.sem(f"{tag}_down_free")
        bias_added = n.sem(f"{tag}_bias_added")
        UPS, DOWNS = B * KT, B * TPB
        block = mem.enter_context(nc.Block())

        @block.sync
        def _(sp):
            def loads(f):
                sp.wait_ge(w2_ready, f + 1)
                sp.dma_start(raw2[:, :, :], n.block(second, f)).then_inc(raw2_loaded, 16)
                sp.wait_ge(hidden_ready, f * UPS + KT)
                at = COLUMNS[bias]
                sp.dma_start(bias_block[:, :], n.dram["columns"][:, bass.ds(f * KT + at, KT)]).then_inc(bias_loaded, 16)

            loads(0)
            with sp.Fori(1, FB) as f:
                sp.wait_ge(w1_ready, f + 1)
                sp.dma_start(raw1[:, :, :], n.block(first, f)).then_inc(raw1_loaded, 16)
                loads(f)

        @block.gpsimd
        def _(pool):
            add_bias(n, pool, bias_row, bias_added)

        @block.tensor
        def _(pe):
            def ups(f, c):
                for m in range(KT):
                    pe.wait_ge(hidden_ready, f * UPS + c * KT + m + 1)
                    for k in range(KT):
                        last = product3(pe, up[:, m, :],
                                        (w1h[:, k, m * P:(m + 1) * P], w1l[:, k, m * P:(m + 1) * P]),
                                        (norm_hi[:, k, c * S:(c + 1) * S], norm_lo[:, k, c * S:(c + 1) * S]),
                                        k == 0, k == KT - 1)
                    last.then_inc(up_done, 1)

            def downs(f, c):
                pe.wait_ge(hidden_split, f * UPS + (c + 1) * KT + 2)
                for j in range(TPB):
                    pe.wait_ge(down_free, f * DOWNS + c * TPB + j + 1)
                    for m in range(KT):
                        last = product3(pe, down[:, j, :],
                                        (hh[:, c % 2, m, j * P:(j + 1) * P], hl[:, c % 2, m, j * P:(j + 1) * P]),
                                        (w2h[:, m, :], w2l[:, m, :]), m == 0, m == KT - 1)
                    last.then_inc(down_done, 1)

            with pe.Fori(0, FB) as f:
                pe.wait_ge(w1_ready, f + 2)
                ups(f, 0)
                pe.wait_ge(w2_ready, f + 2)
                for c in range(B):
                    if c + 1 < B:
                        ups(f, c + 1)
                    downs(f, c)

        @block.scalar
        def _(act):
            act.sem_inc(hidden_ready, KT)
            with act.Fori(0, FB) as f:
                act.wait_ge(bias_loaded, 16 * (f + 1))
                for i in range(UPS):
                    act.wait_ge(up_done, f * UPS + i + 1)
                    act.wait_ge(hidden_split, f * UPS + i + 1)
                    act.activation(hidden[:, i % 2, :], up[:, i % KT, :], activation,
                                   bias=bias_block[:, i % KT:i % KT + 1])\
                        .then_inc(hidden_ready, 1)

        @block.vector
        def _(dve):
            dve.sem_inc(hidden_split, 2)
            dve.sem_inc(w1_ready, 2)
            dve.sem_inc(w2_ready, 1)
            dve.sem_inc(down_free, TPB)
            SPLITS = 2 + UPS

            def split_weights(f, raw, loaded, hi, lo, ready, at):
                dve.wait_ge(loaded, 16 * (f + 1) if ready is w2_ready else 16 * f)
                dve.tensor_copy(hi[:, :, :], raw[:, :, :]).then_inc(split_hi, 1)
                dve.wait_ge(split_hi, at)
                dve.tensor_tensor(lo[:, :, :], raw[:, :, :], hi[:, :, :].bitcast(F32), ALU.subtract).then_inc(ready, 1)

            def split_hidden(f, c):
                for m in range(KT):
                    i = c * KT + m
                    dve.wait_ge(hidden_ready, f * UPS + KT + i + 1)
                    if m == 0 and c >= 2:
                        dve.wait_ge(down_done, f * DOWNS + (c - 1) * TPB)
                    dve.tensor_copy(hh[:, c % 2, m, :], hidden[:, i % 2, :]).then_inc(split_hi, 1)
                    dve.wait_ge(split_hi, f * SPLITS + 2 + i)
                    dve.tensor_tensor(hl[:, c % 2, m, :], hidden[:, i % 2, :], hh[:, c % 2, m, :].bitcast(F32),
                                      ALU.subtract).then_inc(hidden_split, 1)

            def add_downs(f, c):
                for j in range(TPB):
                    dve.wait_ge(bias_added, c * TPB + j + 1)
                    dve.wait_ge(down_done, f * DOWNS + c * TPB + j + 1)
                    dve.tensor_tensor(n.x[:, c * TPB + j, :], down[:, j, :], n.x[:, c * TPB + j, :],
                                      ALU.add).then_inc(down_free, 1)

            def one_block(f, more):
                split_weights(f, raw2, raw2_loaded, w2h, w2l, w2_ready, f * SPLITS + 1)
                split_hidden(f, 0)
                for c in range(B):
                    if c + 1 < B:
                        split_hidden(f, c + 1)
                    if more and c == B - 2:
                        split_weights(f + 1, raw1, raw1_loaded, w1h, w1l, w1_ready, (f + 1) * SPLITS)
                    add_downs(f, c)

            with dve.Fori(0, FB - 1) as f:
                one_block(f, True)
            one_block(FB - 1, False)


def build(nc, dram):
    with ExitStack() as ctx:
        n = Net(nc, ctx, dram)
        for stage in (load_stage, *STAGES, store_stage):
            stage(n)
            n.end_stage()


def weight_buffers(n, tag, names, mem):
    buffers = [n.sbuf(f"{tag}_{w}", [P, KT, D], F32, mem) for w in names]
    return buffers, [(buffer[:, :, :], n.block(f"{tag}_{w}")) for buffer, w in zip(buffers, names)]


def bias_buffer(n, tag, row, mem):
    buffer = n.sbuf(f"{tag}_bias_row", [P, D], F32, mem)
    return buffer, (buffer[:, :], n.row_broadcast(row))


def mlp_operands(n, tag, mem):
    parts = (n.sbuf(f"{tag}_norm_hi", [P, KT, TOK], F32R, mem), n.sbuf(f"{tag}_norm_lo", [P, KT, TOK], F32R, mem))
    return parts, (n.sbuf(f"{tag}_raw1", [P, KT, D], F32, mem), n.sbuf(f"{tag}_w1h", [P, KT, D], F32R, mem),
                   n.sbuf(f"{tag}_w1l", [P, KT, D], F32R, mem))


def stage_mlp(n, tag, scale, offset, row, first, second, bias, activation):
    with ExitStack() as mem:
        parts, first_block = mlp_operands(n, tag, mem)
        bias_row, preload_row = bias_buffer(n, tag, row, mem)
        normalise_stage(n, f"{tag}_norm", n.x, scale, offset, "layer", 1e-5, parts=parts, preload=[preload_row],
                        first_block=(n.block(first), *first_block))
        mlp_stage(n, tag, first, second, bias, activation, parts, first_block, bias_row)


def l0_mlp(n):
    stage_mlp(n, "l0m", "l0m_scale", "l0m_offset", "l0_b2", "l0_fc1", "l0_fc2", "l0_b1", ACT.Gelu)


def l0_attention(tag, row):
    def stage(n):
        with ExitStack() as mem:
            norm = n.sbuf(f"{tag}_norm", [P, KT, TOK], F32, mem)
            blocks, preload = weight_buffers(n, tag, ("wk", "wv", "wqT", "wo"), mem)
            bias_row, preload_row = bias_buffer(n, tag, row, mem)
            normalise_stage(n, f"{tag}_norm", n.x, f"{tag}_scale", f"{tag}_offset", "layer", 1e-5, plain=norm,
                            preload=[*preload, preload_row], src_dram=n.dram["x"].rearrange("(t p) d -> p t d", p=P) if tag == "l0a" else None)
            l0_attention_stage(n, tag, norm, blocks, bias_row)
    return stage


def l1_and_l2_attention(n):
    with ExitStack() as mem:
        l2_weights, l2_preload = weight_buffers(n, "l2", ("wq", "wk", "wv", "wo"), mem)
        with ExitStack() as l1_mem:
            turned_x = n.sbuf("l1_turned_x", [P, KT, TOK], F32, l1_mem)
            weights, preload = weight_buffers(n, "l1", ("wkT", "wvT", "wq", "woT"), l1_mem)
            normalise_stage(n, "l1_turn", n.x, None, None, "none", 0.0, plain=turned_x, preload=preload)
            l1_attention_stage(n, "l1", turned_x, weights, l2_preload)
        n.end_stage()
        l2_attention_stage(n, "l2", l2_weights)


def l2_mlp(n):
    with ExitStack() as mem:
        parts, first_block = mlp_operands(n, "l2m", mem)
        bias_row, preload_row = bias_buffer(n, "l2m", "l2_b2", mem)
        with ExitStack() as inner:
            rows = n.sbuf("l2m_rows", [P, TILES, D], F32, inner)
            normalise_stage(n, "l2m_norm", rows, "l2_scale", None, "rms", 1e-6, parts=parts, preload=[preload_row],
                            first_block=(n.block("l2_fc1"), *first_block), src_dram=n.dram["l2_rows"])
        mlp_stage(n, "l2m", "l2_fc1", "l2_fc2", "l2_b1", ACT.Gelu_apprx_tanh, parts, first_block, bias_row)


def l3_attention(n):
    with ExitStack() as mem:
        norm = n.sbuf("l3_norm", [P, KT, TOK], F32, mem)
        weights, preload = weight_buffers(n, "l3", ("wq", "wk", "wv", "wo"), mem)
        bias_row, preload_row = bias_buffer(n, "l3", "l3_bo", mem)
        normalise_stage(n, "l3_norm", n.x, "l3_scale", "l3_offset", "layer", 1e-5, plain=norm,
                        preload=[*preload, preload_row])
        l3_attention_stage(n, "l3", norm, weights, bias_row)


def l3_mlp(n):
    stage_mlp(n, "l3m", "l3m_scale", "l3m_offset", "l3_b2", "l3_fc1", "l3_fc2", "l3_b1",
              ACT.Gelu_apprx_tanh)


STAGES = (l0_attention("l0a", "l0a_bo"), l0_attention("l0b", "l0b_bo"), l0_mlp, l1_and_l2_attention, l2_mlp,
          l3_attention, l3_mlp)


def kernel(**inputs):
    import numpy as _np
    import concourse.bacc as _bacc
    from concourse.bass_utils import run_bass_kernel_spmd as _run

    a = {k: _np.asarray(v) for k, v in inputs.items()}

    def blocks(w):
        r, c = w.shape[0] // 512, w.shape[1] // 512
        w = w.reshape(r, 4, 128, c, 512).transpose(0, 3, 2, 1, 4)
        return w.reshape(r * c, 128, 2048)

    l0, l1, l2, l3 = "L0_xattn_", "L1_xattn_", "L2_xattn_", "L3_xattn_"
    w = []
    for i in "12":
        w += [a[l0 + "wk" + i], a[l0 + "wv" + i], a[l0 + "wq" + i].T, a[l0 + "wo" + i]]
    w += [a[l0 + "w_fc1"], a[l0 + "w_fc2"]]
    w += [a[l1 + "w_k"].T, a[l1 + "w_v"].T, a[l1 + "w_q"], a[l1 + "w_o"].T]
    w += [a[l2 + "q_w"], a[l2 + "kv_w"][:, 0::2], a[l2 + "kv_w"][:, 1::2], a[l2 + "out_w"], a[l2 + "mlp_w1"], a[l2 + "mlp_w2"]]
    w += [a[l3 + "q_w"], a[l3 + "k_w"], a[l3 + "v_w"], a[l3 + "cproj_w"], a[l3 + "fc_w"], a[l3 + "proj_w"]]
    weights = _np.ascontiguousarray(_np.concatenate([blocks(m) for m in w], axis=0))

    c = [a[l0 + "ln1_scale"], a[l0 + "ln1_offset"], a[l0 + "ln2_scale"], a[l0 + "ln2_offset"],
         a[l0 + "ln_mlp_scale"], a[l0 + "ln_mlp_offset"]]
    for i in "12":
        c += [a[l0 + v + i] for v in ("bq", "bk", "bv", "bias_k", "bias_v")]
    c += [a[l0 + "b_fc1"], a[l2 + "q_b"], a[l2 + "kv_b"][0::2], a[l2 + "postnorm_w"], a[l2 + "mlp_b1"]]
    c += [a[l3 + "ln1_w"], a[l3 + "ln1_b"], a[l3 + "q_b"], a[l3 + "k_b"], a[l3 + "ln2_w"], a[l3 + "ln2_b"], a[l3 + "fc_b"]]
    columns = _np.ascontiguousarray(_np.concatenate([v.reshape(-1, 128) for v in c], axis=0).T)

    rows = _np.stack([a[l0 + "bo1"], a[l0 + "bo2"], a[l0 + "b_fc2"], a[l2 + "kv_b"][1::2], a[l2 + "out_b"],
                      a[l2 + "mlp_b2"], a[l3 + "v_b"], a[l3 + "cproj_b"], a[l3 + "proj_b"]])
    arrays = {
        "x": _np.ascontiguousarray(a["x"].reshape(TOK, D)), "ctx": _np.ascontiguousarray(a["ctx_2048"].reshape(CTOK, D)),
        "weights": weights, "columns": columns, "rows": rows,
        "keep_l2": a["mask_BxS2_ik0"].reshape(1, CTOK), "keep_l3": a["mask_BxS2_bf1"].view(_np.uint8).reshape(1, CTOK),
        "alpha": a[l1 + "alpha"].reshape(1, 1),
    }
    nc = _bacc.Bacc("TRN2", target_bir_lowering=False, num_devices=1)
    types = {"float32": F32, "int32": I32, "uint8": U8}
    dram = {k: nc.dram_tensor(f"in_{k}", v.shape, types[str(v.dtype)], kind="ExternalInput").ap() for k, v in arrays.items()}
    dram["out"] = nc.dram_tensor("out_0", (TOK, D), F32, kind="ExternalOutput").ap()
    for tag in ("l0a", "l0b"):
        dram[f"{tag}_scratch"] = nc.dram_tensor(f"{tag}_scratch", (H, D), F32).ap()
    dram["l2_rows"] = nc.dram_tensor("l2_rows_dram", (P, TILES, D), F32).ap()
    build(nc, dram)
    r = _run(nc, [{f"in_{k}": v for k, v in arrays.items()}], core_ids=[0])
    return r.results[0]["out_0"].reshape(B, S, D)
```
